# Optimizing a Trainium2 kernel written in Bass

```python
import numpy as np
import jax
import jax.numpy as jnp

def _softmax(x, axis=-1):
    return jax.nn.softmax(x, axis=axis)

def _gelu(x):
    return jax.nn.gelu(x, approximate=True)

def _silu(x):
    return jax.nn.silu(x)

def _sigmoid(x):
    return jax.nn.sigmoid(x)

def _layernorm(x, axis=-1, eps=1e-05):
    m = jnp.mean(x, axis=axis, keepdims=True)
    v = jnp.var(x, axis=axis, keepdims=True)
    return (x - m) / jnp.sqrt(v + eps)

def _scatter_add(tgt, idx, src, axis=0):
    return tgt.at[idx].add(src)

def _segment_sum(src, seg, n):
    return jax.ops.segment_sum(src, seg, n)
kernel_name = 'mk_gnn_resnorm_d2_gnn_r8_736775'

def setup_inputs(seed: int=0):
    np.random.seed(seed)
    _w = jnp.asarray

    def _rec_inputs():
        import jax
        import jax.numpy as jnp
        _gk = jax.random.key(seed)
        x = -0.0002117 + 1 * jax.random.normal(jax.random.fold_in(_gk, 1), (6250, 512), jnp.float32)
        _s = jax.random.randint(jax.random.fold_in(_gk, 2), (50000,), 0, 6250, jnp.int32)
        _d = jax.random.randint(jax.random.fold_in(_gk, 3), (50000,), 0, 6250, jnp.int32)
        _loop = jnp.arange(6250, dtype=jnp.int32)
        src = jnp.concatenate([_s, _d, _loop])
        dst = jnp.concatenate([_d, _s, _loop])
        _o = jnp.argsort(dst, stable=True)
        src = src[_o]
        dst = dst[_o]
        return (x, src, dst)
    x, src, dst = _rec_inputs()

    def _L0_gnn_setup():
        import jax, jax.numpy as jnp
        import numpy as np
        N_NODES = 6250
        N_EDGES = 200000
        N_HEADS = 8
        IN_DIM = 512
        OUT_DIM = 64
        LRELU_ALPHA = 0.2
        key = jax.random.key(seed)
        k1, k2, k3, k4, k5 = jax.random.split(key, 5)
        x = jax.random.normal(k1, (N_NODES, IN_DIM), dtype=jnp.float32)
        W = jax.random.normal(k2, (N_HEADS, IN_DIM, OUT_DIM), dtype=jnp.float32) * (1.0 / np.sqrt(IN_DIM))
        att_w = jax.random.normal(k3, (N_HEADS, 2 * OUT_DIM), dtype=jnp.float32) * (1.0 / np.sqrt(2 * OUT_DIM))
        src = jax.random.randint(k4, (N_EDGES,), 0, N_NODES, dtype=jnp.int64 if jax.config.read('jax_enable_x64') else jnp.int32).astype(jnp.int32)
        dst = jax.random.randint(k5, (N_EDGES,), 0, N_NODES, dtype=jnp.int32)
        return {'x': x, 'W': W, 'att_w': att_w, 'src': src, 'dst': dst}
    _L0_gnn_all = _L0_gnn_setup()
    _L0_gnn_in = {k: v for k, v in _L0_gnn_all.items() if k in ('W', 'att_w')}
    del _L0_gnn_all

    def _L1_gnn_setup():
        import jax, jax.numpy as jnp
        import numpy as np
        N, E = (2500, 80000)
        LATENT, HID, OUT, HEADS = (512, 256, 128, 2)
        NEG_SLOPE = 0.2

        def _gat_conv(x, edge_index, Wg, att_src, att_dst, bias_g):
            n = x.shape[0]
            loops = jnp.tile(jnp.arange(n, dtype=edge_index.dtype)[None, :], (2, 1))
            ei = jnp.concatenate([edge_index, loops], axis=1)
            src, dst = (ei[0], ei[1])
            xp = (x @ Wg).reshape(n, HEADS, OUT)
            a_src = jnp.einsum('nhc,hc->nh', xp, att_src)
            a_dst = jnp.einsum('nhc,hc->nh', xp, att_dst)
            alpha = jax.nn.leaky_relu(a_src[src] + a_dst[dst], NEG_SLOPE)
            amax = jax.ops.segment_max(alpha, dst, num_segments=n)
            alpha = jnp.exp(alpha - amax[dst])
            denom = jax.ops.segment_sum(alpha, dst, num_segments=n)
            alpha = alpha / jnp.maximum(denom[dst], 1e-16)
            msg = xp[src] * alpha[:, :, None]
            out = jax.ops.segment_sum(msg, dst, num_segments=n)
            return out.reshape(n, HEADS * OUT) + bias_g
        key = jax.random.key(seed)
        ks = jax.random.split(key, 12)
        s = 0.02
        return {'z': jax.random.normal(ks[0], (N, LATENT), dtype=jnp.float32), 'edge_index': jax.random.randint(ks[1], (2, E), 0, N, dtype=jnp.int64), 'W1': jax.random.normal(ks[2], (LATENT, HID), dtype=jnp.float32) * s, 'b1': jnp.zeros((HID,), dtype=jnp.float32), 'W2': jax.random.normal(ks[3], (HID, HID * HEADS), dtype=jnp.float32) * s, 'b2': jnp.zeros((HID * HEADS,), dtype=jnp.float32), 'Wg': jax.random.normal(ks[4], (HID * HEADS, HEADS * OUT), dtype=jnp.float32) * s, 'att_src': jax.random.normal(ks[5], (HEADS, OUT), dtype=jnp.float32) * s, 'att_dst': jax.random.normal(ks[6], (HEADS, OUT), dtype=jnp.float32) * s, 'bias_g': jnp.zeros((HEADS * OUT,), dtype=jnp.float32), 'W3': jax.random.normal(ks[7], (OUT * HEADS, 512), dtype=jnp.float32) * s, 'b3': jnp.zeros((512,), dtype=jnp.float32)}
    _L1_gnn_all = _L1_gnn_setup()
    _L1_gnn_in = {k: v for k, v in _L1_gnn_all.items() if k in ('W1', 'b1', 'W2', 'b2', 'Wg', 'att_src', 'att_dst', 'bias_g', 'W3', 'b3')}
    del _L1_gnn_all
    return {'x': x, 'src': src, 'dst': dst, 'L0_gnn_W': _L0_gnn_in['W'], 'L0_gnn_att_w': _L0_gnn_in['att_w'], 'L1_gnn_W1': _L1_gnn_in['W1'], 'L1_gnn_b1': _L1_gnn_in['b1'], 'L1_gnn_W2': _L1_gnn_in['W2'], 'L1_gnn_b2': _L1_gnn_in['b2'], 'L1_gnn_Wg': _L1_gnn_in['Wg'], 'L1_gnn_att_src': _L1_gnn_in['att_src'], 'L1_gnn_att_dst': _L1_gnn_in['att_dst'], 'L1_gnn_bias_g': _L1_gnn_in['bias_g'], 'L1_gnn_W3': _L1_gnn_in['W3'], 'L1_gnn_b3': _L1_gnn_in['b3']}

def reference(x, src, dst, L0_gnn_W, L0_gnn_att_w, L1_gnn_W1, L1_gnn_b1, L1_gnn_W2, L1_gnn_b2, L1_gnn_Wg, L1_gnn_att_src, L1_gnn_att_dst, L1_gnn_bias_g, L1_gnn_W3, L1_gnn_b3):
    import jax
    import jax.numpy as jnp

    def _L0_gnn_ref(x, W, att_w, src, dst):
        import jax, jax.numpy as jnp
        import numpy as np
        N_NODES = 6250
        N_EDGES = 200000
        N_HEADS = 8
        IN_DIM = 512
        OUT_DIM = 64
        LRELU_ALPHA = 0.2
        outs = []
        for h in range(N_HEADS):
            feat = x @ W[h]
            a1 = att_w[h, :OUT_DIM]
            a2 = att_w[h, OUT_DIM:]
            alpha_s = feat @ a1
            alpha_d = feat @ a2
            logit = jax.nn.leaky_relu(alpha_s[src] + alpha_d[dst], LRELU_ALPHA)
            m = jax.ops.segment_max(logit, src, num_segments=N_NODES)
            e = jnp.exp(logit - m[src])
            denom = jax.ops.segment_sum(e, src, num_segments=N_NODES)
            att = e / denom[src]
            agg = jax.ops.segment_sum(att[:, None] * feat[dst], src, num_segments=N_NODES)
            outs.append(jax.nn.relu(agg))
        return jnp.concatenate(outs, axis=1)

    def _L1_gnn_ref(z, edge_index, W1, b1, W2, b2, Wg, att_src, att_dst, bias_g, W3, b3):
        import jax, jax.numpy as jnp
        import numpy as np
        N, E = (2500, 80000)
        LATENT, HID, OUT, HEADS = (512, 256, 128, 2)
        NEG_SLOPE = 0.2

        def _gat_conv(x, edge_index, Wg, att_src, att_dst, bias_g):
            n = x.shape[0]
            loops = jnp.tile(jnp.arange(n, dtype=edge_index.dtype)[None, :], (2, 1))
            ei = jnp.concatenate([edge_index, loops], axis=1)
            src, dst = (ei[0], ei[1])
            xp = (x @ Wg).reshape(n, HEADS, OUT)
            a_src = jnp.einsum('nhc,hc->nh', xp, att_src)
            a_dst = jnp.einsum('nhc,hc->nh', xp, att_dst)
            alpha = jax.nn.leaky_relu(a_src[src] + a_dst[dst], NEG_SLOPE)
            amax = jax.ops.segment_max(alpha, dst, num_segments=n)
            alpha = jnp.exp(alpha - amax[dst])
            denom = jax.ops.segment_sum(alpha, dst, num_segments=n)
            alpha = alpha / jnp.maximum(denom[dst], 1e-16)
            msg = xp[src] * alpha[:, :, None]
            out = jax.ops.segment_sum(msg, dst, num_segments=n)
            return out.reshape(n, HEADS * OUT) + bias_g
        x = jax.nn.relu(z @ W1 + b1)
        x = jax.nn.relu(x @ W2 + b2)
        x = _gat_conv(x, edge_index, Wg, att_src, att_dst, bias_g)
        return x @ W3 + b3
    edge_index = jnp.stack([src, dst])
    x = _layernorm(x + _L0_gnn_ref(x, L0_gnn_W, L0_gnn_att_w, src, dst), axis=-1)
    x = _layernorm(x + _L1_gnn_ref(x, edge_index, L1_gnn_W1, L1_gnn_b1, L1_gnn_W2, L1_gnn_b2, L1_gnn_Wg, L1_gnn_att_src, L1_gnn_att_dst, L1_gnn_bias_g, L1_gnn_W3, L1_gnn_b3), axis=-1)
    return x

_drawn_inputs = setup_inputs


def setup_inputs(seed=0):
    import zlib

    import numpy as np

    out = dict(_drawn_inputs(seed))
    spreads = {'L1_gnn_b1': (0.0, 0.8),
     'L1_gnn_b2': (0.0, 0.8),
     'L1_gnn_bias_g': (0.0, 0.8),
     'L1_gnn_b3': (0.0, 0.273)}
    factors = {'L1_gnn_W1': 8.0,
     'L1_gnn_W2': 8.0,
     'L1_gnn_Wg': 4.847,
     'L1_gnn_att_src': 8.0,
     'L1_gnn_att_dst': 8.0}
    for name, (base, spread) in spreads.items():
        noise = np.random.default_rng([zlib.crc32(name.encode()), seed]).standard_normal(out[name].shape)
        drawn = base * np.exp(spread * noise) if base else spread * noise
        out[name] = jnp.asarray(drawn.astype(out[name].dtype))
    for name, factor in factors.items():
        out[name] = (out[name] * factor).astype(out[name].dtype)
    return out
```

```python
from contextlib import ExitStack

import concourse.bass as bass
from concourse import mybir

P = 128
TPB = 8
BATCH = P * TPB
GRP = 4
PAD_LOC = 200
BIG = 1e30
EPS = 1e-5
SLOPE = 0.2

ALU = mybir.AluOpType
ACT = mybir.ActivationFunctionType
AX_X = mybir.AxisListType.X
F32 = mybir.dt.float32
BF16 = mybir.dt.bfloat16
I32 = mybir.dt.int32
U32 = mybir.dt.uint32


def ceil_div(a, b):
    return (a + b - 1) // b


class Shapes:

    def __init__(self, n, d, e):
        self.N, self.D, self.E = n, d, e
        self.BLOCKS = ceil_div(n, P)
        self.BUCKETS = self.BLOCKS + 1
        self.GROUPS = ceil_div(self.BUCKETS, GRP)
        self.SLOTS = self.GROUPS * GRP
        self.COLS = ceil_div(ceil_div(e, P), TPB) * TPB
        filler = P * self.COLS - e
        tiles = (e + self.BLOCKS * (P - 1)) // P + ceil_div(filler, P)
        self.BATCHES = 2 * ceil_div(tiles, 2 * TPB)
        self.TAIL = self.BATCHES + 2
        self.TILES = self.TAIL * TPB


class Chain:

    def __init__(self, eng, sem, start=0):
        self.eng, self.sem, self.value = eng, sem, start

    def step(self, ins):
        ins.then_inc(self.sem, 1)
        self.value = self.value + 1
        self.eng.wait_ge(self.sem, self.value)


def ring(i, u, ahead):
    q = u + ahead
    return q % 2, i + q // 2


def prepare(nc, sh, x, src, dst, W0, att0, lists, tab0, alpha0, look0, block_ids, consts):
    H, _, F = W0.shape
    HF = H * F
    KC = sh.D // P
    C = sh.COLS
    NB = sh.BUCKETS
    iota_n, identity, part_id = consts["iota_n"], consts["identity"], consts["part_id"]
    with ExitStack() as ctx:
        def sb(name, shape, dt):
            return ctx.enter_context(nc.sbuf_tensor(name, shape, dt))

        def psum(name, shape, dt):
            return ctx.enter_context(nc.psum_tensor(name, shape, dt))

        def sem(name):
            return ctx.enter_context(nc.semaphore(name))

        key_i = sb("key_i", [P, C], I32)
        other_i = sb("other_i", [P, C], I32)
        hi_i = sb("hi_i", [P, C], I32)
        hi = sb("hi", [P, C], F32)
        match = sb("match", [P, C], F32)
        rank = sb("rank", [P, C], F32)
        pos = sb("pos", [P, C], F32)
        pos_i = sb("pos_i", [P, C], I32)
        part_a = sb("part_a", [P, C], I32)
        part_b = sb("part_b", [P, C], I32)
        part_c = sb("part_c", [P, C], I32)
        addr = [sb(f"addr{s}", [P, C], I32) for s in range(2)]
        value = [sb(f"value{s}", [P, C, 2], I32) for s in range(2)]
        totals = sb("totals", [P, NB], F32)
        count_i = sb("count_i", [NB, 1], I32)
        aligned_i = sb("aligned_i", [NB, 1], I32)
        aligned = sb("aligned", [NB, 1], F32)
        aligned_bc = sb("aligned_bc", [NB, P], F32)
        starts = sb("starts", [P, NB], F32)
        ends = sb("ends", [NB, 1], F32)
        tile_start = sb("tile_start", [NB, sh.TILES], F32)
        past = sb("past", [NB, sh.TILES], F32)
        before = sb("before", [P, P], F32)
        upto = sb("upto", [P, P], F32)
        ones = sb("ones", [P, 1], F32)
        empty = sb("empty", [P, sh.TILES, 2], I32)
        slot_addr = sb("slot_addr", [P, 4, TPB], I32)
        slot_value = sb("slot_value", [P, 4, TPB, 2], I32)
        w_sb = sb("w_sb", [P, KC, HF], F32)
        att_bc = sb("att_bc", [P, H, 2 * F], F32)
        wa_tmp = sb("wa_tmp", [P, H, F], F32)
        wa = sb("wa", [P, KC, 2 * H], F32)
        x_in = sb("x_in", [P, 2, sh.D], F32)
        xT = sb("xT", [P, 2, KC, P], F32)
        feat = sb("feat", [P, 2, HF + H], F32)
        ps_sort = psum("ps_sort", [P, 512], F32)
        ps_ids = psum("ps_ids", [P, 512], F32)
        ps_xT = psum("ps_xT", [P, 2, 512], F32)
        ps_f = psum("ps_f", [P, 2, 512], F32)
        ps_a = psum("ps_a", [P, 2, 512], F32)

        consts_ready = sem("consts_ready")
        pads_set = sem("pads_set")
        keys_in = sem("keys_in")
        keys_read = sem("keys_read")
        cleared = sem("cleared")
        totals_ready = sem("totals_ready")
        counts_mm = sem("counts_mm")
        aligned_ready = sem("aligned_ready")
        starts_mm = sem("starts_mm")
        past_ready = sem("past_ready")
        ids_mm = sem("ids_mm")
        ids_copied = sem("ids_copied")
        addr_ready = sem("addr_ready")
        slot_in = [sem(f"slot_in{k}") for k in range(4)]
        scattered = [sem(f"scattered{k}") for k in range(4)]
        pool_turn = sem("pool_turn_sort")
        dve = sem("dve_sort")
        pool_step = sem("pool_setup")
        w_in = sem("w_in")
        wa_ready = sem("wa_ready")
        x_loaded = [sem(f"x_loaded{u}") for u in range(2)]
        x_turned = sem("x_turned")
        xT_ready = sem("xT_ready")
        feat_mm = sem("feat_mm")
        feat_copied = sem("feat_copied")
        look_step = sem("look_step")
        feat_stored = [sem(f"feat_stored{u}") for u in range(2)]

        whole = sh.E // C
        rest = sh.E - whole * C
        ROUNDS = C // TPB // 4
        IDC = sh.TILES // 2
        SORTS = ((src, dst), (dst, src))
        block = ctx.enter_context(nc.Block())

        @block.gpsimd
        def _(pool):
            pool.iota(iota_n[:, :], [[1, P]], base=0, channel_multiplier=0,
                      allow_small_or_imprecise_dtypes=True).then_inc(pool_step, 1)
            pool.iota(part_id[:, :], [[1, 1]], base=0, channel_multiplier=1,
                      allow_small_or_imprecise_dtypes=True).then_inc(pool_step, 1)
            pool.iota(tile_start[:, :], [[P, sh.TILES]], base=0, channel_multiplier=0,
                      allow_small_or_imprecise_dtypes=True).then_inc(pool_step, 1)
            pool.memset(ones[:, :], 1.0).then_inc(pool_step, 1)
            pool.wait_ge(pool_step, 4)
            for tri, op in ((identity, ALU.is_equal), (before, ALU.is_gt), (upto, ALU.is_ge)):
                pool.tensor_scalar(tri[:, :], iota_n[:, :], part_id[:, 0:1], None, op).then_inc(consts_ready, 1)
            pool.wait_ge(cleared, 2 * 16)
            for s in range(2):
                with pool.Fori(0, ROUNDS) as i:
                    for k in range(4):
                        pool.wait_ge(slot_in[k], (i + (s * ROUNDS + 1)) * 32)
                        pool.sem_inc(pool_turn)
                        for j in range(TPB):
                            pool.indirect_dma_start(
                                out=lists[s], out_offset=bass.IndirectOffsetOnAxis(
                                    ap=slot_addr[:, k, j:j + 1].bitcast(U32), axis=0),
                                in_=slot_value[:, k, j, :], in_offset=None).then_inc(scattered[k], 16)
            for k in range(4):
                pool.wait_ge(scattered[k], 2 * ROUNDS * TPB * 16)

        @block.sync
        def _(sp):
            sp.wait_ge(pads_set, 3)
            sp.dma_start(lists[0].rearrange("(p c) e -> p (c e)", p=P),
                         empty[:, :, :].rearrange("p c e -> p (c e)")).then_inc(cleared, 16)
            sp.dma_start(lists[1].rearrange("(p c) e -> p (c e)", p=P),
                         empty[:, :, :].rearrange("p c e -> p (c e)")).then_inc(cleared, 16)

            def load_keys(s):
                for tile, arr in zip((key_i, other_i), SORTS[s]):
                    sp.dma_start(tile[0:whole, :], arr[0:whole * C].rearrange("(p c) -> p c", c=C)).then_inc(keys_in, 16)
                    sp.dma_start(tile[whole:whole + 1, 0:rest],
                                 arr[whole * C:sh.E].rearrange("(a c) -> a c", a=1)).then_inc(keys_in, 16)

            load_keys(0)
            sp.wait_ge(keys_read, 1)
            load_keys(1)

            def feed(s, i, k, first):
                if not first:
                    sp.wait_ge(scattered[k], (i + s * ROUNDS) * (16 * TPB))
                at = (i * 4 + k) * TPB
                cut = slice(at, at + TPB) if isinstance(at, int) else bass.ds(at, TPB)
                sp.dma_start(slot_addr[:, k, :], addr[s][:, cut]).then_inc(slot_in[k], 16)
                sp.dma_start(slot_value[:, k, :, :], value[s][:, cut, :]).then_inc(slot_in[k], 16)

            for s in range(2):
                sp.wait_ge(addr_ready, s + 1)
                if s == 0:
                    for k in range(4):
                        feed(0, 0, k, True)
                with sp.Fori(1 if s == 0 else 0, ROUNDS) as i:
                    for k in range(4):
                        feed(s, i, k, False)

        @block.vector
        def _(v):
            v.memset(key_i[:, :], sh.BLOCKS * P).then_inc(pads_set, 1)
            v.memset(other_i[:, :], 0).then_inc(pads_set, 1)
            v.memset(empty[:, :, 0], PAD_LOC).then_inc(dve, 1)
            v.memset(empty[:, :, 1], 0).then_inc(dve, 1)
            v.wait_ge(dve, 2)
            v.memset(empty[:, 0:1, 1], 0).then_inc(pads_set, 1)
            v.wait_ge(w_in, 16 * (KC + 1))
            chain = Chain(v, dve, 2)
            for k in range(KC):
                for part in range(2):
                    a = att_bc[:, :, (1 - part) * F:(2 - part) * F]
                    chain.step(v.tensor_tensor(wa_tmp[:, :, :], w_sb[:, k, :].rearrange("p (h f) -> p h f", h=H), a, ALU.mult))
                    chain.step(v.tensor_reduce(wa[:, k, part * H:(part + 1) * H], wa_tmp[:, :, :], AX_X, ALU.add))
            v.sem_inc(wa_ready)
            v.wait_ge(consts_ready, 3)
            base = chain.value
            for s in range(2):
                chain = Chain(v, dve, base)
                v.wait_ge(keys_in, 64 * (s + 1))
                chain.step(v.tensor_scalar(hi_i[:, :], key_i[:, :], 7, None, ALU.logical_shift_right))
                chain.step(v.tensor_copy(hi[:, :], hi_i[:, :]))
                chain.step(v.tensor_scalar(value[s][:, :, 0], key_i[:, :], P - 1, None, ALU.bitwise_and))
                chain.step(v.tensor_copy(value[s][:, :, 1], other_i[:, :]))
                v.sem_inc(keys_read)
                chain.step(v.memset(pos[:, :], 0.0))
                base = chain.value
                with v.Fori(0, NB) as b:
                    chain = Chain(v, dve, b + base)
                    chain.step(v.tensor_scalar(match[:, :], hi[:, :], iota_n[:, bass.ds(b, 1)], None, ALU.is_equal))
                    v.tensor_reduce(totals[:, bass.ds(b, 1)], match[:, :], AX_X, ALU.add).then_inc(totals_ready, 1)
                    v.wait_ge(totals_ready, b + (s * NB + 1))
                base += NB
                chain = Chain(v, dve, base)
                v.wait_ge(counts_mm, s + 1)
                chain.step(v.tensor_scalar(count_i[:, :], ps_sort[0:NB, 0:1], float(P - 1), None, ALU.add))
                chain.step(v.tensor_scalar(aligned_i[:, :], count_i[:, :], 7, 7, ALU.logical_shift_right, ALU.logical_shift_left))
                chain.step(v.tensor_copy(aligned[:, :], aligned_i[:, :]))
                chain.step(v.tensor_copy(aligned_bc[:, :], aligned[:, 0:1].to_broadcast([NB, P])))
                v.sem_inc(aligned_ready)
                v.wait_ge(starts_mm, s + 1)
                chain.step(v.tensor_copy(starts[:, :], ps_sort[:, 0:NB]))
                chain.step(v.tensor_copy(ends[:, :], ps_sort[0:NB, NB:NB + 1]))
                chain.step(v.tensor_scalar(past[:, :], tile_start[:, :], ends[:, 0:1], None, ALU.is_ge))
                v.sem_inc(past_ready)
                v.wait_ge(ids_mm, s + 1)
                chain.step(v.tensor_scalar(block_ids[s][0:1, 0:IDC], ps_sort[0:1, 0:IDC], float(NB - 1), None, ALU.min))
                chain.step(v.tensor_scalar(block_ids[s][0:1, IDC:2 * IDC], ps_ids[0:1, 0:IDC], float(NB - 1), None, ALU.min))
                v.sem_inc(ids_copied)
                base = chain.value
                with v.Fori(0, NB) as b:
                    chain = Chain(v, dve, b * 4 + base)
                    chain.step(v.tensor_scalar(match[:, :], hi[:, :], iota_n[:, bass.ds(b, 1)], None, ALU.is_equal))
                    chain.step(v.tensor_tensor_scan(rank[:, :], match[:, :], match[:, :], starts[:, bass.ds(b, 1)], ALU.add, ALU.max))
                    chain.step(v.tensor_tensor(match[:, :], match[:, :], rank[:, :], ALU.mult))
                    chain.step(v.tensor_tensor(pos[:, :], pos[:, :], match[:, :], ALU.add))
                base += 4 * NB
                chain = Chain(v, dve, base)
                chain.step(v.tensor_scalar(pos_i[:, :], pos[:, :], -1.0, None, ALU.add))
                chain.step(v.tensor_scalar(part_a[:, :], pos_i[:, :], 10, 10, ALU.logical_shift_right, ALU.logical_shift_left))
                chain.step(v.tensor_scalar(part_b[:, :], pos_i[:, :], P - 1, 3, ALU.bitwise_and, ALU.logical_shift_left))
                chain.step(v.tensor_scalar(part_c[:, :], pos_i[:, :], 7, TPB - 1, ALU.logical_shift_right, ALU.bitwise_and))
                chain.step(v.tensor_tensor(part_a[:, :], part_a[:, :], part_b[:, :], ALU.bitwise_or))
                chain.step(v.tensor_tensor(addr[s][:, :], part_a[:, :], part_c[:, :], ALU.bitwise_or))
                v.sem_inc(addr_ready)
                base = chain.value

        def sort_products(pe, s):
            pe.wait_ge(totals_ready, NB * (s + 1))
            pe.matmul(ps_sort[0:NB, 0:1], totals[:, :], ones[:, 0:1], start=True, stop=True).then_inc(counts_mm, 1)
            pe.wait_ge(aligned_ready, s + 1)
            pe.matmul(ps_sort[:, 0:NB], before[:, :], totals[:, :], start=True, stop=False)
            pe.matmul(ps_sort[:, 0:NB], aligned_bc[:, :], before[0:NB, 0:NB], start=False, stop=True)
            pe.matmul(ps_sort[0:NB, NB:NB + 1], upto[0:NB, 0:NB], aligned[:, :], start=True, stop=True).then_inc(starts_mm, 1)
            pe.wait_ge(past_ready, s + 1)
            pe.matmul(ps_sort[0:1, 0:IDC], ones[0:NB, 0:1], past[:, 0:IDC], start=True, stop=True)
            pe.matmul(ps_ids[0:1, 0:IDC], ones[0:NB, 0:1], past[:, IDC:2 * IDC], start=True, stop=True).then_inc(ids_mm, 1)

        @block.tensor
        def _(pe):
            pe.wait_ge(consts_ready, 3)
            sort_products(pe, 0)
            pe.wait_ge(w_in, 16 * (KC + 1))
            pe.wait_ge(wa_ready, 1)
            with pe.Fori(0, sh.SLOTS // 2) as i:
                for u in range(2):
                    n = i * 2 + u
                    pe.wait_ge(x_loaded[u], i * 16 + 16)
                    for k in range(KC):
                        ins = pe.transpose(ps_xT[:, u, k * P:(k + 1) * P], x_in[:, u, k * P:(k + 1) * P], identity[:, :])
                    ins.then_inc(x_turned, 1)
                    pe.wait_ge(xT_ready, n + 1)
                    pe.wait_ge(feat_copied, n + 1)
                    for k in range(KC):
                        pe.matmul(ps_f[:, u, 0:HF], xT[:, u, k, :], w_sb[:, k, :], start=(k == 0), stop=(k == KC - 1))
                    for k in range(KC):
                        ins = pe.matmul(ps_a[:, u, 0:2 * H], xT[:, u, k, :], wa[:, k, :], start=(k == 0), stop=(k == KC - 1))
                    ins.then_inc(feat_mm, 1)
            pe.wait_ge(ids_copied, 1)
            sort_products(pe, 1)

        @block.scalar
        def _(act):
            for k in range(KC):
                act.dma_start(w_sb[:, k, :].rearrange("p (h f) -> p h f", h=H),
                              W0[:, k * P:(k + 1) * P, :].rearrange("h p f -> p h f")).then_inc(w_in, 16)
            act.dma_start(att_bc[:, :, :], att0.partition_broadcast(P)).then_inc(w_in, 16)
            for u in range(2):
                act.dma_start(x_in[:, u, :], x[u * P:(u + 1) * P, :]).then_inc(x_loaded[u], 16)
            act.sem_inc(feat_copied, 2)

            def one_block(i, u, load, first=False):
                n = i * 2 + u
                act.wait_ge(x_turned, n + 1)
                act.activation(xT[:, u, :, :].rearrange("p k n -> p (k n)"), ps_xT[:, u, :], ACT.Copy).then_inc(xT_ready, 1)
                if load == P:
                    act.dma_start(x_in[:, u, :], x[bass.ds((n + 2) * P, P), :]).then_inc(x_loaded[u], 16)
                elif load:
                    act.dma_start(x_in[0:load, u, :], x[sh.N - load:sh.N, :]).then_inc(x_loaded[u], 16)
                else:
                    act.sem_inc(x_loaded[u], 16)
                act.wait_ge(feat_mm, n + 1)
                if not first:
                    act.wait_ge(feat_stored[u], i * 32)
                act.activation(feat[:, u, 0:HF], ps_f[:, u, 0:HF], ACT.Copy).then_inc(look_step, 1)
                act.activation(feat[:, u, HF:HF + H], ps_a[:, u, 0:H], ACT.Copy).then_inc(look_step, 1)
                act.activation(look_slice(n), ps_a[:, u, H:2 * H], ACT.Copy).then_inc(feat_copied, 1)
                act.wait_ge(look_step, n * 2 + 2)
                rows = bass.ds(n * P, P)
                act.dma_start(tab0[rows, :], feat[:, u, :]).then_inc(feat_stored[u], 16)
                act.dma_start(alpha0[rows, :], feat[:, u, HF:HF + H]).then_inc(feat_stored[u], 16)

            def look_slice(n):
                return look0[:, bass.ds(n * 2 * H, H)]

            last = sh.N - (sh.BLOCKS - 1) * P
            one_block(0, 0, P, first=True)
            one_block(0, 1, P, first=True)
            full = (sh.BLOCKS - 1 - 2) // 2
            with act.Fori(1, full) as i:
                for u in range(2):
                    one_block(i, u, P)
            for n in range(2 * full, sh.SLOTS):
                ahead = n + 2
                load = P if ahead < sh.BLOCKS - 1 else last if ahead == sh.BLOCKS - 1 else None
                one_block(n // 2, n % 2, load)
            for u in range(2):
                act.wait_ge(feat_stored[u], sh.SLOTS // 2 * 32)


def segment_max(nc, sh, tag, H, edges, alpha, look, top, block_ids, consts, unset):
    iota_n, identity = consts["iota_n"], consts["identity"]
    ROW = 3 * H
    HALF = TPB // 2
    HB = min(H, 512 // P)
    BANKS = H // HB
    with ExitStack() as ctx:
        def sb(name, shape, dt):
            return ctx.enter_context(nc.sbuf_tensor(f"{name}{tag}", shape, dt))

        def psum(name, shape, dt):
            return ctx.enter_context(nc.psum_tensor(f"{name}{tag}", shape, dt))

        def sem(name):
            return ctx.enter_context(nc.semaphore(f"{name}{tag}"))

        cols = sb("cols", [P, 2, TPB, 2], I32)
        al = sb("al", [P, 2, TPB, H], F32)
        other_node = sb("other_node", [P, 2, TPB, P], BF16)
        part = sb("part", [P, 2, TPB, 3, H], BF16)
        rem1 = sb("rem1", [P, TPB, H], F32)
        rem2 = sb("rem2", [P, TPB, H], F32)
        partT = sb("partT", [HALF * ROW, 2, 2, P], BF16)
        pick = sb("pick", [HALF * ROW, HALF, H, P], BF16)
        minus_big = sb("minus_big", [P, P], BF16)
        ident_b = sb("ident_b", [P, P], BF16)
        tile_max = sb("tile_max", [P, TPB, H], F32)
        ps_T = psum("ps_T", [HALF * ROW, 2, P], BF16)
        ps_m = psum("ps_m", [P, 2, BANKS, 512], F32)

        cols_in = [sem(f"cols_in{u}_") for u in range(2)]
        gathered = [sem(f"gathered{u}_") for u in range(2)]
        set_up = sem("set_up")
        pick_step = sem("pick_step")
        masks = sem("masks")
        split = sem("split")
        turned = sem("turned")
        turned_copied = sem("turned_copied")
        masked = sem("masked")
        reduced = sem("reduced")
        merged = sem("merged")
        dve = sem("dve_max")
        pool_turn = sem("pool_turn")
        block = ctx.enter_context(nc.Block())

        @block.sync
        def _(sp):
            for u in range(2):
                sp.dma_start(cols[:, u, :, :], edges[u]).then_inc(cols_in[u], 16)
            with sp.Fori(1, sh.TAIL // 2) as i:
                for u in range(2):
                    sp.wait_ge(gathered[u], i * (16 * TPB))
                    sp.wait_ge(masks, i * 2 + (u - 1))
                    sp.dma_start(cols[:, u, :, :], edges[bass.ds(i * 2 + u, 1)].rearrange("a p j e -> (a p) j e")).then_inc(cols_in[u], 16)
            for u in range(2):
                sp.wait_ge(cols_in[u], sh.TAIL // 2 * 16)

        @block.gpsimd
        def _(pool):
            pool.memset(pick[:, :, :, :], 0.0).then_inc(pick_step, 1)
            for part_no in range(3):
                pool.wait_ge(pick_step, part_no + 1)
                pool.affine_select(out=pick[:, :, :, :], in_=pick[:, :, :, :], compare_op=ALU.not_equal, fill=1.0,
                                   base=-part_no * H, pattern=[[-ROW, HALF], [-1, H], [0, P]],
                                   channel_multiplier=1).then_inc(pick_step, 1)

            def gather(i, u):
                pool.wait_ge(cols_in[u], i * 16 + 16)
                pool.sem_inc(pool_turn)
                pool.wait_ge(split, i * 2 + (u + 1))
                pool.sem_inc(pool_turn)
                for j in range(TPB):
                    pool.indirect_dma_start(
                        out=al[:, u, j, :], out_offset=None, in_=alpha,
                        in_offset=bass.IndirectOffsetOnAxis(ap=cols[:, u, j, 1:2].bitcast(U32), axis=0)).then_inc(gathered[u], 16)

            with pool.Fori(0, sh.BATCHES // 2) as i:
                for u in range(2):
                    gather(i, u)
            gather(sh.BATCHES // 2, 0)

        @block.vector
        def _(v):
            v.tensor_scalar(minus_big[:, :], identity[:, :], -BIG, None, ALU.mult).then_inc(set_up, 1)
            v.tensor_copy(ident_b[:, :], identity[:, :]).then_inc(set_up, 1)
            if unset:
                v.memset(top[:, :], -BIG).then_inc(merged, 1)
            else:
                v.sem_inc(merged)
            v.sem_inc(split, 2)
            v.sem_inc(reduced, 2)
            v.sem_inc(masked)

            def mask(i, u):
                v.wait_ge(cols_in[u], i * 16 + 16)
                v.tensor_tensor(other_node[:, u, :, :], iota_n[:, :].unsqueeze(1).broadcast_to([P, TPB, P]),
                                cols[:, u, :, 0:1].broadcast_to([P, TPB, P]), ALU.not_equal).then_inc(masks, 1)

            def split_values(i, u, base):
                v.wait_ge(gathered[u], i * (16 * TPB) + 16 * TPB)
                chain = Chain(v, dve, base)
                chain.step(v.tensor_copy(part[:, u, :, 0, :], al[:, u, :, :]))
                chain.step(v.tensor_tensor(rem1[:, :, :], al[:, u, :, :], part[:, u, :, 0, :], ALU.subtract))
                chain.step(v.tensor_copy(part[:, u, :, 1, :], rem1[:, :, :]))
                chain.step(v.tensor_tensor(rem2[:, :, :], rem1[:, :, :], part[:, u, :, 1, :], ALU.subtract))
                v.tensor_copy(part[:, u, :, 2, :], rem2[:, :, :]).then_inc(split, 1)

            def merge(i, u):
                for j in range(TPB):
                    n = i * (2 * TPB) + (u * TPB + j)
                    b = v.value_load(block_ids[0:1, bass.ds(n, 1)], min_val=0, max_val=sh.BUCKETS - 1)
                    v.wait_ge(masked, n + 2)
                    if H == HB:
                        v.tensor_reduce(tile_max[:, j, :], ps_m[:, j % 2, 0, 0:H * P].rearrange("p (h e) -> p h e", h=H), AX_X, ALU.max).then_inc(reduced, 1)
                    else:
                        v.tensor_reduce(tile_max[:, j, :], ps_m[:, j % 2, :, :].rearrange("p a (h e) -> p (a h) e", h=HB), AX_X, ALU.max).then_inc(reduced, 1)
                    v.wait_ge(reduced, n + 3)
                    v.wait_ge(merged, n + 1)
                    here = top[:, bass.ds(b * H, H)]
                    v.tensor_tensor(here, here, tile_max[:, j, :], ALU.max).then_inc(merged, 1)

            mask(0, 0)
            split_values(0, 0, 0)
            with v.Fori(0, sh.BATCHES // 2) as i:
                for u in range(2):
                    s, k = ring(i, u, 1)
                    v.wait_ge(masked, (i * 2 + u) * TPB + 1)
                    mask(k, s)
                    split_values(k, s, (i * 2 + (u + 1)) * 4)
                    merge(i, u)

        @block.tensor
        def _(pe):
            pe.wait_ge(set_up, 2)
            pe.wait_ge(pick_step, 4)

            def turn(i, u):
                n = i * 2 + u
                pe.wait_ge(split, n + 3)
                pe.wait_ge(turned_copied, n + 1)
                for half in range(2):
                    ins = pe.transpose(ps_T[:, half, :], part[:, u, half * HALF:(half + 1) * HALF, :, :].rearrange("p j s h -> p (j s h)"), ident_b[:, :])
                ins.then_inc(turned, 1)

            turn(0, 0)
            with pe.Fori(0, sh.BATCHES // 2) as i:
                for u in range(2):
                    for j in range(TPB):
                        n = i * (2 * TPB) + (u * TPB + j)
                        if j == 0:
                            pe.wait_ge(masks, i * 2 + (u + 1))
                            pe.wait_ge(turned_copied, i * 2 + (u + 2))
                        if j == HALF:
                            s, k = ring(i, u, 1)
                            turn(k, s)
                        pe.wait_ge(reduced, n + 1)
                        for a in range(BANKS):
                            pe.matmul(ps_m[:, j % 2, a, 0:HB * P], other_node[:, u, j, :],
                                      minus_big[:, :].unsqueeze(1).broadcast_to([P, HB, P]), start=True, stop=False)
                            for h in range(HB):
                                ins = pe.matmul(ps_m[:, j % 2, a, h * P:(h + 1) * P], pick[:, j % HALF, a * HB + h, :],
                                                partT[:, u, j // HALF, :], start=False, stop=(h == HB - 1))
                        ins.then_inc(masked, 1)

        @block.scalar
        def _(act):
            act.sem_inc(turned_copied, 1)

            def copy_turned(i, u):
                act.wait_ge(turned, i * 2 + (u + 1))
                if not isinstance(i, int):
                    act.wait_ge(masked, (i * 2 + (u - 1)) * TPB + 1)
                act.activation(partT[:, u, :, :], ps_T[:, :, :], ACT.Copy).then_inc(turned_copied, 1)

            copy_turned(0, 0)
            with act.Fori(0, sh.BATCHES // 2) as i:
                for u in range(2):
                    s, k = ring(i, u, 1)
                    copy_turned(k, s)


def weighted_sums(nc, sh, tag, H, F, edges, table, look, total, block_ids, consts):
    iota_n, identity = consts["iota_n"], consts["identity"]
    HF = H * F
    R = HF + H
    BANKS = ceil_div(R, 512)
    RB = R // BANKS
    with ExitStack() as ctx:
        def sb(name, shape, dt):
            return ctx.enter_context(nc.sbuf_tensor(f"{name}{tag}", shape, dt))

        def psum(name, shape, dt):
            return ctx.enter_context(nc.psum_tensor(f"{name}{tag}", shape, dt))

        def sem(name):
            return ctx.enter_context(nc.semaphore(f"{name}{tag}"))

        cols = sb("w_cols", [P, 2, TPB, 2], I32)
        rows = sb("w_rows", [P, 2, TPB, R], F32)
        own_node = sb("own_node", [P, 2, TPB, P], F32)
        own_nodeT = sb("own_nodeT", [P, 2, TPB, P], F32)
        z = sb("z", [P, TPB, H], F32)
        z2 = sb("z2", [P, TPB, H], F32)
        arg = sb("arg", [P, TPB, H], F32)
        ps_T = psum("ps_oT", [P, TPB, P], F32)
        ps_look = psum("ps_look", [P, TPB, 2 * H], F32)
        ps_sum = psum("ps_sum", [P, 2, BANKS, 512], F32)

        cols_in = [sem(f"w_cols_in{u}_") for u in range(2)]
        gathered = [sem(f"w_gathered{u}_") for u in range(2)]
        own = sem("own")
        turned = sem("w_turned")
        turned_copied = sem("w_turned_copied")
        looked_up = sem("looked_up")
        arg_ready = sem("arg_ready")
        weights_ready = sem("weights_ready")
        weighted = sem("weighted")
        summed = sem("summed")
        added = sem("added")
        dve = sem("w_dve")
        pool_turn = sem("w_pool_turn")
        block = ctx.enter_context(nc.Block())

        @block.sync
        def _(sp):
            for u in range(2):
                sp.dma_start(cols[:, u, :, :], edges[u]).then_inc(cols_in[u], 16)
            with sp.Fori(1, sh.TAIL // 2) as i:
                for u in range(2):
                    sp.wait_ge(gathered[u], i * (16 * TPB))
                    sp.wait_ge(own, i * 2 + (u - 1))
                    sp.dma_start(cols[:, u, :, :], edges[bass.ds(i * 2 + u, 1)].rearrange("a p j e -> (a p) j e")).then_inc(cols_in[u], 16)
            for u in range(2):
                sp.wait_ge(cols_in[u], sh.TAIL // 2 * 16)

        @block.gpsimd
        def _(pool):
            with pool.Fori(0, sh.BATCHES // 2) as i:
                for u in range(2):
                    pool.wait_ge(cols_in[u], i * 16 + 16)
                    pool.sem_inc(pool_turn)
                    for j in range(TPB):
                        pool.wait_ge(summed, i * (2 * TPB) + (u * TPB + j + 1))
                        pool.sem_inc(pool_turn)
                        pool.indirect_dma_start(
                            out=rows[:, u, j, :], out_offset=None, in_=table,
                            in_offset=bass.IndirectOffsetOnAxis(ap=cols[:, u, j, 1:2].bitcast(U32), axis=0)).then_inc(gathered[u], 16)

        @block.vector
        def _(v):
            v.sem_inc(summed, 2 * TPB)
            v.memset(total[:, :], 0.0).then_inc(added, 2)

            def one_hot(i, u):
                v.wait_ge(cols_in[u], i * 16 + 16)
                v.tensor_tensor(own_node[:, u, :, :], iota_n[:, :].unsqueeze(1).broadcast_to([P, TPB, P]),
                                cols[:, u, :, 0:1].broadcast_to([P, TPB, P]), ALU.is_equal).then_inc(own, 1)

            def arguments(i, u):
                g = i * 2 + u
                v.wait_ge(looked_up, g + 1)
                v.wait_ge(gathered[u], i * (16 * TPB) + 16 * TPB)
                chain = Chain(v, dve, g * 3)
                chain.step(v.tensor_tensor(z[:, :, :], ps_look[:, :, 0:H], rows[:, u, :, HF:R], ALU.add))
                chain.step(v.scalar_tensor_tensor(z2[:, :, :], z[:, :, :], SLOPE, z[:, :, :], ALU.mult, ALU.max))
                chain.step(v.tensor_tensor(z[:, :, :], z2[:, :, :], ps_look[:, :, H:2 * H], ALU.subtract))
                v.tensor_scalar(arg[:, :, :], z[:, :, :], 0.0, None, ALU.min).then_inc(arg_ready, 1)

            def add_tile(i, u, j):
                n = i * (2 * TPB) + (u * TPB + j)
                b = v.value_load(block_ids[0:1, bass.ds(n, 1)], min_val=0, max_val=sh.BUCKETS - 1)
                v.wait_ge(summed, n + (2 * TPB + 1))
                v.wait_ge(added, n + 2)
                here = total[:, bass.ds(b * R, R)].rearrange("p (a c) -> p a c", a=BANKS)
                v.tensor_tensor(here, here, ps_sum[:, j % 2, :, 0:RB], ALU.add).then_inc(added, 1)

            one_hot(0, 0)
            with v.Fori(0, sh.BATCHES // 2) as i:
                for u in range(2):
                    arguments(i, u)
                    s, k = ring(i, u, 1)
                    v.wait_ge(summed, (i * 2 + (u + 2)) * TPB)
                    one_hot(k, s)
                    v.wait_ge(weights_ready, i * 2 + (u + 1))
                    for j in range(TPB):
                        feats = rows[:, u, j, 0:HF].rearrange("p (h f) -> p h f", h=H)
                        v.tensor_tensor(feats, feats, rows[:, u, j, HF:R].unsqueeze(2).broadcast_to([P, H, F]), ALU.mult).then_inc(weighted, 1)
                        if j:
                            add_tile(i, u, j - 1)
                    add_tile(i, u, TPB - 1)

        @block.scalar
        def _(act):
            def copy_turned(i, u):
                act.wait_ge(turned, i * 2 + (u + 1))
                act.activation(own_nodeT[:, u, :, :], ps_T[:, :, :], ACT.Copy).then_inc(turned_copied, 1)

            act.sem_inc(turned_copied)
            copy_turned(0, 0)
            with act.Fori(0, sh.BATCHES // 2) as i:
                for u in range(2):
                    act.wait_ge(arg_ready, i * 2 + (u + 1))
                    act.activation(rows[:, u, :, HF:R], arg[:, :, :], ACT.Exp).then_inc(weights_ready, 1)
                    s, k = ring(i, u, 1)
                    copy_turned(k, s)

        @block.tensor
        def _(pe):
            def turn(i, u):
                g = i * 2 + u
                pe.wait_ge(own, g + 1)
                pe.wait_ge(turned_copied, g + 1)
                for j in range(TPB):
                    ins = pe.transpose(ps_T[:, j, :], own_node[:, u, j, :], identity[:, :])
                ins.then_inc(turned, 1)

            def look_up(i, u):
                g = i * 2 + u
                pe.wait_ge(turned_copied, g + 2)
                for j in range(TPB):
                    b = pe.value_load(block_ids[0:1, bass.ds(i * (2 * TPB) + (u * TPB + j), 1)], min_val=0, max_val=sh.BUCKETS - 1)
                    ins = pe.matmul(ps_look[:, j, :], own_nodeT[:, u, j, :], look[:, bass.ds(b * 2 * H, 2 * H)], start=True, stop=True)
                ins.then_inc(looked_up, 1)

            turn(0, 0)
            look_up(0, 0)
            with pe.Fori(0, sh.BATCHES // 2) as i:
                for u in range(2):
                    s, k = ring(i, u, 1)
                    for j in range(TPB):
                        n = i * (2 * TPB) + (u * TPB + j)
                        if j == TPB // 2:
                            turn(k, s)
                        pe.wait_ge(weighted, n + 1)
                        pe.wait_ge(added, n + 1)
                        for a in range(BANKS):
                            ins = pe.matmul(ps_sum[:, j % 2, a, 0:RB], own_node[:, u, j, :], rows[:, u, j, a * RB:(a + 1) * RB], start=True, stop=True)
                        ins.then_inc(summed, 1)
                    look_up(k, s)


def leaky_max(v, chain, sh, look, top, tmp, H):
    lk = look[:, :].rearrange("p (b c) -> p b c", c=2 * H)
    tp = top[:, :].rearrange("p (b c) -> p b c", c=H)
    tm = tmp[:, :].rearrange("p (b c) -> p b c", c=H)
    chain.step(v.tensor_tensor(tm, lk[:, :, 0:H], tp, ALU.add))
    chain.step(v.scalar_tensor_tensor(lk[:, :, H:2 * H], tm, SLOPE, tm, ALU.mult, ALU.max))


def dense_between(nc, sh, x, H0, F0, total0, zbuf, W1, b1, W2, b2, Wg, att_src, att_dst, tab1, alpha1,
                  look1, top1, self1, consts):
    identity = consts["identity"]
    D = sh.D
    R0 = H0 * F0 + H0
    K0 = D // P
    HID = W1.shape[1]
    M1 = HID // P
    D2 = W2.shape[1]
    M2 = D2 // P
    H1, F1 = att_src.shape
    HF1 = H1 * F1
    R1 = HF1 + H1
    GN = GRP * P
    with ExitStack() as ctx:
        def sb(name, shape, dt):
            return ctx.enter_context(nc.sbuf_tensor(name, shape, dt))

        def psum(name, shape, dt):
            return ctx.enter_context(nc.psum_tensor(name, shape, dt))

        def sem(name):
            return ctx.enter_context(nc.semaphore(name))

        w1 = sb("w1", [P, K0, HID], F32)
        w2 = sb("w2", [P, M1, D2], F32)
        wg = sb("wg", [P, M2, HF1 + 2 * H1], F32)
        att = sb("att", [P, 2, HF1], F32)
        att_tmp = sb("att_tmp", [P, HF1], F32)
        b1c = sb("b1c", [P, M1], F32)
        b2c = sb("b2c", [P, M2], F32)
        x4 = sb("x4", [P, GRP, D], F32)
        y4 = sb("y4", [P, GRP, D], F32)
        z4 = sb("z4", [P, GRP, D], F32)
        den = sb("den", [P, GRP, H0], F32)
        rden = sb("rden", [P, GRP, H0], F32)
        stats = sb("stats", [P, GRP, 6], F32)
        mv = sb("mv", [P, GRP, 2], F32)
        var = sb("var", [P, GRP], F32)
        std = sb("std", [P, GRP], F32)
        rstd = sb("rstd", [P, GRP], F32)
        zT = sb("zT", [P, K0, GN], F32)
        h1T = sb("h1T", [P, M1, GN], F32)
        h2T = sb("h2T", [P, M2, GN], F32)
        row1 = sb("row1", [P, GRP, R1], F32)
        ps_z = psum("ps_z", [P, 2, 512], F32)
        ps_1 = psum("ps_1", [P, 2, 512], F32)
        ps_2 = psum("ps_2", [P, 2, 512], F32)
        ps_x = psum("ps_x", [P, 2, 512], F32)

        weights_in = sem("weights_in")
        att_ready = sem("att_ready")
        x4_in = sem("x4_in")
        added_x = sem("added_x")
        y_ready = sem("y_ready")
        var_ready = sem("var_ready")
        std_ready = sem("std_ready")
        z_ready = sem("z_ready")
        z_turned = sem("z_turned")
        zT_copied = sem("zT_copied")
        h1_mm = sem("h1_mm")
        h1_ready = sem("h1_ready")
        h2_mm = sem("h2_mm")
        h2_ready = sem("h2_ready")
        x1_mm = sem("x1_mm")
        x1_copied = sem("x1_copied")
        row_step = sem("row_step")
        z_stored = sem("z_stored")
        row_stored = sem("row_stored")
        stats_turn = sem("stats_turn")
        aggregated = sem("aggregated")
        dve = sem("dve_dense")
        block = ctx.enter_context(nc.Block())
        FULL = sh.N // GN
        rest = sh.N - FULL * GN
        assert rest and FULL == sh.GROUPS - 1
        full_rest = rest // P
        DSTEPS = 2 * GRP + 4

        @block.sync
        def _(sp):
            sp.dma_start(w1[:, :, :], W1.rearrange("(k p) m -> p k m", p=P)).then_inc(weights_in, 16)
            sp.dma_start(w2[:, :, :], W2.rearrange("(k p) m -> p k m", p=P)).then_inc(weights_in, 16)
            sp.dma_start(wg[:, :, 0:HF1], Wg.rearrange("(k p) m -> p k m", p=P)).then_inc(weights_in, 16)
            sp.dma_start(att[:, 0, :], att_src.rearrange("h f -> (h f)").partition_broadcast(P)).then_inc(weights_in, 16)
            sp.dma_start(att[:, 1, :], att_dst.rearrange("h f -> (h f)").partition_broadcast(P)).then_inc(weights_in, 16)
            with nc.allow_non_contiguous_dma("biases as columns, 3 KB in all"):
                sp.dma_start(b1c[:, :], b1.rearrange("(m p) -> p m", p=P)).then_inc(weights_in, 16)
                sp.dma_start(b2c[:, :], b2.rearrange("(m p) -> p m", p=P)).then_inc(weights_in, 16)

            def load_x(i):
                sp.dma_start(x4[:, :, :], x[bass.ds(i * GN, GN), :].rearrange("(j p) d -> p j d", p=P)).then_inc(x4_in, 16)

            load_x(0)
            with sp.Fori(1, FULL) as i:
                sp.wait_ge(y_ready, i)
                load_x(i)
            sp.wait_ge(y_ready, FULL)
            for j in range(full_rest):
                sp.dma_start(x4[:, j, :], x[FULL * GN + j * P:FULL * GN + (j + 1) * P, :]).then_inc(x4_in, 16)
            if rest % P:
                sp.dma_start(x4[0:rest % P, full_rest, :], x[FULL * GN + full_rest * P:sh.N, :]).then_inc(x4_in, 16)

        @block.vector
        def _(v):
            v.wait_ge(weights_in, 16 * 7)
            chain = Chain(v, dve)
            for k in range(M2):
                for part in range(2):
                    chain.step(v.tensor_tensor(att_tmp[:, :], wg[:, k, 0:HF1], att[:, part, :], ALU.mult))
                    chain.step(v.tensor_reduce(wg[:, k, HF1 + part * H1:HF1 + (part + 1) * H1],
                                               att_tmp[:, :].rearrange("p (h f) -> p h f", h=H1), AX_X, ALU.add))
            v.sem_inc(att_ready)
            base = chain.value

            def group(i, loads, first=False):
                chain = Chain(v, dve, i * DSTEPS + base)
                at = i * (GRP * R0)
                tot = total0[:, bass.ds(at, GRP * R0)].rearrange("p (j r) -> p j r", r=R0)
                chain.step(v.tensor_scalar(den[:, :, :], tot[:, :, H0 * F0:R0], 1e-30, None, ALU.max))
                chain.step(v.reciprocal(rden[:, :, :], den[:, :, :]))
                for j in range(GRP):
                    chain.step(v.tensor_tensor(y4[:, j, :].rearrange("p (h f) -> p h f", h=H0),
                                               tot[:, j, 0:H0 * F0].rearrange("p (h f) -> p h f", h=H0),
                                               rden[:, j, :].unsqueeze(2).broadcast_to([P, H0, F0]), ALU.mult))
                v.wait_ge(x4_in, loads)
                for j in range(GRP):
                    v.scalar_tensor_tensor(y4[:, j, :], y4[:, j, :], 0.0, x4[:, j, :], ALU.max, ALU.add).then_inc(added_x, 1)
                v.wait_ge(added_x, i * GRP + GRP)
                v.sem_inc(y_ready)
                for j in range(GRP):
                    chain.step(v.bn_stats(stats[:, j, :], y4[:, j, :]))
                v.sem_inc(stats_turn)
                for j in range(GRP):
                    v.bn_aggr(mv[:, j, :], stats[:, j, :]).then_inc(aggregated, 1)
                v.wait_ge(aggregated, i * GRP + GRP)
                chain.step(v.tensor_scalar(var[:, :], mv[:, :, 1], EPS, None, ALU.add))
                v.sem_inc(var_ready)
                v.wait_ge(std_ready, i + 1)
                chain.step(v.reciprocal(rstd[:, :], std[:, :]))
                if not first:
                    v.wait_ge(z_stored, i * 16)
                v.wait_ge(z_turned, i * K0 + 1)
                for j in range(GRP):
                    v.tensor_scalar(z4[:, j, :], y4[:, j, :], mv[:, j, 0:1], rstd[:, j:j + 1], ALU.subtract, ALU.mult).then_inc(z_ready, 1)
                v.wait_ge(z_ready, i * GRP + GRP)

            v.sem_inc(z_turned)
            group(0, 16, first=True)
            with v.Fori(1, FULL) as i:
                group(i, i * 16 + 16)
            group(FULL, FULL * 16 + 16 * (full_rest + (1 if rest % P else 0)))

        @block.scalar
        def _(act):
            act.wait_ge(weights_in, 16 * 7)

            def std_and_store(i):
                act.wait_ge(var_ready, i + 1)
                act.activation(std[:, :], var[:, :], ACT.Sqrt).then_inc(std_ready, 1)
                act.wait_ge(z_ready, i * GRP + GRP)
                act.dma_start(zbuf[bass.ds(i * GN, GN), :].rearrange("(j p) d -> p j d", p=P), z4[:, :, :]).then_inc(z_stored, 16)

            def chain_of_layers(i, first=False):
                for k in range(K0):
                    act.wait_ge(z_turned, i * K0 + (k + 2))
                    act.activation(zT[:, k, :], ps_z[:, k % 2, :], ACT.Copy).then_inc(zT_copied, 1)
                for m in range(M1):
                    act.wait_ge(h1_mm, i * M1 + (m + 1))
                    act.activation(h1T[:, m, :], ps_1[:, m % 2, :], ACT.Relu, bias=b1c[:, m:m + 1]).then_inc(h1_ready, 1)
                for m in range(M2):
                    act.wait_ge(h2_mm, i * M2 + (m + 1))
                    act.activation(h2T[:, m, :], ps_2[:, m % 2, :], ACT.Relu, bias=b2c[:, m:m + 1]).then_inc(h2_ready, 1)
                if not first:
                    act.wait_ge(row_stored, i * 32)
                for j in range(GRP):
                    act.wait_ge(x1_mm, i * GRP + (j + 1))
                    ps = ps_x[:, j % 2, :]
                    at = i * GRP + j
                    act.activation(row1[:, j, :], ps[:, 0:R1], ACT.Copy).then_inc(row_step, 1)
                    act.activation(top1[:, bass.ds(at * H1, H1)], ps[:, HF1:R1], ACT.Copy).then_inc(row_step, 1)
                    act.activation(self1[:, bass.ds(at * H1, H1)], ps[:, HF1:R1], ACT.Copy).then_inc(row_step, 1)
                    act.activation(look1[:, bass.ds(at * 2 * H1, H1)], ps[:, R1:R1 + H1], ACT.Copy).then_inc(x1_copied, 1)
                act.wait_ge(row_step, i * (3 * GRP) + 3 * GRP)
                nodes = bass.ds(i * GN, GN)
                act.dma_start(tab1[nodes, :].rearrange("(j p) d -> p j d", p=P), row1[:, :, :]).then_inc(row_stored, 16)
                act.dma_start(alpha1[nodes, :].rearrange("(j p) d -> p j d", p=P), row1[:, :, HF1:R1]).then_inc(row_stored, 16)

            act.sem_inc(x1_copied, 2)
            std_and_store(0)
            chain_of_layers(0, first=True)
            with act.Fori(1, sh.GROUPS) as i:
                std_and_store(i)
                chain_of_layers(i)
            act.wait_ge(z_stored, sh.GROUPS * 16)
            act.wait_ge(row_stored, sh.GROUPS * 32)

        @block.tensor
        def _(pe):
            pe.wait_ge(att_ready, 1)
            with pe.Fori(0, sh.GROUPS) as i:
                pe.wait_ge(z_ready, i * GRP + GRP)
                for k in range(K0):
                    if k >= 2:
                        pe.wait_ge(zT_copied, i * K0 + (k - 1))
                    for j in range(GRP):
                        ins = pe.transpose(ps_z[:, k % 2, j * P:(j + 1) * P], z4[:, j, k * P:(k + 1) * P], identity[:, :])
                    ins.then_inc(z_turned, 1)
                pe.wait_ge(zT_copied, i * K0 + K0)
                for m in range(M1):
                    for k in range(K0):
                        ins = pe.matmul(ps_1[:, m % 2, :], w1[:, k, m * P:(m + 1) * P], zT[:, k, :], start=(k == 0), stop=(k == K0 - 1))
                    ins.then_inc(h1_mm, 1)
                pe.wait_ge(h1_ready, i * M1 + M1)
                for m in range(M2):
                    if m >= 2:
                        pe.wait_ge(h2_ready, i * M2 + (m - 1))
                    for k in range(M1):
                        ins = pe.matmul(ps_2[:, m % 2, :], w2[:, k, m * P:(m + 1) * P], h1T[:, k, :], start=(k == 0), stop=(k == M1 - 1))
                    ins.then_inc(h2_mm, 1)
                pe.wait_ge(h2_ready, i * M2 + M2)
                for j in range(GRP):
                    pe.wait_ge(x1_copied, i * GRP + (j + 1))
                    for k in range(M2):
                        ins = pe.matmul(ps_x[:, j % 2, 0:R1 + H1], h2T[:, k, j * P:(j + 1) * P], wg[:, k, :], start=(k == 0), stop=(k == M2 - 1))
                    ins.then_inc(x1_mm, 1)


def output(nc, sh, H, F, total1, zbuf, tab1, look1, top1, self1, bias_g, W3, b3, out, consts):
    identity = consts["identity"]
    D = sh.D
    HF = H * F
    R = HF + H
    K = HF // P
    GN = GRP * P
    S = sh.SLOTS
    with ExitStack() as ctx:
        def sb(name, shape, dt):
            return ctx.enter_context(nc.sbuf_tensor(name, shape, dt))

        def psum(name, shape, dt):
            return ctx.enter_context(nc.psum_tensor(name, shape, dt))

        def sem(name):
            return ctx.enter_context(nc.semaphore(name))

        w3 = sb("w3", [P, K, D], F32)
        b3r = sb("b3r", [P, D], F32)
        bg = sb("bg", [P, HF], F32)
        self_z = sb("self_z", [P, S, H], F32)
        self_l = sb("self_l", [P, S, H], F32)
        self_a = sb("self_a", [P, S, H], F32)
        self_w = sb("self_w", [P, S, H], F32)
        den = sb("o_den", [P, S, H], F32)
        den2 = sb("o_den2", [P, S, H], F32)
        rden = sb("o_rden", [P, S, H], F32)
        zin = sb("zin", [P, 2, D], F32)
        xp = sb("xp", [P, 2, R], F32)
        num = sb("num", [P, 2, HF], F32)
        agg = sb("agg", [P, 2, HF], F32)
        aggT = sb("aggT", [P, 2, K, P], F32)
        y = sb("o_y", [P, 2, D], F32)
        y2 = sb("o_y2", [P, 2, D], F32)
        stats = sb("o_stats", [P, 2, 6], F32)
        mv = sb("o_mv", [P, 2, 2], F32)
        var = sb("o_var", [P, 2], F32)
        std = sb("o_std", [P, 2], F32)
        rstd = sb("o_rstd", [P, 2], F32)
        res = sb("res", [P, 2, D], F32)
        ps_t = psum("o_ps_t", [P, 2, 512], F32)
        ps_o = psum("o_ps_o", [P, 2, 512], F32)

        weights_in = sem("o_weights_in")
        rows_in = [sem(f"o_rows_in{u}") for u in range(2)]
        self_step = sem("self_step")
        self_exp = sem("self_exp")
        num_ready = sem("num_ready")
        agg_ready = sem("agg_ready")
        turned = sem("o_turned")
        aggT_ready = sem("aggT_ready")
        out_mm = sem("out_mm")
        y_ready = sem("o_y_ready")
        var_ready = sem("o_var_ready")
        std_ready = sem("o_std_ready")
        res_ready = sem("res_ready")
        stored = [sem(f"o_stored{u}") for u in range(2)]
        stats_turn = sem("o_stats_turn")
        dve = sem("o_dve")
        block = ctx.enter_context(nc.Block())
        last = sh.N - (sh.BLOCKS - 1) * P
        PAIRS = ceil_div(sh.BLOCKS, 2)
        STEPS = 5

        @block.sync
        def _(sp):
            sp.dma_start(w3[:, :, :], W3.rearrange("(k p) m -> p k m", p=P)).then_inc(weights_in, 16)
            sp.dma_start(b3r[:, :], b3.partition_broadcast(P)).then_inc(weights_in, 16)
            sp.dma_start(bg[:, :], bias_g.partition_broadcast(P)).then_inc(weights_in, 16)

            def load(i, u):
                at = bass.ds((i * 2 + u) * P, P)
                sp.dma_start(zin[:, u, :], zbuf[at, :]).then_inc(rows_in[u], 16)
                sp.dma_start(xp[:, u, :], tab1[at, :]).then_inc(rows_in[u], 16)

            load(0, 0)
            load(0, 1)
            with sp.Fori(1, PAIRS) as i:
                for u in range(2):
                    sp.wait_ge(y_ready, i * 2 + (u + 1))
                    load(i, u)

        @block.vector
        def _(v):
            v.sem_inc(y_ready, 2)
            tot = total1[:, :].rearrange("p (b r) -> p b r", r=R)
            lk = look1[:, :].rearrange("p (b c) -> p b c", c=2 * H)
            chain = Chain(v, self_step)
            chain.step(v.tensor_tensor(self_z[:, :, :], lk[:, :, 0:H], self1[:, :].rearrange("p (b c) -> p b c", c=H), ALU.add))
            chain.step(v.scalar_tensor_tensor(self_l[:, :, :], self_z[:, :, :], SLOPE, self_z[:, :, :], ALU.mult, ALU.max))
            chain.step(v.tensor_tensor(self_a[:, :, :], self_l[:, :, :], lk[:, :, H:2 * H], ALU.subtract))
            v.wait_ge(self_exp, 1)
            chain.step(v.tensor_tensor(den[:, :, :], tot[:, :, HF:R], self_w[:, :, :], ALU.add))
            chain.step(v.tensor_scalar(den2[:, :, :], den[:, :, :], 1e-16, None, ALU.max))
            chain.step(v.reciprocal(rden[:, :, :], den2[:, :, :]))
            v.wait_ge(weights_in, 48)

            def heads(i, u, first=False):
                n = i * 2 + u
                v.wait_ge(rows_in[u], i * 32 + 32)
                for h in range(H):
                    c = slice(h * F, (h + 1) * F)
                    sw = self_w[:, :, :].rearrange("p b h -> p (b h)")[:, bass.ds(n * H + h, 1)]
                    v.scalar_tensor_tensor(num[:, u, c], xp[:, u, c], sw, total1[:, bass.ds(n * R + h * F, F)],
                                           ALU.mult, ALU.add).then_inc(num_ready, 1)
                v.wait_ge(num_ready, n * H + H)
                if not first:
                    v.wait_ge(turned, n - 1)
                for h in range(H):
                    c = slice(h * F, (h + 1) * F)
                    rd = rden[:, :, :].rearrange("p b h -> p (b h)")[:, bass.ds(n * H + h, 1)]
                    v.scalar_tensor_tensor(agg[:, u, c], num[:, u, c], rd, bg[:, c], ALU.mult, ALU.add).then_inc(agg_ready, 1)

            def norm(i, u, first=False):
                n = i * 2 + u
                chain = Chain(v, dve, n * STEPS)
                v.wait_ge(out_mm, n + 1)
                chain.step(v.tensor_tensor(y[:, u, :], ps_o[:, u, :], zin[:, u, :], ALU.add))
                v.sem_inc(y_ready)
                chain.step(v.tensor_tensor(y2[:, u, :], y[:, u, :], b3r[:, :], ALU.add))
                chain.step(v.bn_stats(stats[:, u, :], y2[:, u, :]))
                v.sem_inc(stats_turn)
                chain.step(v.bn_aggr(mv[:, u, :], stats[:, u, :]))
                v.tensor_scalar(var[:, u:u + 1], mv[:, u, 1:2], EPS, None, ALU.add).then_inc(var_ready, 1)
                v.wait_ge(std_ready, n + 1)
                chain.step(v.reciprocal(rstd[:, u:u + 1], std[:, u:u + 1]))
                if not first:
                    v.wait_ge(stored[u], i * 16)
                v.tensor_scalar(res[:, u, :], y2[:, u, :], mv[:, u, 0:1], rstd[:, u:u + 1], ALU.subtract, ALU.mult).then_inc(res_ready, 1)

            heads(0, 0, first=True)
            heads(0, 1, first=True)
            norm(0, 0, first=True)
            heads(1, 0)
            norm(0, 1, first=True)
            heads(1, 1)
            norm(1, 0)
            with v.Fori(2, PAIRS) as i:
                heads(i, 0)
                norm(i - 1, 1)
                heads(i, 1)
                norm(i, 0)
            norm(PAIRS - 1, 1)

        @block.tensor
        def _(pe):
            pe.wait_ge(weights_in, 48)
            with pe.Fori(0, PAIRS) as i:
                for u in range(2):
                    n = i * 2 + u
                    pe.wait_ge(agg_ready, n * H + H)
                    for k in range(K):
                        ins = pe.transpose(ps_t[:, u, k * P:(k + 1) * P], agg[:, u, k * P:(k + 1) * P], identity[:, :])
                    ins.then_inc(turned, 1)
                    pe.wait_ge(aggT_ready, n + 1)
                    pe.wait_ge(y_ready, n + 1)
                    for k in range(K):
                        ins = pe.matmul(ps_o[:, u, 0:D], aggT[:, u, k, :], w3[:, k, :], start=(k == 0), stop=(k == K - 1))
                    ins.then_inc(out_mm, 1)

        @block.scalar
        def _(act):
            act.wait_ge(self_step, 3)
            act.activation(self_w[:, :, :], self_a[:, :, :], ACT.Exp).then_inc(self_exp, 1)

            def one_block(i, u, count):
                n = i * 2 + u
                act.wait_ge(turned, n + 1)
                act.activation(aggT[:, u, :, :].rearrange("p k n -> p (k n)"), ps_t[:, u, 0:HF], ACT.Copy).then_inc(aggT_ready, 1)
                act.wait_ge(var_ready, n + 1)
                act.activation(std[:, u:u + 1], var[:, u:u + 1], ACT.Sqrt).then_inc(std_ready, 1)
                act.wait_ge(res_ready, n + 1)
                if count == P:
                    act.dma_start(out[bass.ds(n * P, P), :], res[:, u, :]).then_inc(stored[u], 16)
                elif count:
                    act.dma_start(out[sh.N - count:sh.N, :], res[0:count, u, :]).then_inc(stored[u], 16)

            full = (sh.BLOCKS - 1) // 2
            with act.Fori(0, full) as i:
                for u in range(2):
                    one_block(i, u, P)
            for n in range(2 * full, 2 * PAIRS):
                one_block(n // 2, n % 2, P if n < sh.BLOCKS - 1 else last if n == sh.BLOCKS - 1 else 0)
            for u in range(2):
                act.wait_ge(stored[u], 16 * ((sh.BLOCKS + 1 - u) // 2))


def gnn(nc, x, src, dst, W0, att0, W1, b1, W2, b2, Wg, att_src, att_dst, bias_g, W3, b3, out):
    sh = Shapes(x.shape[0], x.shape[1], src.shape[0])
    H0, _, F0 = W0.shape
    H1, F1 = att_src.shape
    R0, R1 = H0 * F0 + H0, H1 * F1 + H1
    rows = sh.SLOTS * P

    def dram(name, shape, dt):
        return nc.dram_tensor(name, shape, dt, kind="Internal").ap()

    lists = [dram(f"edges_{s}", (sh.TAIL * BATCH, 2), I32) for s in ("by_src", "by_dst")]
    batches = [l.rearrange("(g p j) e -> g p j e", p=P, j=TPB) for l in lists]
    tab0 = dram("table0", (rows, R0), F32)
    alpha0 = dram("alpha0", (rows, H0), F32)
    zbuf = dram("z", (rows, sh.D), F32)
    tab1 = dram("table1", (rows, R1), F32)
    alpha1 = dram("alpha1", (rows, H1), F32)

    with ExitStack() as ctx:
        def sb(name, shape, dt):
            return ctx.enter_context(nc.sbuf_tensor(name, shape, dt))

        def sem(name):
            return ctx.enter_context(nc.semaphore(name))

        consts = {
            "iota_n": sb("iota_n", [P, P], F32),
            "identity": sb("identity", [P, P], F32),
            "part_id": sb("part_id", [P, 1], F32),
        }
        block_ids = [sb(f"block_ids{s}", [1, sh.TILES], I32) for s in range(2)]
        look0 = sb("look0", [P, sh.SLOTS * 2 * H0], F32)
        top0 = sb("top0", [P, sh.SLOTS * H0], F32)
        look1 = sb("look1", [P, sh.SLOTS * 2 * H1], F32)
        top1 = sb("top1", [P, sh.SLOTS * H1], F32)
        self1 = sb("self1", [P, sh.SLOTS * H1], F32)
        max_tmp = sb("max_tmp", [P, sh.SLOTS * max(H0, H1)], F32)

        def finish_max(name, look, top, H):
            with nc.semaphore(name) as step, nc.Block() as block:
                @block.vector
                def _(v):
                    leaky_max(v, Chain(v, step), sh, look, top, max_tmp[:, 0:sh.SLOTS * H], H)

        prepare(nc, sh, x, src, dst, W0, att0, lists, tab0, alpha0, look0, block_ids, consts)
        segment_max(nc, sh, "_0", H0, batches[0], alpha0, look0, top0, block_ids[0], consts, unset=True)
        finish_max("max_step_0", look0, top0, H0)
        with nc.sbuf_tensor("total0", [P, sh.SLOTS * R0], F32) as total0:
            weighted_sums(nc, sh, "_0", H0, F0, batches[0], tab0, look0, total0, block_ids[0], consts)
            dense_between(nc, sh, x, H0, F0, total0, zbuf, W1, b1, W2, b2, Wg, att_src, att_dst,
                          tab1, alpha1, look1, top1, self1, consts)
        segment_max(nc, sh, "_1", H1, batches[1], alpha1, look1, top1, block_ids[1], consts, unset=False)
        finish_max("max_step_1", look1, top1, H1)
        with nc.sbuf_tensor("total1", [P, sh.SLOTS * R1], F32) as total1:
            weighted_sums(nc, sh, "_1", H1, F1, batches[1], tab1, look1, total1, block_ids[1], consts)
            output(nc, sh, H1, F1, total1, zbuf, tab1, look1, top1, self1, bias_g, W3, b3, out, consts)


_INS = ['x', 'src', 'dst', 'L0_gnn_W', 'L0_gnn_att_w', 'L1_gnn_W1', 'L1_gnn_b1', 'L1_gnn_W2', 'L1_gnn_b2', 'L1_gnn_Wg',
        'L1_gnn_att_src', 'L1_gnn_att_dst', 'L1_gnn_bias_g', 'L1_gnn_W3', 'L1_gnn_b3']


def kernel(**inputs):
    import numpy as _np
    import concourse.bacc as _bacc
    from concourse import mybir as _mybir
    from concourse.bass_utils import run_bass_kernel_spmd as _run

    nc = _bacc.Bacc("TRN2", target_bir_lowering=False, num_devices=1)
    arrays, args = {}, []
    for name in _INS:
        a = _np.ascontiguousarray(inputs[name])
        arrays[f"in_{name}_dram"] = a
        args.append(nc.dram_tensor(f"in_{name}_dram", a.shape, _mybir.dt.from_np(a.dtype), kind="ExternalInput").ap())
    args.append(nc.dram_tensor("out_0_dram", inputs['x'].shape, F32, kind="ExternalOutput").ap())
    gnn(nc, *args)
    r = _run(nc, [arrays], core_ids=[0])
    return r.results[0]["out_0_dram"]
```

```python
from contextlib import ExitStack

import concourse.bass as bass
from concourse import mybir

P = 128
TPB = 8
BATCH = P * TPB
GRP = 4
PAD_LOC = 200
BIG = 1e30
EPS = 1e-5
SLOPE = 0.2

ALU = mybir.AluOpType
ACT = mybir.ActivationFunctionType
AX_X = mybir.AxisListType.X
F32 = mybir.dt.float32
BF16 = mybir.dt.bfloat16
I32 = mybir.dt.int32
U32 = mybir.dt.uint32


BANK_HELD = [1, 1] + [0] * (TPB - 2)


def ceil_div(a, b):
    return (a + b - 1) // b


class Shapes:

    def __init__(self, n, d, e):
        self.N, self.D, self.E = n, d, e
        self.BLOCKS = ceil_div(n, P)
        self.BUCKETS = self.BLOCKS + 1
        self.GROUPS = ceil_div(self.BUCKETS, GRP)
        self.SLOTS = self.GROUPS * GRP
        self.COLS = ceil_div(ceil_div(e, P), TPB) * TPB
        filler = P * self.COLS - e
        tiles = (e + self.BLOCKS * (P - 1)) // P + ceil_div(filler, P)
        self.BATCHES = 2 * ceil_div(tiles, 2 * TPB)
        self.TAIL = self.BATCHES + 2
        self.TILES = self.TAIL * TPB


class Chain:

    def __init__(self, eng, sem, start=0):
        self.eng, self.sem, self.value = eng, sem, start

    def step(self, ins):
        ins.then_inc(self.sem, 1)
        self.value = self.value + 1
        self.eng.wait_ge(self.sem, self.value)


def ring(i, u, ahead):
    q = u + ahead
    return q % 2, i + q // 2


def blocks_of(nc, sh, engine, block_ids, i, u):
    at = (i * 2 + u) * TPB
    ids = block_ids[0:1, bass.ds(at, TPB)]
    return nc.values_load_multi_w_load_instructions(
        ids, engines=(engine,), min_val=0, max_val=sh.BUCKETS - 1,
        skip_runtime_bounds_check_because="the table's values are a count from 0, capped when it is made")[1]


def prepare(nc, sh, x, src, dst, W0, att0, lists, addr1, value1, tab0, alpha0, look0, block_ids, consts):
    H, _, F = W0.shape
    HF = H * F
    KC = sh.D // P
    C = sh.COLS
    NB = sh.BUCKETS
    iota_n, identity, part_id = consts["iota_n"], consts["identity"], consts["part_id"]
    with ExitStack() as ctx:
        def sb(name, shape, dt):
            return ctx.enter_context(nc.sbuf_tensor(name, shape, dt))

        def psum(name, shape, dt):
            return ctx.enter_context(nc.psum_tensor(name, shape, dt))

        def sem(name):
            return ctx.enter_context(nc.semaphore(name))

        key_i = sb("key_i", [P, C], I32)
        other_i = sb("other_i", [P, C], I32)
        hi_i = sb("hi_i", [P, C], I32)
        hi = sb("hi", [P, C], F32)
        match = sb("match", [P, C], F32)
        rank = sb("rank", [P, C], F32)
        pos = sb("pos", [P, C], F32)
        pos_i = sb("pos_i", [P, C], I32)
        part_a = sb("part_a", [P, C], I32)
        part_b = sb("part_b", [P, C], I32)
        part_c = sb("part_c", [P, C], I32)
        addr = [sb("addr0", [P, C], I32), addr1]
        value = [sb("value0", [P, C, 2], I32), value1]
        totals = sb("totals", [P, NB], F32)
        count_i = sb("count_i", [NB, 1], I32)
        aligned_i = sb("aligned_i", [NB, 1], I32)
        aligned = sb("aligned", [NB, 1], F32)
        aligned_bc = sb("aligned_bc", [NB, P], F32)
        starts = sb("starts", [P, NB], F32)
        ends = sb("ends", [NB, 1], F32)
        tile_start = sb("tile_start", [NB, sh.TILES], F32)
        past = sb("past", [NB, sh.TILES], F32)
        before = sb("before", [P, P], F32)
        upto = sb("upto", [P, P], F32)
        ones = sb("ones", [P, 1], F32)
        empty = sb("empty", [P, sh.TILES, 2], I32)
        slot_addr = sb("slot_addr", [P, 4, TPB], I32)
        slot_value = sb("slot_value", [P, 4, TPB, 2], I32)
        w_sb = sb("w_sb", [P, KC, HF], F32)
        att_bc = sb("att_bc", [P, H, 2 * F], F32)
        wa_tmp = sb("wa_tmp", [P, H, F], F32)
        wa = sb("wa", [P, KC, 2 * H], F32)
        x_in = sb("x_in", [P, 2, sh.D], F32)
        xT = sb("xT", [P, 2, KC, P], F32)
        feat = sb("feat", [P, 2, HF + H], F32)
        ps_sort = psum("ps_sort", [P, 512], F32)
        ps_ids = psum("ps_ids", [P, 512], F32)
        ps_xT = psum("ps_xT", [P, 2, 512], F32)
        ps_f = psum("ps_f", [P, 2, 512], F32)
        ps_a = psum("ps_a", [P, 2, 512], F32)

        consts_ready = sem("consts_ready")
        pads_set = sem("pads_set")
        keys_in = sem("keys_in")
        keys_read = sem("keys_read")
        cleared = sem("cleared")
        totals_ready = sem("totals_ready")
        counts_mm = sem("counts_mm")
        aligned_ready = sem("aligned_ready")
        starts_mm = sem("starts_mm")
        past_ready = sem("past_ready")
        ids_mm = sem("ids_mm")
        ids_copied = sem("ids_copied")
        addr_ready = sem("addr_ready")
        slot_in = [sem(f"slot_in{k}") for k in range(4)]
        scattered = [sem(f"scattered{k}") for k in range(4)]
        pool_turn = sem("pool_turn_sort")
        dve = sem("dve_sort")
        pool_step = sem("pool_setup")
        w_in = sem("w_in")
        wa_ready = sem("wa_ready")
        x_loaded = [sem(f"x_loaded{u}") for u in range(2)]
        x_turned = sem("x_turned")
        xT_ready = sem("xT_ready")
        feat_mm = sem("feat_mm")
        feat_copied = sem("feat_copied")
        look_step = sem("look_step")
        feat_stored = [sem(f"feat_stored{u}") for u in range(2)]

        whole = sh.E // C
        rest = sh.E - whole * C
        ROUNDS = C // TPB // 4
        IDC = sh.TILES // 2
        SORTS = ((src, dst), (dst, src))
        block = ctx.enter_context(nc.Block())

        @block.gpsimd
        def _(pool):
            pool.iota(iota_n[:, :], [[1, P]], base=0, channel_multiplier=0,
                      allow_small_or_imprecise_dtypes=True).then_inc(pool_step, 1)
            pool.iota(part_id[:, :], [[1, 1]], base=0, channel_multiplier=1,
                      allow_small_or_imprecise_dtypes=True).then_inc(pool_step, 1)
            pool.iota(tile_start[:, :], [[P, sh.TILES]], base=0, channel_multiplier=0,
                      allow_small_or_imprecise_dtypes=True).then_inc(pool_step, 1)
            pool.memset(ones[:, :], 1.0).then_inc(pool_step, 1)
            pool.wait_ge(pool_step, 4)
            for tri, op in ((identity, ALU.is_equal), (before, ALU.is_gt), (upto, ALU.is_ge)):
                pool.tensor_scalar(tri[:, :], iota_n[:, :], part_id[:, 0:1], None, op).then_inc(consts_ready, 1)
            pool.wait_ge(cleared, 2 * 16)
            with pool.Fori(0, ROUNDS) as i:
                for k in range(4):
                    pool.wait_ge(slot_in[k], i * 32 + 32)
                    pool.sem_inc(pool_turn)
                    for j in range(TPB):
                        pool.indirect_dma_start(
                            out=lists[0], out_offset=bass.IndirectOffsetOnAxis(
                                ap=slot_addr[:, k, j:j + 1].bitcast(U32), axis=0),
                            in_=slot_value[:, k, j, :], in_offset=None).then_inc(scattered[k], 16)
            for k in range(4):
                pool.wait_ge(scattered[k], ROUNDS * TPB * 16)

        @block.sync
        def _(sp):
            sp.wait_ge(pads_set, 3)
            sp.dma_start(lists[0].rearrange("(p c) e -> p (c e)", p=P),
                         empty[:, :, :].rearrange("p c e -> p (c e)")).then_inc(cleared, 16)
            sp.dma_start(lists[1].rearrange("(p c) e -> p (c e)", p=P),
                         empty[:, :, :].rearrange("p c e -> p (c e)")).then_inc(cleared, 16)

            def load_keys(s):
                for tile, arr in zip((key_i, other_i), SORTS[s]):
                    sp.dma_start(tile[0:whole, :], arr[0:whole * C].rearrange("(p c) -> p c", c=C)).then_inc(keys_in, 16)
                    sp.dma_start(tile[whole:whole + 1, 0:rest],
                                 arr[whole * C:sh.E].rearrange("(a c) -> a c", a=1)).then_inc(keys_in, 16)

            load_keys(0)
            sp.wait_ge(keys_read, 1)
            load_keys(1)

            def feed(i, k, first=False):
                if not first:
                    sp.wait_ge(scattered[k], i * (16 * TPB))
                cut = bass.ds((i * 4 + k) * TPB, TPB)
                sp.dma_start(slot_addr[:, k, :], addr[0][:, cut]).then_inc(slot_in[k], 16)
                sp.dma_start(slot_value[:, k, :, :], value[0][:, cut, :]).then_inc(slot_in[k], 16)

            sp.wait_ge(addr_ready, 1)
            for k in range(4):
                feed(0, k, first=True)
            with sp.Fori(1, ROUNDS) as i:
                for k in range(4):
                    feed(i, k)

        @block.vector
        def _(v):
            v.memset(key_i[:, :], sh.BLOCKS * P).then_inc(pads_set, 1)
            v.memset(other_i[:, :], 0).then_inc(pads_set, 1)
            v.memset(empty[:, :, 0], PAD_LOC).then_inc(dve, 1)
            v.memset(empty[:, :, 1], 0).then_inc(dve, 1)
            v.wait_ge(dve, 2)
            v.memset(empty[:, 0:1, 1], 0).then_inc(pads_set, 1)
            v.wait_ge(w_in, 16 * (KC + 1))
            chain = Chain(v, dve, 2)
            for k in range(KC):
                for part in range(2):
                    a = att_bc[:, :, (1 - part) * F:(2 - part) * F]
                    chain.step(v.tensor_tensor(wa_tmp[:, :, :], w_sb[:, k, :].rearrange("p (h f) -> p h f", h=H), a, ALU.mult))
                    chain.step(v.tensor_reduce(wa[:, k, part * H:(part + 1) * H], wa_tmp[:, :, :], AX_X, ALU.add))
            v.sem_inc(wa_ready)
            v.wait_ge(consts_ready, 3)
            base = chain.value
            for s in range(2):
                chain = Chain(v, dve, base)
                v.wait_ge(keys_in, 64 * (s + 1))
                chain.step(v.tensor_scalar(hi_i[:, :], key_i[:, :], 7, None, ALU.logical_shift_right))
                chain.step(v.tensor_copy(hi[:, :], hi_i[:, :]))
                chain.step(v.tensor_scalar(value[s][:, :, 0], key_i[:, :], P - 1, None, ALU.bitwise_and))
                chain.step(v.tensor_copy(value[s][:, :, 1], other_i[:, :]))
                v.sem_inc(keys_read)
                chain.step(v.memset(pos[:, :], 0.0))
                base = chain.value
                with v.Fori(0, NB) as b:
                    chain = Chain(v, dve, b + base)
                    chain.step(v.tensor_scalar(match[:, :], hi[:, :], iota_n[:, bass.ds(b, 1)], None, ALU.is_equal))
                    v.tensor_reduce(totals[:, bass.ds(b, 1)], match[:, :], AX_X, ALU.add).then_inc(totals_ready, 1)
                    v.wait_ge(totals_ready, b + (s * NB + 1))
                base += NB
                chain = Chain(v, dve, base)
                v.wait_ge(counts_mm, s + 1)
                chain.step(v.tensor_scalar(count_i[:, :], ps_sort[0:NB, 0:1], float(P - 1), None, ALU.add))
                chain.step(v.tensor_scalar(aligned_i[:, :], count_i[:, :], 7, 7, ALU.logical_shift_right, ALU.logical_shift_left))
                chain.step(v.tensor_copy(aligned[:, :], aligned_i[:, :]))
                chain.step(v.tensor_copy(aligned_bc[:, :], aligned[:, 0:1].to_broadcast([NB, P])))
                v.sem_inc(aligned_ready)
                v.wait_ge(starts_mm, s + 1)
                chain.step(v.tensor_copy(starts[:, :], ps_sort[:, 0:NB]))
                chain.step(v.tensor_copy(ends[:, :], ps_sort[0:NB, NB:NB + 1]))
                chain.step(v.tensor_scalar(past[:, :], tile_start[:, :], ends[:, 0:1], None, ALU.is_ge))
                v.sem_inc(past_ready)
                v.wait_ge(ids_mm, s + 1)
                chain.step(v.tensor_scalar(block_ids[s][0:1, 0:IDC], ps_sort[0:1, 0:IDC], float(NB - 1), None, ALU.min))
                chain.step(v.tensor_scalar(block_ids[s][0:1, IDC:2 * IDC], ps_ids[0:1, 0:IDC], float(NB - 1), None, ALU.min))
                v.sem_inc(ids_copied)
                base = chain.value
                with v.Fori(0, NB) as b:
                    chain = Chain(v, dve, b * 4 + base)
                    chain.step(v.tensor_scalar(match[:, :], hi[:, :], iota_n[:, bass.ds(b, 1)], None, ALU.is_equal))
                    chain.step(v.tensor_tensor_scan(rank[:, :], match[:, :], match[:, :], starts[:, bass.ds(b, 1)], ALU.add, ALU.max))
                    chain.step(v.tensor_tensor(match[:, :], match[:, :], rank[:, :], ALU.mult))
                    chain.step(v.tensor_tensor(pos[:, :], pos[:, :], match[:, :], ALU.add))
                base += 4 * NB
                chain = Chain(v, dve, base)
                chain.step(v.tensor_scalar(pos_i[:, :], pos[:, :], -1.0, None, ALU.add))
                chain.step(v.tensor_scalar(part_a[:, :], pos_i[:, :], 10, 10, ALU.logical_shift_right, ALU.logical_shift_left))
                chain.step(v.tensor_scalar(part_b[:, :], pos_i[:, :], P - 1, 3, ALU.bitwise_and, ALU.logical_shift_left))
                chain.step(v.tensor_scalar(part_c[:, :], pos_i[:, :], 7, TPB - 1, ALU.logical_shift_right, ALU.bitwise_and))
                chain.step(v.tensor_tensor(part_a[:, :], part_a[:, :], part_b[:, :], ALU.bitwise_or))
                chain.step(v.tensor_tensor(addr[s][:, :], part_a[:, :], part_c[:, :], ALU.bitwise_or))
                v.sem_inc(addr_ready)
                base = chain.value

        def sort_products(pe, s):
            pe.wait_ge(totals_ready, NB * (s + 1))
            pe.matmul(ps_sort[0:NB, 0:1], totals[:, :], ones[:, 0:1], start=True, stop=True).then_inc(counts_mm, 1)
            pe.wait_ge(aligned_ready, s + 1)
            pe.matmul(ps_sort[:, 0:NB], before[:, :], totals[:, :], start=True, stop=False)
            pe.matmul(ps_sort[:, 0:NB], aligned_bc[:, :], before[0:NB, 0:NB], start=False, stop=True)
            pe.matmul(ps_sort[0:NB, NB:NB + 1], upto[0:NB, 0:NB], aligned[:, :], start=True, stop=True).then_inc(starts_mm, 1)
            pe.wait_ge(past_ready, s + 1)
            pe.matmul(ps_sort[0:1, 0:IDC], ones[0:NB, 0:1], past[:, 0:IDC], start=True, stop=True)
            pe.matmul(ps_ids[0:1, 0:IDC], ones[0:NB, 0:1], past[:, IDC:2 * IDC], start=True, stop=True).then_inc(ids_mm, 1)

        @block.tensor
        def _(pe):
            pe.wait_ge(consts_ready, 3)
            sort_products(pe, 0)
            pe.wait_ge(w_in, 16 * (KC + 1))
            pe.wait_ge(wa_ready, 1)
            with pe.Fori(0, sh.SLOTS // 2) as i:
                for u in range(2):
                    n = i * 2 + u
                    pe.wait_ge(x_loaded[u], i * 16 + 16)
                    for k in range(KC):
                        ins = pe.transpose(ps_xT[:, u, k * P:(k + 1) * P], x_in[:, u, k * P:(k + 1) * P], identity[:, :])
                    ins.then_inc(x_turned, 1)
                    pe.wait_ge(xT_ready, n + 1)
                    pe.wait_ge(feat_copied, n + 1)
                    for k in range(KC):
                        pe.matmul(ps_f[:, u, 0:HF], xT[:, u, k, :], w_sb[:, k, :], start=(k == 0), stop=(k == KC - 1))
                    for k in range(KC):
                        ins = pe.matmul(ps_a[:, u, 0:2 * H], xT[:, u, k, :], wa[:, k, :], start=(k == 0), stop=(k == KC - 1))
                    ins.then_inc(feat_mm, 1)
            pe.wait_ge(ids_copied, 1)
            sort_products(pe, 1)

        @block.scalar
        def _(act):
            for k in range(KC):
                act.dma_start(w_sb[:, k, :].rearrange("p (h f) -> p h f", h=H),
                              W0[:, k * P:(k + 1) * P, :].rearrange("h p f -> p h f")).then_inc(w_in, 16)
            act.dma_start(att_bc[:, :, :], att0.partition_broadcast(P)).then_inc(w_in, 16)
            for u in range(2):
                act.dma_start(x_in[:, u, :], x[u * P:(u + 1) * P, :]).then_inc(x_loaded[u], 16)
            act.sem_inc(feat_copied, 2)

            def one_block(i, u, load, first=False):
                n = i * 2 + u
                act.wait_ge(x_turned, n + 1)
                act.activation(xT[:, u, :, :].rearrange("p k n -> p (k n)"), ps_xT[:, u, :], ACT.Copy).then_inc(xT_ready, 1)
                if load == P:
                    act.dma_start(x_in[:, u, :], x[bass.ds((n + 2) * P, P), :]).then_inc(x_loaded[u], 16)
                elif load:
                    act.dma_start(x_in[0:load, u, :], x[sh.N - load:sh.N, :]).then_inc(x_loaded[u], 16)
                else:
                    act.sem_inc(x_loaded[u], 16)
                act.wait_ge(feat_mm, n + 1)
                if not first:
                    act.wait_ge(feat_stored[u], i * 32)
                act.activation(feat[:, u, 0:HF], ps_f[:, u, 0:HF], ACT.Copy).then_inc(look_step, 1)
                act.activation(feat[:, u, HF:HF + H], ps_a[:, u, 0:H], ACT.Copy).then_inc(look_step, 1)
                act.activation(look_slice(n), ps_a[:, u, H:2 * H], ACT.Copy).then_inc(feat_copied, 1)
                act.wait_ge(look_step, n * 2 + 2)
                rows = bass.ds(n * P, P)
                act.dma_start(tab0[rows, :], feat[:, u, :]).then_inc(feat_stored[u], 16)
                act.dma_start(alpha0[rows, :], feat[:, u, HF:HF + H]).then_inc(feat_stored[u], 16)

            def look_slice(n):
                return look0[:, bass.ds(n * 2 * H, H)]

            last = sh.N - (sh.BLOCKS - 1) * P
            one_block(0, 0, P, first=True)
            one_block(0, 1, P, first=True)
            full = (sh.BLOCKS - 1 - 2) // 2
            with act.Fori(1, full) as i:
                for u in range(2):
                    one_block(i, u, P)
            for n in range(2 * full, sh.SLOTS):
                ahead = n + 2
                load = P if ahead < sh.BLOCKS - 1 else last if ahead == sh.BLOCKS - 1 else None
                one_block(n // 2, n % 2, load)
            for u in range(2):
                act.wait_ge(feat_stored[u], sh.SLOTS // 2 * 32)


class Scatter:

    PART = TPB // 2

    def __init__(self, nc, ctx, tag, out, addr, value, first, rounds):
        self.out, self.addr, self.value, self.first, self.rounds = out, addr, value, first, rounds
        self.slot_addr = ctx.enter_context(nc.sbuf_tensor(f"s_addr{first}", [P, 2, self.PART], I32))
        self.slot_value = ctx.enter_context(nc.sbuf_tensor(f"s_value{first}", [P, 2, self.PART, 2], I32))
        self.slot_in = [ctx.enter_context(nc.semaphore(f"s_slot_in{u}_{first}")) for u in range(2)]
        self.scattered = [ctx.enter_context(nc.semaphore(f"s_scattered{u}_{first}")) for u in range(2)]

    def feed(self, sp, i, u, first=False):
        if not first:
            sp.wait_ge(self.scattered[u], i * (16 * self.PART))
        cut = bass.ds((i * 2 + u) * self.PART + self.first, self.PART)
        sp.dma_start(self.slot_addr[:, u, :], self.addr[:, cut]).then_inc(self.slot_in[u], 16)
        sp.dma_start(self.slot_value[:, u, :, :], self.value[:, cut, :]).then_inc(self.slot_in[u], 16)

    def wait_slot(self, pool, turn, i, u):
        pool.wait_ge(self.slot_in[u], i * 32 + 32)
        pool.sem_inc(turn)

    def put(self, pool, u, c):
        pool.indirect_dma_start(
            out=self.out, out_offset=bass.IndirectOffsetOnAxis(ap=self.slot_addr[:, u, c:c + 1].bitcast(U32), axis=0),
            in_=self.slot_value[:, u, c, :], in_offset=None).then_inc(self.scattered[u], 16)

    def wait_all(self, pool):
        for u in range(2):
            pool.wait_ge(self.scattered[u], self.rounds * 16 * self.PART)


def segment_max(nc, sh, tag, H, edges, alpha, look, top, block_ids, consts, unset, scatter=None):
    iota_n, identity = consts["iota_n"], consts["identity"]
    ROW = 3 * H
    HALF = TPB // 2
    HB = min(H, 512 // P)
    BANKS = H // HB
    with ExitStack() as ctx:
        def sb(name, shape, dt):
            return ctx.enter_context(nc.sbuf_tensor(f"{name}{tag}", shape, dt))

        def psum(name, shape, dt):
            return ctx.enter_context(nc.psum_tensor(f"{name}{tag}", shape, dt))

        def sem(name):
            return ctx.enter_context(nc.semaphore(f"{name}{tag}"))

        cols = sb("cols", [P, 2, TPB, 2], I32)
        al = sb("al", [P, 2, TPB, H], F32)
        other_node = sb("other_node", [P, 2, TPB, P], BF16)
        part = sb("part", [P, 2, TPB, 3, H], BF16)
        rem1 = sb("rem1", [P, TPB, H], F32)
        rem2 = sb("rem2", [P, TPB, H], F32)
        partT = sb("partT", [HALF * ROW, 2, 2, P], BF16)
        pick = sb("pick", [HALF * ROW, HALF, H, P], BF16)
        minus_big = sb("minus_big", [P, P], BF16)
        ident_b = sb("ident_b", [P, P], BF16)
        tile_max = sb("tile_max", [P, TPB, H], F32)
        ps_T = psum("ps_T", [HALF * ROW, 2, P], BF16)
        ps_m = psum("ps_m", [P, 3, BANKS, 512], F32)

        cols_in = [sem(f"cols_in{u}_") for u in range(2)]
        gathered = [sem(f"gathered{u}_") for u in range(2)]
        set_up = sem("set_up")
        pick_step = sem("pick_step")
        side = Scatter(nc, ctx, tag, *scatter) if scatter else None
        masks = sem("masks")
        split = sem("split")
        turned = sem("turned")
        turned_copied = sem("turned_copied")
        masked = sem("masked")
        reduced = sem("reduced")
        merged = sem("merged")
        dve = sem("dve_max")
        pool_turn = sem("pool_turn")
        block = ctx.enter_context(nc.Block())

        @block.sync
        def _(sp):
            for u in range(2):
                sp.dma_start(cols[:, u, :, :], edges[u]).then_inc(cols_in[u], 16)
            if side:
                for u in range(2):
                    side.feed(sp, 0, u, first=True)

            def load(i, u, feed):
                sp.wait_ge(gathered[u], i * (16 * TPB))
                sp.wait_ge(masks, i * 2 + (u - 1))
                sp.dma_start(cols[:, u, :, :], edges[bass.ds(i * 2 + u, 1)].rearrange("a p j e -> (a p) j e")).then_inc(cols_in[u], 16)
                if feed:
                    side.feed(sp, i, u)

            with_side = side.rounds if side else 1
            if side:
                with sp.Fori(1, with_side) as i:
                    for u in range(2):
                        load(i, u, True)
            with sp.Fori(with_side, sh.TAIL // 2) as i:
                for u in range(2):
                    load(i, u, False)
            for u in range(2):
                sp.wait_ge(cols_in[u], sh.TAIL // 2 * 16)

        @block.gpsimd
        def _(pool):
            pool.memset(pick[:, :, :, :], 0.0).then_inc(pick_step, 1)
            for part_no in range(3):
                pool.wait_ge(pick_step, part_no + 1)
                pool.affine_select(out=pick[:, :, :, :], in_=pick[:, :, :, :], compare_op=ALU.not_equal, fill=1.0,
                                   base=-part_no * H, pattern=[[-ROW, HALF], [-1, H], [0, P]],
                                   channel_multiplier=1).then_inc(pick_step, 1)

            def gather(i, u, beside=False):
                pool.wait_ge(cols_in[u], i * 16 + 16)
                pool.sem_inc(pool_turn)
                pool.wait_ge(split, i * 2 + (u + 1))
                pool.sem_inc(pool_turn)
                if beside:
                    side.wait_slot(pool, pool_turn, i, u)
                for j in range(TPB):
                    pool.indirect_dma_start(
                        out=al[:, u, j, :], out_offset=None, in_=alpha,
                        in_offset=bass.IndirectOffsetOnAxis(ap=cols[:, u, j, 1:2].bitcast(U32), axis=0)).then_inc(gathered[u], 16)
                    if beside and j % 2:
                        side.put(pool, u, j // 2)

            with_side = side.rounds if side else 0
            if side:
                with pool.Fori(0, with_side) as i:
                    for u in range(2):
                        gather(i, u, beside=True)
            if with_side < sh.BATCHES // 2:
                with pool.Fori(with_side, sh.BATCHES // 2) as i:
                    for u in range(2):
                        gather(i, u)
            gather(sh.BATCHES // 2, 0)
            if side:
                side.wait_all(pool)

        @block.vector
        def _(v):
            v.tensor_scalar(minus_big[:, :], identity[:, :], -BIG, None, ALU.mult).then_inc(set_up, 1)
            v.tensor_copy(ident_b[:, :], identity[:, :]).then_inc(set_up, 1)
            if unset:
                v.memset(top[:, :], -BIG).then_inc(merged, 1)
            else:
                v.sem_inc(merged)
            v.sem_inc(split, 2)
            v.sem_inc(reduced, 3)
            v.sem_inc(masked)

            def mask(i, u):
                v.wait_ge(cols_in[u], i * 16 + 16)
                v.tensor_tensor(other_node[:, u, :, :], iota_n[:, :].unsqueeze(1).broadcast_to([P, TPB, P]),
                                cols[:, u, :, 0:1].broadcast_to([P, TPB, P]), ALU.not_equal).then_inc(masks, 1)

            def split_values(i, u, base):
                v.wait_ge(gathered[u], i * (16 * TPB) + 16 * TPB)
                chain = Chain(v, dve, base)
                chain.step(v.tensor_copy(part[:, u, :, 0, :], al[:, u, :, :]))
                chain.step(v.tensor_tensor(rem1[:, :, :], al[:, u, :, :], part[:, u, :, 0, :], ALU.subtract))
                chain.step(v.tensor_copy(part[:, u, :, 1, :], rem1[:, :, :]))
                chain.step(v.tensor_tensor(rem2[:, :, :], rem1[:, :, :], part[:, u, :, 1, :], ALU.subtract))
                v.tensor_copy(part[:, u, :, 2, :], rem2[:, :, :]).then_inc(split, 1)

            def merge(i, u):
                blocks = blocks_of(nc, sh, mybir.EngineType.DVE, block_ids, i, u)
                first = i * (2 * TPB) + u * TPB
                for j in range(TPB + 1):
                    if j < TPB:
                        v.wait_ge(masked, first + (j + 2))
                        if H == HB:
                            in_ = ps_m[:, j % 3, 0, 0:H * P].rearrange("p (h e) -> p h e", h=H)
                        else:
                            in_ = ps_m[:, j % 3, :, :].rearrange("p a (h e) -> p (a h) e", h=HB)
                        v.tensor_reduce(tile_max[:, j, :], in_, AX_X, ALU.max).then_inc(reduced, 1)
                    if j:
                        v.wait_ge(reduced, first + (j + 3))
                        v.wait_ge(merged, first + j)
                        here = top[:, bass.ds(blocks[j - 1] * H, H)]
                        v.tensor_tensor(here, here, tile_max[:, j - 1, :], ALU.max).then_inc(merged, 1)

            mask(0, 0)
            split_values(0, 0, 0)
            with v.Fori(0, sh.BATCHES // 2) as i:
                for u in range(2):
                    s, k = ring(i, u, 1)
                    v.wait_ge(masked, (i * 2 + u) * TPB + 1)
                    mask(k, s)
                    split_values(k, s, (i * 2 + (u + 1)) * 4)
                    merge(i, u)

        @block.tensor
        def _(pe):
            pe.wait_ge(set_up, 2)
            pe.wait_ge(pick_step, 4)

            def turn(i, u):
                n = i * 2 + u
                pe.wait_ge(split, n + 3)
                pe.wait_ge(turned_copied, n + 1)
                for half in range(2):
                    ins = pe.transpose(ps_T[:, half, :], part[:, u, half * HALF:(half + 1) * HALF, :, :].rearrange("p j s h -> p (j s h)"), ident_b[:, :])
                ins.then_inc(turned, 1)

            turn(0, 0)
            with pe.Fori(0, sh.BATCHES // 2) as i:
                for u in range(2):
                    for j in range(TPB):
                        n = i * (2 * TPB) + (u * TPB + j)
                        if j == 0:
                            pe.wait_ge(masks, i * 2 + (u + 1))
                            pe.wait_ge(turned_copied, i * 2 + (u + 2))
                        if j == HALF:
                            s, k = ring(i, u, 1)
                            turn(k, s)
                        pe.wait_ge(reduced, n + 1 + BANK_HELD[j])
                        for a in range(BANKS):
                            pe.matmul(ps_m[:, j % 3, a, 0:HB * P], other_node[:, u, j, :],
                                      minus_big[:, :].unsqueeze(1).broadcast_to([P, HB, P]), start=True, stop=False)
                            for h in range(HB):
                                ins = pe.matmul(ps_m[:, j % 3, a, h * P:(h + 1) * P], pick[:, j % HALF, a * HB + h, :],
                                                partT[:, u, j // HALF, :], start=False, stop=(h == HB - 1))
                        ins.then_inc(masked, 1)

        @block.scalar
        def _(act):
            act.sem_inc(turned_copied, 1)

            def copy_turned(i, u):
                act.wait_ge(turned, i * 2 + (u + 1))
                if not isinstance(i, int):
                    act.wait_ge(masked, (i * 2 + (u - 1)) * TPB + 1)
                act.activation(partT[:, u, :, :], ps_T[:, :, :], ACT.Copy).then_inc(turned_copied, 1)

            copy_turned(0, 0)
            with act.Fori(0, sh.BATCHES // 2) as i:
                for u in range(2):
                    s, k = ring(i, u, 1)
                    copy_turned(k, s)


def weighted_sums(nc, sh, tag, H, F, edges, table, look, total, block_ids, consts, scatter=None):
    iota_n, identity = consts["iota_n"], consts["identity"]
    HF = H * F
    R = HF + H
    BANKS = ceil_div(R, 512)
    RB = R // BANKS
    HALF = TPB // 2
    with ExitStack() as ctx:
        def sb(name, shape, dt):
            return ctx.enter_context(nc.sbuf_tensor(f"{name}{tag}", shape, dt))

        def psum(name, shape, dt):
            return ctx.enter_context(nc.psum_tensor(f"{name}{tag}", shape, dt))

        def sem(name):
            return ctx.enter_context(nc.semaphore(f"{name}{tag}"))

        cols = sb("w_cols", [P, 2, TPB, 2], I32)
        rows = sb("w_rows", [P, 2, TPB, R], F32)
        own_node = sb("own_node", [P, 2, TPB, P], F32)
        own_nodeT = sb("own_nodeT", [P, 2, TPB, P], F32)
        z = sb("z", [P, TPB, H], F32)
        z2 = sb("z2", [P, TPB, H], F32)
        arg = sb("arg", [P, TPB, H], F32)
        ps_T = psum("ps_oT", [P, HALF, P], F32)
        ps_look = psum("ps_look", [P, TPB, 2 * H], F32)
        ps_sum = psum("ps_sum", [P, 3, BANKS, 512], F32)

        cols_in = [sem(f"w_cols_in{u}_") for u in range(2)]
        gathered = [sem(f"w_gathered{u}_") for u in range(2)]
        own = sem("own")
        turned = sem("w_turned")
        turned_copied = sem("w_turned_copied")
        looked_up = sem("looked_up")
        arg_ready = sem("arg_ready")
        weights_ready = sem("weights_ready")
        side = Scatter(nc, ctx, tag, *scatter) if scatter else None
        weighted = sem("weighted")
        summed = sem("summed")
        added = sem("added")
        dve = sem("w_dve")
        pool_turn = sem("w_pool_turn")
        block = ctx.enter_context(nc.Block())

        @block.sync
        def _(sp):
            for u in range(2):
                sp.dma_start(cols[:, u, :, :], edges[u]).then_inc(cols_in[u], 16)
            if side:
                for u in range(2):
                    side.feed(sp, 0, u, first=True)

            def load(i, u, feed):
                sp.wait_ge(gathered[u], i * (16 * TPB))
                sp.wait_ge(own, i * 2 + (u - 1))
                sp.dma_start(cols[:, u, :, :], edges[bass.ds(i * 2 + u, 1)].rearrange("a p j e -> (a p) j e")).then_inc(cols_in[u], 16)
                if feed:
                    side.feed(sp, i, u)

            with_side = side.rounds if side else 1
            if side:
                with sp.Fori(1, with_side) as i:
                    for u in range(2):
                        load(i, u, True)
            with sp.Fori(with_side, sh.TAIL // 2) as i:
                for u in range(2):
                    load(i, u, False)
            for u in range(2):
                sp.wait_ge(cols_in[u], sh.TAIL // 2 * 16)

        @block.gpsimd
        def _(pool):
            def gather(i, u, beside=False):
                pool.wait_ge(cols_in[u], i * 16 + 16)
                pool.sem_inc(pool_turn)
                if beside:
                    side.wait_slot(pool, pool_turn, i, u)
                for j in range(TPB):
                    pool.wait_ge(summed, i * (2 * TPB) + (u * TPB + j + 1))
                    pool.sem_inc(pool_turn)
                    pool.indirect_dma_start(
                        out=rows[:, u, j, :], out_offset=None, in_=table,
                        in_offset=bass.IndirectOffsetOnAxis(ap=cols[:, u, j, 1:2].bitcast(U32), axis=0)).then_inc(gathered[u], 16)
                    if beside and j % 2:
                        side.put(pool, u, j // 2)

            with_side = side.rounds if side else 0
            if side:
                with pool.Fori(0, with_side) as i:
                    for u in range(2):
                        gather(i, u, beside=True)
            if with_side < sh.BATCHES // 2:
                with pool.Fori(with_side, sh.BATCHES // 2) as i:
                    for u in range(2):
                        gather(i, u)
            gather(sh.BATCHES // 2, 0)
            if side:
                side.wait_all(pool)

        @block.vector
        def _(v):
            v.sem_inc(summed, 2 * TPB)
            v.memset(total[:, :], 0.0).then_inc(added, 3)

            def one_hot(i, u):
                v.wait_ge(cols_in[u], i * 16 + 16)
                v.tensor_tensor(own_node[:, u, :, :], iota_n[:, :].unsqueeze(1).broadcast_to([P, TPB, P]),
                                cols[:, u, :, 0:1].broadcast_to([P, TPB, P]), ALU.is_equal).then_inc(own, 1)

            def arguments(i, u):
                g = i * 2 + u
                v.wait_ge(looked_up, g + 1)
                v.wait_ge(gathered[u], i * (16 * TPB) + 16 * TPB)
                chain = Chain(v, dve, g * 3)
                chain.step(v.tensor_tensor(z[:, :, :], ps_look[:, :, 0:H], rows[:, u, :, HF:R], ALU.add))
                chain.step(v.scalar_tensor_tensor(z2[:, :, :], z[:, :, :], SLOPE, z[:, :, :], ALU.mult, ALU.max))
                chain.step(v.tensor_tensor(z[:, :, :], z2[:, :, :], ps_look[:, :, H:2 * H], ALU.subtract))
                if not (isinstance(g, int) and g == 0):
                    v.wait_ge(weights_ready, g)
                v.tensor_scalar(arg[:, :, :], z[:, :, :], 0.0, None, ALU.min).then_inc(arg_ready, 1)

            def weigh(i, u, j):
                feats = rows[:, u, j, 0:HF].rearrange("p (h f) -> p h f", h=H)
                v.tensor_tensor(feats, feats, rows[:, u, j, HF:R].unsqueeze(2).broadcast_to([P, H, F]), ALU.mult).then_inc(weighted, 1)

            def add_tile(i, u, j, b):
                n = i * (2 * TPB) + (u * TPB + j)
                v.wait_ge(summed, n + (2 * TPB + 1))
                v.wait_ge(added, n + 3)
                here = total[:, bass.ds(b * R, R)].rearrange("p (a c) -> p a c", a=BANKS)
                v.tensor_tensor(here, here, ps_sum[:, j % 3, :, 0:RB], ALU.add).then_inc(added, 1)

            one_hot(0, 0)
            arguments(0, 0)
            with v.Fori(0, sh.BATCHES // 2) as i:
                for u in range(2):
                    blocks = blocks_of(nc, sh, mybir.EngineType.DVE, block_ids, i, u)
                    s, k = ring(i, u, 1)
                    v.wait_ge(weights_ready, i * 2 + (u + 1))
                    for j in range(TPB):
                        weigh(i, u, j)
                        if j == 0:
                            v.wait_ge(summed, (i * 2 + (u + 2)) * TPB)
                            one_hot(k, s)
                        if j >= 2:
                            add_tile(i, u, j - 2, blocks[j - 2])
                    arguments(k, s)
                    add_tile(i, u, TPB - 2, blocks[TPB - 2])
                    add_tile(i, u, TPB - 1, blocks[TPB - 1])

        @block.scalar
        def _(act):
            def copy_turned(i, u, half):
                act.wait_ge(turned, (i * 2 + u) * 2 + (half + 1))
                act.activation(own_nodeT[:, u, half * HALF:(half + 1) * HALF, :], ps_T[:, :, :], ACT.Copy).then_inc(turned_copied, 1)

            def exponentials(i, u):
                act.wait_ge(arg_ready, i * 2 + (u + 1))
                act.activation(rows[:, u, :, HF:R], arg[:, :, :], ACT.Exp).then_inc(weights_ready, 1)

            act.sem_inc(turned_copied)
            for half in range(2):
                copy_turned(0, 0, half)
            exponentials(0, 0)
            with act.Fori(0, sh.BATCHES // 2) as i:
                for u in range(2):
                    s, k = ring(i, u, 1)
                    for half in range(2):
                        copy_turned(k, s, half)
                    exponentials(k, s)

        @block.tensor
        def _(pe):
            def turn(i, u, half):
                g = i * 2 + u
                pe.wait_ge(own, g + 1)
                pe.wait_ge(turned_copied, g * 2 + (half + 1))
                for j in range(HALF):
                    ins = pe.transpose(ps_T[:, j, :], own_node[:, u, half * HALF + j, :], identity[:, :])
                ins.then_inc(turned, 1)

            def look_up(i, u, blocks):
                g = i * 2 + u
                pe.wait_ge(turned_copied, g * 2 + 3)
                if not (isinstance(g, int) and g == 0):
                    pe.wait_ge(arg_ready, g)
                for j, b in enumerate(blocks):
                    ins = pe.matmul(ps_look[:, j, :], own_nodeT[:, u, j, :], look[:, bass.ds(b * 2 * H, 2 * H)], start=True, stop=True)
                ins.then_inc(looked_up, 1)

            turn(0, 0, 0)
            turn(0, 0, 1)
            look_up(0, 0, blocks_of(nc, sh, mybir.EngineType.PE, block_ids, 0, 0))
            with pe.Fori(0, sh.BATCHES // 2) as i:
                for u in range(2):
                    s, k = ring(i, u, 1)
                    blocks = blocks_of(nc, sh, mybir.EngineType.PE, block_ids, k, s)
                    for j in range(TPB):
                        n = i * (2 * TPB) + (u * TPB + j)
                        if j == 2 or j == 4:
                            turn(k, s, j // 2 - 1)
                        if j == 6:
                            look_up(k, s, blocks)
                        pe.wait_ge(weighted, n + 1)
                        pe.wait_ge(added, n + 1 + BANK_HELD[j])
                        for a in range(BANKS):
                            ins = pe.matmul(ps_sum[:, j % 3, a, 0:RB], own_node[:, u, j, :], rows[:, u, j, a * RB:(a + 1) * RB], start=True, stop=True)
                        ins.then_inc(summed, 1)


def leaky_max(v, chain, sh, look, top, tmp, H):
    lk = look[:, :].rearrange("p (b c) -> p b c", c=2 * H)
    tp = top[:, :].rearrange("p (b c) -> p b c", c=H)
    tm = tmp[:, :].rearrange("p (b c) -> p b c", c=H)
    chain.step(v.tensor_tensor(tm, lk[:, :, 0:H], tp, ALU.add))
    chain.step(v.scalar_tensor_tensor(lk[:, :, H:2 * H], tm, SLOPE, tm, ALU.mult, ALU.max))


def dense_between(nc, sh, x, H0, F0, total0, zbuf, W1, b1, W2, b2, Wg, att_src, att_dst, tab1, alpha1,
                  look1, top1, self1, consts):
    identity = consts["identity"]
    D = sh.D
    R0 = H0 * F0 + H0
    K0 = D // P
    HID = W1.shape[1]
    M1 = HID // P
    D2 = W2.shape[1]
    M2 = D2 // P
    H1, F1 = att_src.shape
    HF1 = H1 * F1
    R1 = HF1 + H1
    GN = GRP * P
    with ExitStack() as ctx:
        def sb(name, shape, dt):
            return ctx.enter_context(nc.sbuf_tensor(name, shape, dt))

        def psum(name, shape, dt):
            return ctx.enter_context(nc.psum_tensor(name, shape, dt))

        def sem(name):
            return ctx.enter_context(nc.semaphore(name))

        w1 = sb("w1", [P, K0, HID], F32)
        w2 = sb("w2", [P, M1, D2], F32)
        wg = sb("wg", [P, M2, HF1 + 2 * H1], F32)
        att = sb("att", [P, 2, HF1], F32)
        att_tmp = sb("att_tmp", [P, HF1], F32)
        b1c = sb("b1c", [P, M1], F32)
        b2c = sb("b2c", [P, M2], F32)
        x4 = sb("x4", [P, GRP, D], F32)
        y4 = sb("y4", [P, GRP, D], F32)
        z4 = sb("z4", [P, GRP, D], F32)
        den = sb("den", [P, GRP, H0], F32)
        rden = sb("rden", [P, GRP, H0], F32)
        stats = sb("stats", [P, GRP, 6], F32)
        mv = sb("mv", [P, GRP, 2], F32)
        var = sb("var", [P, GRP], F32)
        std = sb("std", [P, GRP], F32)
        rstd = sb("rstd", [P, GRP], F32)
        zT = sb("zT", [P, K0, GN], F32)
        h1T = sb("h1T", [P, M1, GN], F32)
        h2T = sb("h2T", [P, M2, GN], F32)
        row1 = sb("row1", [P, GRP, R1], F32)
        ps_z = psum("ps_z", [P, 2, 512], F32)
        ps_1 = psum("ps_1", [P, 2, 512], F32)
        ps_2 = psum("ps_2", [P, 2, 512], F32)
        ps_x = psum("ps_x", [P, 2, 512], F32)

        weights_in = sem("weights_in")
        att_ready = sem("att_ready")
        x4_in = sem("x4_in")
        added_x = sem("added_x")
        y_ready = sem("y_ready")
        var_ready = sem("var_ready")
        std_ready = sem("std_ready")
        z_ready = sem("z_ready")
        z_turned = sem("z_turned")
        zT_copied = sem("zT_copied")
        h1_mm = sem("h1_mm")
        h1_ready = sem("h1_ready")
        h2_mm = sem("h2_mm")
        h2_ready = sem("h2_ready")
        x1_mm = sem("x1_mm")
        x1_copied = sem("x1_copied")
        row_step = sem("row_step")
        z_stored = sem("z_stored")
        row_stored = sem("row_stored")
        stats_turn = sem("stats_turn")
        aggregated = sem("aggregated")
        dve = sem("dve_dense")
        block = ctx.enter_context(nc.Block())
        FULL = sh.N // GN
        rest = sh.N - FULL * GN
        assert rest and FULL == sh.GROUPS - 1
        full_rest = rest // P
        DSTEPS = 2 * GRP + 4

        @block.sync
        def _(sp):
            sp.dma_start(w1[:, :, :], W1.rearrange("(k p) m -> p k m", p=P)).then_inc(weights_in, 16)
            sp.dma_start(w2[:, :, :], W2.rearrange("(k p) m -> p k m", p=P)).then_inc(weights_in, 16)
            sp.dma_start(wg[:, :, 0:HF1], Wg.rearrange("(k p) m -> p k m", p=P)).then_inc(weights_in, 16)
            sp.dma_start(att[:, 0, :], att_src.rearrange("h f -> (h f)").partition_broadcast(P)).then_inc(weights_in, 16)
            sp.dma_start(att[:, 1, :], att_dst.rearrange("h f -> (h f)").partition_broadcast(P)).then_inc(weights_in, 16)
            with nc.allow_non_contiguous_dma("biases as columns, 3 KB in all"):
                sp.dma_start(b1c[:, :], b1.rearrange("(m p) -> p m", p=P)).then_inc(weights_in, 16)
                sp.dma_start(b2c[:, :], b2.rearrange("(m p) -> p m", p=P)).then_inc(weights_in, 16)

            def load_x(i):
                sp.dma_start(x4[:, :, :], x[bass.ds(i * GN, GN), :].rearrange("(j p) d -> p j d", p=P)).then_inc(x4_in, 16)

            load_x(0)
            with sp.Fori(1, FULL) as i:
                sp.wait_ge(y_ready, i)
                load_x(i)
            sp.wait_ge(y_ready, FULL)
            for j in range(full_rest):
                sp.dma_start(x4[:, j, :], x[FULL * GN + j * P:FULL * GN + (j + 1) * P, :]).then_inc(x4_in, 16)
            if rest % P:
                sp.dma_start(x4[0:rest % P, full_rest, :], x[FULL * GN + full_rest * P:sh.N, :]).then_inc(x4_in, 16)

        @block.vector
        def _(v):
            v.wait_ge(weights_in, 16 * 7)
            chain = Chain(v, dve)
            for k in range(M2):
                for part in range(2):
                    chain.step(v.tensor_tensor(att_tmp[:, :], wg[:, k, 0:HF1], att[:, part, :], ALU.mult))
                    chain.step(v.tensor_reduce(wg[:, k, HF1 + part * H1:HF1 + (part + 1) * H1],
                                               att_tmp[:, :].rearrange("p (h f) -> p h f", h=H1), AX_X, ALU.add))
            v.sem_inc(att_ready)
            base = chain.value

            def group(i, loads, first=False):
                chain = Chain(v, dve, i * DSTEPS + base)
                at = i * (GRP * R0)
                tot = total0[:, bass.ds(at, GRP * R0)].rearrange("p (j r) -> p j r", r=R0)
                chain.step(v.tensor_scalar(den[:, :, :], tot[:, :, H0 * F0:R0], 1e-30, None, ALU.max))
                chain.step(v.reciprocal(rden[:, :, :], den[:, :, :]))
                for j in range(GRP):
                    chain.step(v.tensor_tensor(y4[:, j, :].rearrange("p (h f) -> p h f", h=H0),
                                               tot[:, j, 0:H0 * F0].rearrange("p (h f) -> p h f", h=H0),
                                               rden[:, j, :].unsqueeze(2).broadcast_to([P, H0, F0]), ALU.mult))
                v.wait_ge(x4_in, loads)
                for j in range(GRP):
                    v.scalar_tensor_tensor(y4[:, j, :], y4[:, j, :], 0.0, x4[:, j, :], ALU.max, ALU.add).then_inc(added_x, 1)
                v.wait_ge(added_x, i * GRP + GRP)
                v.sem_inc(y_ready)
                for j in range(GRP):
                    chain.step(v.bn_stats(stats[:, j, :], y4[:, j, :]))
                v.sem_inc(stats_turn)
                for j in range(GRP):
                    v.bn_aggr(mv[:, j, :], stats[:, j, :]).then_inc(aggregated, 1)
                v.wait_ge(aggregated, i * GRP + GRP)
                chain.step(v.tensor_scalar(var[:, :], mv[:, :, 1], EPS, None, ALU.add))
                v.sem_inc(var_ready)
                v.wait_ge(std_ready, i + 1)
                chain.step(v.reciprocal(rstd[:, :], std[:, :]))
                if not first:
                    v.wait_ge(z_stored, i * 16)
                v.wait_ge(z_turned, i * K0 + 1)
                for j in range(GRP):
                    v.tensor_scalar(z4[:, j, :], y4[:, j, :], mv[:, j, 0:1], rstd[:, j:j + 1], ALU.subtract, ALU.mult).then_inc(z_ready, 1)
                v.wait_ge(z_ready, i * GRP + GRP)

            v.sem_inc(z_turned)
            group(0, 16, first=True)
            with v.Fori(1, FULL) as i:
                group(i, i * 16 + 16)
            group(FULL, FULL * 16 + 16 * (full_rest + (1 if rest % P else 0)))

        @block.scalar
        def _(act):
            act.wait_ge(weights_in, 16 * 7)

            def std_and_store(i):
                act.wait_ge(var_ready, i + 1)
                act.activation(std[:, :], var[:, :], ACT.Sqrt).then_inc(std_ready, 1)
                act.wait_ge(z_ready, i * GRP + GRP)
                act.dma_start(zbuf[bass.ds(i * GN, GN), :].rearrange("(j p) d -> p j d", p=P), z4[:, :, :]).then_inc(z_stored, 16)

            def chain_of_layers(i, first=False):
                for k in range(K0):
                    act.wait_ge(z_turned, i * K0 + (k + 2))
                    act.activation(zT[:, k, :], ps_z[:, k % 2, :], ACT.Copy).then_inc(zT_copied, 1)
                for m in range(M1):
                    act.wait_ge(h1_mm, i * M1 + (m + 1))
                    act.activation(h1T[:, m, :], ps_1[:, m % 2, :], ACT.Relu, bias=b1c[:, m:m + 1]).then_inc(h1_ready, 1)
                for m in range(M2):
                    act.wait_ge(h2_mm, i * M2 + (m + 1))
                    act.activation(h2T[:, m, :], ps_2[:, m % 2, :], ACT.Relu, bias=b2c[:, m:m + 1]).then_inc(h2_ready, 1)
                if not first:
                    act.wait_ge(row_stored, i * 32)
                for j in range(GRP):
                    act.wait_ge(x1_mm, i * GRP + (j + 1))
                    ps = ps_x[:, j % 2, :]
                    at = i * GRP + j
                    act.activation(row1[:, j, :], ps[:, 0:R1], ACT.Copy).then_inc(row_step, 1)
                    act.activation(top1[:, bass.ds(at * H1, H1)], ps[:, HF1:R1], ACT.Copy).then_inc(row_step, 1)
                    act.activation(self1[:, bass.ds(at * H1, H1)], ps[:, HF1:R1], ACT.Copy).then_inc(row_step, 1)
                    act.activation(look1[:, bass.ds(at * 2 * H1, H1)], ps[:, R1:R1 + H1], ACT.Copy).then_inc(x1_copied, 1)
                act.wait_ge(row_step, i * (3 * GRP) + 3 * GRP)
                nodes = bass.ds(i * GN, GN)
                act.dma_start(tab1[nodes, :].rearrange("(j p) d -> p j d", p=P), row1[:, :, :]).then_inc(row_stored, 16)
                act.dma_start(alpha1[nodes, :].rearrange("(j p) d -> p j d", p=P), row1[:, :, HF1:R1]).then_inc(row_stored, 16)

            act.sem_inc(x1_copied, 2)
            std_and_store(0)
            chain_of_layers(0, first=True)
            with act.Fori(1, sh.GROUPS) as i:
                std_and_store(i)
                chain_of_layers(i)
            act.wait_ge(z_stored, sh.GROUPS * 16)
            act.wait_ge(row_stored, sh.GROUPS * 32)

        @block.tensor
        def _(pe):
            pe.wait_ge(att_ready, 1)
            with pe.Fori(0, sh.GROUPS) as i:
                pe.wait_ge(z_ready, i * GRP + GRP)
                for k in range(K0):
                    if k >= 2:
                        pe.wait_ge(zT_copied, i * K0 + (k - 1))
                    for j in range(GRP):
                        ins = pe.transpose(ps_z[:, k % 2, j * P:(j + 1) * P], z4[:, j, k * P:(k + 1) * P], identity[:, :])
                    ins.then_inc(z_turned, 1)
                pe.wait_ge(zT_copied, i * K0 + K0)
                for m in range(M1):
                    for k in range(K0):
                        ins = pe.matmul(ps_1[:, m % 2, :], w1[:, k, m * P:(m + 1) * P], zT[:, k, :], start=(k == 0), stop=(k == K0 - 1))
                    ins.then_inc(h1_mm, 1)
                pe.wait_ge(h1_ready, i * M1 + M1)
                for m in range(M2):
                    if m >= 2:
                        pe.wait_ge(h2_ready, i * M2 + (m - 1))
                    for k in range(M1):
                        ins = pe.matmul(ps_2[:, m % 2, :], w2[:, k, m * P:(m + 1) * P], h1T[:, k, :], start=(k == 0), stop=(k == M1 - 1))
                    ins.then_inc(h2_mm, 1)
                pe.wait_ge(h2_ready, i * M2 + M2)
                for j in range(GRP):
                    pe.wait_ge(x1_copied, i * GRP + (j + 1))
                    for k in range(M2):
                        ins = pe.matmul(ps_x[:, j % 2, 0:R1 + H1], h2T[:, k, j * P:(j + 1) * P], wg[:, k, :], start=(k == 0), stop=(k == M2 - 1))
                    ins.then_inc(x1_mm, 1)


def output(nc, sh, H, F, total1, zbuf, tab1, look1, top1, self1, bias_g, W3, b3, out, consts):
    identity = consts["identity"]
    D = sh.D
    HF = H * F
    R = HF + H
    K = HF // P
    GN = GRP * P
    S = sh.SLOTS
    with ExitStack() as ctx:
        def sb(name, shape, dt):
            return ctx.enter_context(nc.sbuf_tensor(name, shape, dt))

        def psum(name, shape, dt):
            return ctx.enter_context(nc.psum_tensor(name, shape, dt))

        def sem(name):
            return ctx.enter_context(nc.semaphore(name))

        w3 = sb("w3", [P, K, D], F32)
        b3r = sb("b3r", [P, D], F32)
        bg = sb("bg", [P, HF], F32)
        self_z = sb("self_z", [P, S, H], F32)
        self_l = sb("self_l", [P, S, H], F32)
        self_a = sb("self_a", [P, S, H], F32)
        self_w = sb("self_w", [P, S, H], F32)
        den = sb("o_den", [P, S, H], F32)
        den2 = sb("o_den2", [P, S, H], F32)
        rden = sb("o_rden", [P, S, H], F32)
        zin = sb("zin", [P, 2, D], F32)
        xp = sb("xp", [P, 2, R], F32)
        num = sb("num", [P, 2, HF], F32)
        agg = sb("agg", [P, 2, HF], F32)
        aggT = sb("aggT", [P, 2, K, P], F32)
        y = sb("o_y", [P, 2, D], F32)
        y2 = sb("o_y2", [P, 2, D], F32)
        stats = sb("o_stats", [P, 2, 6], F32)
        mv = sb("o_mv", [P, 2, 2], F32)
        var = sb("o_var", [P, 2], F32)
        std = sb("o_std", [P, 2], F32)
        rstd = sb("o_rstd", [P, 2], F32)
        res = sb("res", [P, 2, D], F32)
        ps_t = psum("o_ps_t", [P, 2, 512], F32)
        ps_o = psum("o_ps_o", [P, 2, 512], F32)

        weights_in = sem("o_weights_in")
        rows_in = [sem(f"o_rows_in{u}") for u in range(2)]
        self_step = sem("self_step")
        self_exp = sem("self_exp")
        num_ready = sem("num_ready")
        agg_ready = sem("agg_ready")
        turned = sem("o_turned")
        aggT_ready = sem("aggT_ready")
        out_mm = sem("out_mm")
        y_ready = sem("o_y_ready")
        var_ready = sem("o_var_ready")
        std_ready = sem("o_std_ready")
        res_ready = sem("res_ready")
        stored = [sem(f"o_stored{u}") for u in range(2)]
        stats_turn = sem("o_stats_turn")
        dve = sem("o_dve")
        block = ctx.enter_context(nc.Block())
        last = sh.N - (sh.BLOCKS - 1) * P
        PAIRS = ceil_div(sh.BLOCKS, 2)
        STEPS = 5

        @block.sync
        def _(sp):
            sp.dma_start(w3[:, :, :], W3.rearrange("(k p) m -> p k m", p=P)).then_inc(weights_in, 16)
            sp.dma_start(b3r[:, :], b3.partition_broadcast(P)).then_inc(weights_in, 16)
            sp.dma_start(bg[:, :], bias_g.partition_broadcast(P)).then_inc(weights_in, 16)

            def load(i, u):
                at = bass.ds((i * 2 + u) * P, P)
                sp.dma_start(zin[:, u, :], zbuf[at, :]).then_inc(rows_in[u], 16)
                sp.dma_start(xp[:, u, :], tab1[at, :]).then_inc(rows_in[u], 16)

            load(0, 0)
            load(0, 1)
            with sp.Fori(1, PAIRS) as i:
                for u in range(2):
                    sp.wait_ge(y_ready, i * 2 + (u + 1))
                    load(i, u)

        @block.vector
        def _(v):
            v.sem_inc(y_ready, 2)
            tot = total1[:, :].rearrange("p (b r) -> p b r", r=R)
            lk = look1[:, :].rearrange("p (b c) -> p b c", c=2 * H)
            chain = Chain(v, self_step)
            chain.step(v.tensor_tensor(self_z[:, :, :], lk[:, :, 0:H], self1[:, :].rearrange("p (b c) -> p b c", c=H), ALU.add))
            chain.step(v.scalar_tensor_tensor(self_l[:, :, :], self_z[:, :, :], SLOPE, self_z[:, :, :], ALU.mult, ALU.max))
            chain.step(v.tensor_tensor(self_a[:, :, :], self_l[:, :, :], lk[:, :, H:2 * H], ALU.subtract))
            v.wait_ge(self_exp, 1)
            chain.step(v.tensor_tensor(den[:, :, :], tot[:, :, HF:R], self_w[:, :, :], ALU.add))
            chain.step(v.tensor_scalar(den2[:, :, :], den[:, :, :], 1e-16, None, ALU.max))
            chain.step(v.reciprocal(rden[:, :, :], den2[:, :, :]))
            v.wait_ge(weights_in, 48)

            def heads(i, u, first=False):
                n = i * 2 + u
                v.wait_ge(rows_in[u], i * 32 + 32)
                for h in range(H):
                    c = slice(h * F, (h + 1) * F)
                    sw = self_w[:, :, :].rearrange("p b h -> p (b h)")[:, bass.ds(n * H + h, 1)]
                    v.scalar_tensor_tensor(num[:, u, c], xp[:, u, c], sw, total1[:, bass.ds(n * R + h * F, F)],
                                           ALU.mult, ALU.add).then_inc(num_ready, 1)
                v.wait_ge(num_ready, n * H + H)
                if not first:
                    v.wait_ge(turned, n - 1)
                for h in range(H):
                    c = slice(h * F, (h + 1) * F)
                    rd = rden[:, :, :].rearrange("p b h -> p (b h)")[:, bass.ds(n * H + h, 1)]
                    v.scalar_tensor_tensor(agg[:, u, c], num[:, u, c], rd, bg[:, c], ALU.mult, ALU.add).then_inc(agg_ready, 1)

            def norm(i, u, first=False):
                n = i * 2 + u
                chain = Chain(v, dve, n * STEPS)
                v.wait_ge(out_mm, n + 1)
                chain.step(v.tensor_tensor(y[:, u, :], ps_o[:, u, :], zin[:, u, :], ALU.add))
                v.sem_inc(y_ready)
                chain.step(v.tensor_tensor(y2[:, u, :], y[:, u, :], b3r[:, :], ALU.add))
                chain.step(v.bn_stats(stats[:, u, :], y2[:, u, :]))
                v.sem_inc(stats_turn)
                chain.step(v.bn_aggr(mv[:, u, :], stats[:, u, :]))
                v.tensor_scalar(var[:, u:u + 1], mv[:, u, 1:2], EPS, None, ALU.add).then_inc(var_ready, 1)
                v.wait_ge(std_ready, n + 1)
                chain.step(v.reciprocal(rstd[:, u:u + 1], std[:, u:u + 1]))
                if not first:
                    v.wait_ge(stored[u], i * 16)
                v.tensor_scalar(res[:, u, :], y2[:, u, :], mv[:, u, 0:1], rstd[:, u:u + 1], ALU.subtract, ALU.mult).then_inc(res_ready, 1)

            heads(0, 0, first=True)
            heads(0, 1, first=True)
            norm(0, 0, first=True)
            heads(1, 0)
            norm(0, 1, first=True)
            heads(1, 1)
            norm(1, 0)
            with v.Fori(2, PAIRS) as i:
                heads(i, 0)
                norm(i - 1, 1)
                heads(i, 1)
                norm(i, 0)
            norm(PAIRS - 1, 1)

        @block.tensor
        def _(pe):
            pe.wait_ge(weights_in, 48)
            with pe.Fori(0, PAIRS) as i:
                for u in range(2):
                    n = i * 2 + u
                    pe.wait_ge(agg_ready, n * H + H)
                    for k in range(K):
                        ins = pe.transpose(ps_t[:, u, k * P:(k + 1) * P], agg[:, u, k * P:(k + 1) * P], identity[:, :])
                    ins.then_inc(turned, 1)
                    pe.wait_ge(aggT_ready, n + 1)
                    pe.wait_ge(y_ready, n + 1)
                    for k in range(K):
                        ins = pe.matmul(ps_o[:, u, 0:D], aggT[:, u, k, :], w3[:, k, :], start=(k == 0), stop=(k == K - 1))
                    ins.then_inc(out_mm, 1)

        @block.scalar
        def _(act):
            act.wait_ge(self_step, 3)
            act.activation(self_w[:, :, :], self_a[:, :, :], ACT.Exp).then_inc(self_exp, 1)

            def one_block(i, u, count):
                n = i * 2 + u
                act.wait_ge(turned, n + 1)
                act.activation(aggT[:, u, :, :].rearrange("p k n -> p (k n)"), ps_t[:, u, 0:HF], ACT.Copy).then_inc(aggT_ready, 1)
                act.wait_ge(var_ready, n + 1)
                act.activation(std[:, u:u + 1], var[:, u:u + 1], ACT.Sqrt).then_inc(std_ready, 1)
                act.wait_ge(res_ready, n + 1)
                if count == P:
                    act.dma_start(out[bass.ds(n * P, P), :], res[:, u, :]).then_inc(stored[u], 16)
                elif count:
                    act.dma_start(out[sh.N - count:sh.N, :], res[0:count, u, :]).then_inc(stored[u], 16)

            full = (sh.BLOCKS - 1) // 2
            with act.Fori(0, full) as i:
                for u in range(2):
                    one_block(i, u, P)
            for n in range(2 * full, 2 * PAIRS):
                one_block(n // 2, n % 2, P if n < sh.BLOCKS - 1 else last if n == sh.BLOCKS - 1 else 0)
            for u in range(2):
                act.wait_ge(stored[u], 16 * ((sh.BLOCKS + 1 - u) // 2))


def gnn(nc, x, src, dst, W0, att0, W1, b1, W2, b2, Wg, att_src, att_dst, bias_g, W3, b3, out):
    sh = Shapes(x.shape[0], x.shape[1], src.shape[0])
    H0, _, F0 = W0.shape
    H1, F1 = att_src.shape
    R0, R1 = H0 * F0 + H0, H1 * F1 + H1
    rows = sh.SLOTS * P

    def dram(name, shape, dt):
        return nc.dram_tensor(name, shape, dt, kind="Internal").ap()

    lists = [dram(f"edges_{s}", (sh.TAIL * BATCH, 2), I32) for s in ("by_src", "by_dst")]
    batches = [l.rearrange("(g p j) e -> g p j e", p=P, j=TPB) for l in lists]
    tab0 = dram("table0", (rows, R0), F32)
    alpha0 = dram("alpha0", (rows, H0), F32)
    zbuf = dram("z", (rows, sh.D), F32)
    tab1 = dram("table1", (rows, R1), F32)
    alpha1 = dram("alpha1", (rows, H1), F32)

    with ExitStack() as ctx:
        def sb(name, shape, dt):
            return ctx.enter_context(nc.sbuf_tensor(name, shape, dt))

        def sem(name):
            return ctx.enter_context(nc.semaphore(name))

        consts = {
            "iota_n": sb("iota_n", [P, P], F32),
            "identity": sb("identity", [P, P], F32),
            "part_id": sb("part_id", [P, 1], F32),
        }
        block_ids = [sb(f"block_ids{s}", [1, sh.TILES], I32) for s in range(2)]
        addr1 = sb("addr1", [P, sh.COLS], I32)
        value1 = sb("value1", [P, sh.COLS, 2], I32)
        look0 = sb("look0", [P, sh.SLOTS * 2 * H0], F32)
        top0 = sb("top0", [P, sh.SLOTS * H0], F32)
        look1 = sb("look1", [P, sh.SLOTS * 2 * H1], F32)
        top1 = sb("top1", [P, sh.SLOTS * H1], F32)
        self1 = sb("self1", [P, sh.SLOTS * H1], F32)
        max_tmp = sb("max_tmp", [P, sh.SLOTS * max(H0, H1)], F32)

        def finish_max(name, look, top, H):
            with nc.semaphore(name) as step, nc.Block() as block:
                @block.vector
                def _(v):
                    leaky_max(v, Chain(v, step), sh, look, top, max_tmp[:, 0:sh.SLOTS * H], H)

        total_rounds = sh.COLS // (2 * Scatter.PART)
        rounds = min(total_rounds, sh.BATCHES // 2)
        side = (lists[1], addr1, value1)
        assert total_rounds - rounds <= sh.BATCHES // 2
        prepare(nc, sh, x, src, dst, W0, att0, lists, addr1, value1, tab0, alpha0, look0, block_ids, consts)
        segment_max(nc, sh, "_0", H0, batches[0], alpha0, look0, top0, block_ids[0], consts, unset=True,
                    scatter=(*side, 0, rounds))
        finish_max("max_step_0", look0, top0, H0)
        with nc.sbuf_tensor("total0", [P, sh.SLOTS * R0], F32) as total0:
            weighted_sums(nc, sh, "_0", H0, F0, batches[0], tab0, look0, total0, block_ids[0], consts,
                          scatter=(*side, rounds * 2 * Scatter.PART, total_rounds - rounds))
            dense_between(nc, sh, x, H0, F0, total0, zbuf, W1, b1, W2, b2, Wg, att_src, att_dst,
                          tab1, alpha1, look1, top1, self1, consts)
        segment_max(nc, sh, "_1", H1, batches[1], alpha1, look1, top1, block_ids[1], consts, unset=False)
        finish_max("max_step_1", look1, top1, H1)
        with nc.sbuf_tensor("total1", [P, sh.SLOTS * R1], F32) as total1:
            weighted_sums(nc, sh, "_1", H1, F1, batches[1], tab1, look1, total1, block_ids[1], consts)
            output(nc, sh, H1, F1, total1, zbuf, tab1, look1, top1, self1, bias_g, W3, b3, out, consts)


_INS = ['x', 'src', 'dst', 'L0_gnn_W', 'L0_gnn_att_w', 'L1_gnn_W1', 'L1_gnn_b1', 'L1_gnn_W2', 'L1_gnn_b2', 'L1_gnn_Wg',
        'L1_gnn_att_src', 'L1_gnn_att_dst', 'L1_gnn_bias_g', 'L1_gnn_W3', 'L1_gnn_b3']


def kernel(**inputs):
    import numpy as _np
    import concourse.bacc as _bacc
    from concourse import mybir as _mybir
    from concourse.bass_utils import run_bass_kernel_spmd as _run

    nc = _bacc.Bacc("TRN2", target_bir_lowering=False, num_devices=1)
    arrays, args = {}, []
    for name in _INS:
        a = _np.ascontiguousarray(inputs[name])
        arrays[f"in_{name}_dram"] = a
        args.append(nc.dram_tensor(f"in_{name}_dram", a.shape, _mybir.dt.from_np(a.dtype), kind="ExternalInput").ap())
    args.append(nc.dram_tensor("out_0_dram", inputs['x'].shape, F32, kind="ExternalOutput").ap())
    gnn(nc, *args)
    r = _run(nc, [arrays], core_ids=[0])
    return r.results[0]["out_0_dram"]
```

```python
from contextlib import ExitStack

import concourse.bass as bass
from concourse import mybir

P = 128
TPB = 8
BATCH = P * TPB
GRP = 4
SIDE = 2
DENSE_SIDE = 4
PAD_LOC = 200
BIG = 1e30
EPS = 1e-5
SLOPE = 0.2

ALU = mybir.AluOpType
ACT = mybir.ActivationFunctionType
AX_X = mybir.AxisListType.X
F32 = mybir.dt.float32
BF16 = mybir.dt.bfloat16
I32 = mybir.dt.int32
U32 = mybir.dt.uint32
U16 = mybir.dt.uint16


BANK_HELD = [1, 1] + [0] * (TPB - 2)


def ceil_div(a, b):
    return (a + b - 1) // b


class Shapes:

    def __init__(self, n, d, e):
        self.N, self.D, self.E = n, d, e
        self.BLOCKS = ceil_div(n, P)
        self.BUCKETS = self.BLOCKS + 1
        self.GROUPS = ceil_div(self.BUCKETS, GRP)
        self.SLOTS = self.GROUPS * GRP
        self.COLS = ceil_div(ceil_div(e, P), TPB) * TPB
        filler = P * self.COLS - e
        tiles = (e + self.BLOCKS * (P - 1)) // P + ceil_div(filler, P)
        self.BATCHES = 2 * ceil_div(tiles, 2 * TPB)
        self.TAIL = self.BATCHES + 2
        self.TILES = self.TAIL * TPB


class Chain:

    def __init__(self, eng, sem, start=0):
        self.eng, self.sem, self.value = eng, sem, start

    def step(self, ins):
        ins.then_inc(self.sem, 1)
        self.value = self.value + 1
        self.eng.wait_ge(self.sem, self.value)


def ring(i, u, ahead):
    q = u + ahead
    return q % 2, i + q // 2


def blocks_of(nc, sh, engine, block_ids, i, u):
    at = (i * 2 + u) * TPB
    ids = block_ids[0:1, bass.ds(at, TPB)]
    return nc.values_load_multi_w_load_instructions(
        ids, engines=(engine,), min_val=0, max_val=sh.BUCKETS - 1,
        skip_runtime_bounds_check_because="the table's values are a count from 0, capped when it is made")[1]


def prepare(nc, sh, x, src, dst, W0, att0, lists, addr1, value1, tab0, alpha0, look0, block_ids, consts):
    H, _, F = W0.shape
    HF = H * F
    KC = sh.D // P
    C = sh.COLS
    NB = sh.BUCKETS
    iota_n, identity, part_id = consts["iota_n"], consts["identity"], consts["part_id"]
    with ExitStack() as ctx:
        def sb(name, shape, dt):
            return ctx.enter_context(nc.sbuf_tensor(name, shape, dt))

        def psum(name, shape, dt):
            return ctx.enter_context(nc.psum_tensor(name, shape, dt))

        def sem(name):
            return ctx.enter_context(nc.semaphore(name))

        key_i = sb("key_i", [P, C], I32)
        other_i = sb("other_i", [P, C], I32)
        hi_i = sb("hi_i", [P, C], I32)
        hi = sb("hi", [P, C], BF16)
        match = sb("match", [P, 2, C], BF16)
        rank = sb("rank", [P, 2, C], F32)
        pos = sb("pos", [P, C], F32)
        pos_i = sb("pos_i", [P, C], I32)
        part_a = sb("part_a", [P, C], I32)
        part_b = sb("part_b", [P, C], I32)
        part_c = sb("part_c", [P, C], I32)
        addr = [sb("addr0", [P, C], I32), addr1]
        value = [sb("value0", [P, C, 2], I32), value1]
        totals = sb("totals", [P, NB], F32)
        count_i = sb("count_i", [NB, 1], I32)
        aligned_i = sb("aligned_i", [NB, 1], I32)
        aligned = sb("aligned", [NB, 1], F32)
        aligned_bc = sb("aligned_bc", [NB, P], F32)
        starts = sb("starts", [P, NB], F32)
        ends = sb("ends", [NB, 1], F32)
        tile_start = sb("tile_start", [NB, sh.TILES], F32)
        past = sb("past", [NB, sh.TILES], F32)
        before = sb("before", [P, P], F32)
        upto = sb("upto", [P, P], F32)
        ones = sb("ones", [P, 1], F32)
        empty = sb("empty", [P, sh.TILES, 2], I32)
        slot_addr = sb("slot_addr", [P, 4, TPB], I32)
        slot_value = sb("slot_value", [P, 4, TPB, 2], I32)
        w_sb = sb("w_sb", [P, KC, HF], F32)
        att_bc = sb("att_bc", [P, H, 2 * F], F32)
        wa_tmp = sb("wa_tmp", [P, H, F], F32)
        wa = sb("wa", [P, KC, 2 * H], F32)
        x_in = sb("x_in", [P, 2, sh.D], F32)
        xT = sb("xT", [P, 2, KC, P], F32)
        feat = sb("feat", [P, 2, HF + H], F32)
        ps_sort = psum("ps_sort", [P, 512], F32)
        ps_ids = psum("ps_ids", [P, 512], F32)
        ps_xT = psum("ps_xT", [P, 2, 512], F32)
        ps_f = psum("ps_f", [P, 2, 512], F32)
        ps_a = psum("ps_a", [P, 2, 512], F32)

        consts_ready = sem("consts_ready")
        pads_set = sem("pads_set")
        keys_in = sem("keys_in")
        keys_read = sem("keys_read")
        cleared = sem("cleared")
        totals_ready = sem("totals_ready")
        counts_mm = sem("counts_mm")
        aligned_ready = sem("aligned_ready")
        starts_mm = sem("starts_mm")
        past_ready = sem("past_ready")
        matched = sem("matched")
        ranked = sem("ranked")
        placed = sem("placed")
        ids_mm = sem("ids_mm")
        addr_ready = sem("addr_ready")
        slot_in = [sem(f"slot_in{k}") for k in range(4)]
        scattered = [sem(f"scattered{k}") for k in range(4)]
        pool_turn, dve_turn = consts["pool_turn"], consts["dve_turn"]
        dve = sem("dve_sort")
        pool_step = sem("pool_setup")
        w_in = sem("w_in")
        wa_ready = sem("wa_ready")
        x_loaded = [sem(f"x_loaded{u}") for u in range(2)]
        x_turned = sem("x_turned")
        xT_ready = sem("xT_ready")
        feat_mm = sem("feat_mm")
        feat_copied = sem("feat_copied")
        look_step = sem("look_step")
        feat_stored = [sem(f"feat_stored{u}") for u in range(2)]

        whole = sh.E // C
        rest = sh.E - whole * C
        ROUNDS = C // TPB // 4
        IDC = sh.TILES // 2
        SORTS = ((src, dst), (dst, src))
        assert NB % 2 == 0
        block = ctx.enter_context(nc.Block())

        @block.gpsimd
        def _(pool):
            pool.iota(iota_n[:, :], [[1, P]], base=0, channel_multiplier=0,
                      allow_small_or_imprecise_dtypes=True).then_inc(pool_step, 1)
            pool.iota(part_id[:, :], [[1, 1]], base=0, channel_multiplier=1,
                      allow_small_or_imprecise_dtypes=True).then_inc(pool_step, 1)
            pool.iota(tile_start[:, :], [[P, sh.TILES]], base=0, channel_multiplier=0,
                      allow_small_or_imprecise_dtypes=True).then_inc(pool_step, 1)
            pool.memset(ones[:, :], 1.0).then_inc(pool_step, 1)
            pool.wait_ge(pool_step, 4)
            for tri, op in ((identity, ALU.is_equal), (before, ALU.is_gt), (upto, ALU.is_ge)):
                pool.tensor_scalar(tri[:, :], iota_n[:, :], part_id[:, 0:1], None, op).then_inc(consts_ready, 1)
            pool.wait_ge(cleared, 2 * 16)
            with pool.Fori(0, ROUNDS) as i:
                for k in range(4):
                    pool.wait_ge(slot_in[k], i * 32 + 32)
                    pool.sem_inc(pool_turn)
                    for j in range(TPB):
                        pool.indirect_dma_start(
                            out=lists[0], out_offset=bass.IndirectOffsetOnAxis(
                                ap=slot_addr[:, k, j:j + 1].bitcast(U32), axis=0),
                            in_=slot_value[:, k, j, :], in_offset=None).then_inc(scattered[k], 16)
            for k in range(4):
                pool.wait_ge(scattered[k], ROUNDS * TPB * 16)

        @block.sync
        def _(sp):
            sp.wait_ge(pads_set, 3)
            sp.dma_start(lists[0].rearrange("(p c) e -> p (c e)", p=P),
                         empty[:, :, :].rearrange("p c e -> p (c e)")).then_inc(cleared, 16)
            sp.dma_start(lists[1].rearrange("(p c) e -> p (c e)", p=P),
                         empty[:, :, :].rearrange("p c e -> p (c e)")).then_inc(cleared, 16)

            def load_keys(s):
                for tile, arr in zip((key_i, other_i), SORTS[s]):
                    sp.dma_start(tile[0:whole, :], arr[0:whole * C].rearrange("(p c) -> p c", c=C)).then_inc(keys_in, 16)
                    sp.dma_start(tile[whole:whole + 1, 0:rest],
                                 arr[whole * C:sh.E].rearrange("(a c) -> a c", a=1)).then_inc(keys_in, 16)

            load_keys(0)
            sp.wait_ge(keys_read, 1)
            load_keys(1)

            def feed(i, k, first=False):
                if not first:
                    sp.wait_ge(scattered[k], i * (16 * TPB))
                cut = bass.ds((i * 4 + k) * TPB, TPB)
                sp.dma_start(slot_addr[:, k, :], addr[0][:, cut]).then_inc(slot_in[k], 16)
                sp.dma_start(slot_value[:, k, :, :], value[0][:, cut, :]).then_inc(slot_in[k], 16)

            sp.wait_ge(addr_ready, 1)
            for k in range(4):
                feed(0, k, first=True)
            with sp.Fori(1, ROUNDS) as i:
                for k in range(4):
                    feed(i, k)

        @block.vector
        def _(v):
            v.memset(key_i[:, :], sh.BLOCKS * P).then_inc(pads_set, 1)
            v.memset(other_i[:, :], 0).then_inc(pads_set, 1)
            v.memset(empty[:, :, 0], PAD_LOC).then_inc(dve, 1)
            v.memset(empty[:, :, 1], 0).then_inc(dve, 1)
            v.wait_ge(dve, 2)
            v.memset(empty[:, 0:1, 1], 0).then_inc(pads_set, 1)
            v.wait_ge(consts_ready, 3)
            chain = Chain(v, dve, 2)
            v.sem_inc(totals_ready, 2)
            v.sem_inc(placed)
            for s in range(2):
                if s == 1:
                    v.wait_ge(w_in, 16 * (KC + 1))
                    for k in range(KC):
                        for part in range(2):
                            a = att_bc[:, :, (1 - part) * F:(2 - part) * F]
                            chain.step(v.tensor_tensor(wa_tmp[:, :, :], w_sb[:, k, :].rearrange("p (h f) -> p h f", h=H), a, ALU.mult))
                            chain.step(v.tensor_reduce(wa[:, k, part * H:(part + 1) * H], wa_tmp[:, :, :], AX_X, ALU.add))
                    v.sem_inc(wa_ready)
                v.wait_ge(keys_in, 64 * (s + 1))
                chain.step(v.tensor_scalar(hi_i[:, :], key_i[:, :], 7, None, ALU.logical_shift_right))
                chain.step(v.tensor_copy(hi[:, :], hi_i[:, :]))
                chain.step(v.tensor_scalar(value[s][:, :, 0], key_i[:, :], P - 1, None, ALU.bitwise_and))
                chain.step(v.tensor_copy(value[s][:, :, 1], other_i[:, :]))
                v.sem_inc(keys_read)
                chain.step(v.memset(pos[:, :], 0.0))
                with v.Fori(0, NB // 2) as i:
                    for k in range(2):
                        b = i * 2 + k
                        v.wait_ge(totals_ready, b + (s * NB + 1))
                        v.tensor_scalar(match[:, k, :], hi[:, :], iota_n[:, bass.ds(b, 1)], 0.0, ALU.is_equal, ALU.add,
                                        accum_out=totals[:, bass.ds(b, 1)]).then_inc(totals_ready, 1)
                v.wait_ge(totals_ready, (s + 1) * NB + 2)
                v.wait_ge(counts_mm, s + 1)
                chain.step(v.tensor_scalar(count_i[:, :], ps_sort[0:NB, 0:1], float(P - 1), None, ALU.add))
                chain.step(v.tensor_scalar(aligned_i[:, :], count_i[:, :], 7, 7, ALU.logical_shift_right, ALU.logical_shift_left))
                chain.step(v.tensor_copy(aligned[:, :], aligned_i[:, :]))
                chain.step(v.tensor_copy(aligned_bc[:, :], aligned[:, 0:1].to_broadcast([NB, P])))
                v.sem_inc(aligned_ready)
                v.wait_ge(starts_mm, s + 1)
                chain.step(v.tensor_copy(starts[:, :], ps_sort[:, 0:NB]))
                chain.step(v.tensor_copy(ends[:, :], ps_sort[0:NB, NB:NB + 1]))
                chain.step(v.tensor_scalar(past[:, :], tile_start[:, :], ends[:, 0:1], None, ALU.is_ge))
                v.sem_inc(past_ready)
                v.wait_ge(ids_mm, s + 1)
                chain.step(v.tensor_scalar(block_ids[s][0:1, 0:IDC], ps_sort[0:1, 0:IDC], float(NB - 1), None, ALU.min))
                chain.step(v.tensor_scalar(block_ids[s][0:1, IDC:2 * IDC], ps_ids[0:1, 0:IDC], float(NB - 1), None, ALU.min))
                def match_bucket(b, k):
                    v.tensor_scalar(match[:, k, :], hi[:, :], iota_n[:, bass.ds(b, 1)], None, ALU.is_equal).then_inc(matched, 1)

                match_bucket(0, 0)
                with v.Fori(0, NB // 2) as i:
                    for k in range(2):
                        b = i * 2 + k
                        v.wait_ge(matched, b + (s * (NB + 1) + 1))
                        v.tensor_tensor_scan(rank[:, k, :], match[:, k, :], match[:, k, :], starts[:, bass.ds(b, 1)],
                                             ALU.add, ALU.max).then_inc(ranked, 1)
                        v.wait_ge(placed, b + (s * NB + 1))
                        match_bucket(b + 1, 1 - k)
                        v.wait_ge(ranked, b + (s * NB + 1))
                        v.sem_inc(dve_turn)
                        v.copy_predicated(pos[:, :], match[:, k, :].bitcast(U16), rank[:, k, :]).then_inc(placed, 1)
                v.wait_ge(matched, (s + 1) * (NB + 1))
                v.wait_ge(placed, (s + 1) * NB + 1)
                chain.step(v.tensor_scalar(pos_i[:, :], pos[:, :], -1.0, None, ALU.add))
                chain.step(v.tensor_scalar(part_a[:, :], pos_i[:, :], 10, 10, ALU.logical_shift_right, ALU.logical_shift_left))
                chain.step(v.tensor_scalar(part_b[:, :], pos_i[:, :], P - 1, 3, ALU.bitwise_and, ALU.logical_shift_left))
                chain.step(v.tensor_scalar(part_c[:, :], pos_i[:, :], 7, TPB - 1, ALU.logical_shift_right, ALU.bitwise_and))
                chain.step(v.tensor_tensor(part_a[:, :], part_a[:, :], part_b[:, :], ALU.bitwise_or))
                chain.step(v.tensor_tensor(addr[s][:, :], part_a[:, :], part_c[:, :], ALU.bitwise_or))
                v.sem_inc(addr_ready)

        def sort_products(pe, s):
            pe.wait_ge(totals_ready, NB * (s + 1) + 2)
            pe.matmul(ps_sort[0:NB, 0:1], totals[:, :], ones[:, 0:1], start=True, stop=True).then_inc(counts_mm, 1)
            pe.wait_ge(aligned_ready, s + 1)
            pe.matmul(ps_sort[:, 0:NB], before[:, :], totals[:, :], start=True, stop=False)
            pe.matmul(ps_sort[:, 0:NB], aligned_bc[:, :], before[0:NB, 0:NB], start=False, stop=True)
            pe.matmul(ps_sort[0:NB, NB:NB + 1], upto[0:NB, 0:NB], aligned[:, :], start=True, stop=True).then_inc(starts_mm, 1)
            pe.wait_ge(past_ready, s + 1)
            pe.matmul(ps_sort[0:1, 0:IDC], ones[0:NB, 0:1], past[:, 0:IDC], start=True, stop=True)
            pe.matmul(ps_ids[0:1, 0:IDC], ones[0:NB, 0:1], past[:, IDC:2 * IDC], start=True, stop=True).then_inc(ids_mm, 1)

        @block.tensor
        def _(pe):
            pe.wait_ge(consts_ready, 3)
            sort_products(pe, 0)
            pe.wait_ge(w_in, 16 * (KC + 1))
            pe.wait_ge(wa_ready, 1)
            with pe.Fori(0, sh.SLOTS // 2) as i:
                for u in range(2):
                    n = i * 2 + u
                    pe.wait_ge(x_loaded[u], i * 16 + 16)
                    for k in range(KC):
                        ins = pe.transpose(ps_xT[:, u, k * P:(k + 1) * P], x_in[:, u, k * P:(k + 1) * P], identity[:, :])
                    ins.then_inc(x_turned, 1)
                    pe.wait_ge(xT_ready, n + 1)
                    pe.wait_ge(feat_copied, n + 1)
                    for k in range(KC):
                        pe.matmul(ps_f[:, u, 0:HF], xT[:, u, k, :], w_sb[:, k, :], start=(k == 0), stop=(k == KC - 1))
                    for k in range(KC):
                        ins = pe.matmul(ps_a[:, u, 0:2 * H], xT[:, u, k, :], wa[:, k, :], start=(k == 0), stop=(k == KC - 1))
                    ins.then_inc(feat_mm, 1)
            sort_products(pe, 1)

        @block.scalar
        def _(act):
            for k in range(KC):
                act.dma_start(w_sb[:, k, :].rearrange("p (h f) -> p h f", h=H),
                              W0[:, k * P:(k + 1) * P, :].rearrange("h p f -> p h f")).then_inc(w_in, 16)
            act.dma_start(att_bc[:, :, :], att0.partition_broadcast(P)).then_inc(w_in, 16)
            for u in range(2):
                act.dma_start(x_in[:, u, :], x[u * P:(u + 1) * P, :]).then_inc(x_loaded[u], 16)
            act.sem_inc(feat_copied, 2)

            def one_block(i, u, load, first=False):
                n = i * 2 + u
                act.wait_ge(x_turned, n + 1)
                act.activation(xT[:, u, :, :].rearrange("p k n -> p (k n)"), ps_xT[:, u, :], ACT.Copy).then_inc(xT_ready, 1)
                if load == P:
                    act.dma_start(x_in[:, u, :], x[bass.ds((n + 2) * P, P), :]).then_inc(x_loaded[u], 16)
                elif load:
                    act.dma_start(x_in[0:load, u, :], x[sh.N - load:sh.N, :]).then_inc(x_loaded[u], 16)
                else:
                    act.sem_inc(x_loaded[u], 16)
                act.wait_ge(feat_mm, n + 1)
                if not first:
                    act.wait_ge(feat_stored[u], i * 32)
                act.activation(feat[:, u, 0:HF], ps_f[:, u, 0:HF], ACT.Copy).then_inc(look_step, 1)
                act.activation(feat[:, u, HF:HF + H], ps_a[:, u, 0:H], ACT.Copy).then_inc(look_step, 1)
                act.activation(look_slice(n), ps_a[:, u, H:2 * H], ACT.Copy).then_inc(feat_copied, 1)
                act.wait_ge(look_step, n * 2 + 2)
                rows = bass.ds(n * P, P)
                act.dma_start(tab0[rows, :], feat[:, u, :]).then_inc(feat_stored[u], 16)
                act.dma_start(alpha0[rows, :], feat[:, u, HF:HF + H]).then_inc(feat_stored[u], 16)

            def look_slice(n):
                return look0[:, bass.ds(n * 2 * H, H)]

            last = sh.N - (sh.BLOCKS - 1) * P
            one_block(0, 0, P, first=True)
            one_block(0, 1, P, first=True)
            full = (sh.BLOCKS - 1 - 2) // 2
            with act.Fori(1, full) as i:
                for u in range(2):
                    one_block(i, u, P)
            for n in range(2 * full, sh.SLOTS):
                ahead = n + 2
                load = P if ahead < sh.BLOCKS - 1 else last if ahead == sh.BLOCKS - 1 else None
                one_block(n // 2, n % 2, load)
            for u in range(2):
                act.wait_ge(feat_stored[u], sh.SLOTS // 2 * 32)


class Scatter:

    def __init__(self, nc, ctx, out, addr, value, first, part, rounds):
        self.out, self.addr, self.value = out, addr, value
        self.first, self.PART, self.rounds = first, part, rounds
        self.slot_addr = ctx.enter_context(nc.sbuf_tensor(f"s_addr{first}", [P, 2, self.PART], I32))
        self.slot_value = ctx.enter_context(nc.sbuf_tensor(f"s_value{first}", [P, 2, self.PART, 2], I32))
        self.slot_in = [ctx.enter_context(nc.semaphore(f"s_slot_in{u}_{first}")) for u in range(2)]
        self.scattered = [ctx.enter_context(nc.semaphore(f"s_scattered{u}_{first}")) for u in range(2)]

    def feed(self, sp, i, u, first=False):
        if not first:
            sp.wait_ge(self.scattered[u], i * (16 * self.PART))
        cut = bass.ds((i * 2 + u) * self.PART + self.first, self.PART)
        sp.dma_start(self.slot_addr[:, u, :], self.addr[:, cut]).then_inc(self.slot_in[u], 16)
        sp.dma_start(self.slot_value[:, u, :, :], self.value[:, cut, :]).then_inc(self.slot_in[u], 16)

    def wait_slot(self, pool, turn, i, u):
        pool.wait_ge(self.slot_in[u], i * 32 + 32)
        pool.sem_inc(turn)

    def put(self, pool, u, c):
        pool.indirect_dma_start(
            out=self.out, out_offset=bass.IndirectOffsetOnAxis(ap=self.slot_addr[:, u, c:c + 1].bitcast(U32), axis=0),
            in_=self.slot_value[:, u, c, :], in_offset=None).then_inc(self.scattered[u], 16)

    def wait_all(self, pool):
        for u in range(2):
            pool.wait_ge(self.scattered[u], self.rounds * 16 * self.PART)


def segment_max(nc, sh, tag, H, edges, alpha, look, top, block_ids, consts, unset, scatter=None):
    iota_n, identity = consts["iota_n"], consts["identity"]
    ROW = 3 * H
    HALF = TPB // 2
    HB = min(H, 512 // P)
    BANKS = H // HB
    with ExitStack() as ctx:
        def sb(name, shape, dt):
            return ctx.enter_context(nc.sbuf_tensor(f"{name}{tag}", shape, dt))

        def psum(name, shape, dt):
            return ctx.enter_context(nc.psum_tensor(f"{name}{tag}", shape, dt))

        def sem(name):
            return ctx.enter_context(nc.semaphore(f"{name}{tag}"))

        cols = sb("cols", [P, 2, TPB, 2], I32)
        own_f = sb("own_f", [P, 2, TPB], F32)
        al = sb("al", [P, 2, TPB, H], F32)
        other_node = sb("other_node", [P, 2, TPB, P], BF16)
        part = sb("part", [P, 2, TPB, 3, H], BF16)
        rem1 = sb("rem1", [P, TPB, H], F32)
        rem2 = sb("rem2", [P, TPB, H], F32)
        partT = sb("partT", [HALF * ROW, 2, 2, P], BF16)
        pick = sb("pick", [HALF * ROW, HALF, H, P], BF16)
        minus_big = sb("minus_big", [P, P], BF16)
        ident_b = sb("ident_b", [P, P], BF16)
        tile_max = sb("tile_max", [P, TPB, H], F32)
        ps_T = psum("ps_T", [HALF * ROW, 2, P], BF16)
        ps_m = psum("ps_m", [P, 3, BANKS, 512], F32)

        cols_in = [sem(f"cols_in{u}_") for u in range(2)]
        gathered = [sem(f"gathered{u}_") for u in range(2)]
        set_up = sem("set_up")
        pick_step = sem("pick_step")
        side = Scatter(nc, ctx, *scatter) if scatter else None
        masks = sem("masks")
        own_read = sem("own_read")
        split = sem("split")
        turned = sem("turned")
        turned_copied = sem("turned_copied")
        masked = sem("masked")
        reduced = sem("reduced")
        merged = sem("merged")
        dve = sem("dve_max")
        pool_turn = consts["pool_turn"]
        block = ctx.enter_context(nc.Block())

        @block.sync
        def _(sp):
            for u in range(2):
                sp.dma_start(cols[:, u, :, :], edges[u]).then_inc(cols_in[u], 16)
            if side:
                for u in range(2):
                    side.feed(sp, 0, u, first=True)

            def load(i, u, feed):
                sp.wait_ge(gathered[u], i * (16 * TPB))
                sp.wait_ge(masks, i * 2 + (u - 1))
                sp.dma_start(cols[:, u, :, :], edges[bass.ds(i * 2 + u, 1)].rearrange("a p j e -> (a p) j e")).then_inc(cols_in[u], 16)
                if feed:
                    side.feed(sp, i, u)

            with_side = side.rounds if side else 1
            if side:
                with sp.Fori(1, with_side) as i:
                    for u in range(2):
                        load(i, u, True)
            with sp.Fori(with_side, sh.TAIL // 2) as i:
                for u in range(2):
                    load(i, u, False)
            for u in range(2):
                sp.wait_ge(cols_in[u], sh.TAIL // 2 * 16)

        @block.gpsimd
        def _(pool):
            pool.memset(pick[:, :, :, :], 0.0).then_inc(pick_step, 1)
            for part_no in range(3):
                pool.wait_ge(pick_step, part_no + 1)
                pool.affine_select(out=pick[:, :, :, :], in_=pick[:, :, :, :], compare_op=ALU.not_equal, fill=1.0,
                                   base=-part_no * H, pattern=[[-ROW, HALF], [-1, H], [0, P]],
                                   channel_multiplier=1).then_inc(pick_step, 1)

            def gather(i, u, beside=False):
                pool.wait_ge(cols_in[u], i * 16 + 16)
                pool.sem_inc(pool_turn)
                pool.wait_ge(split, i * 2 + (u + 1))
                pool.sem_inc(pool_turn)
                if beside:
                    side.wait_slot(pool, pool_turn, i, u)
                for j in range(TPB):
                    pool.indirect_dma_start(
                        out=al[:, u, j, :], out_offset=None, in_=alpha,
                        in_offset=bass.IndirectOffsetOnAxis(ap=cols[:, u, j, 1:2].bitcast(U32), axis=0)).then_inc(gathered[u], 16)
                    if beside and j < side.PART:
                        side.put(pool, u, j)

            with_side = side.rounds if side else 0
            if side:
                with pool.Fori(0, with_side) as i:
                    for u in range(2):
                        gather(i, u, beside=True)
            if with_side < sh.BATCHES // 2:
                with pool.Fori(with_side, sh.BATCHES // 2) as i:
                    for u in range(2):
                        gather(i, u)
            gather(sh.BATCHES // 2, 0)
            if side:
                side.wait_all(pool)

        @block.vector
        def _(v):
            v.tensor_scalar(minus_big[:, :], identity[:, :], -BIG, None, ALU.mult).then_inc(set_up, 1)
            v.tensor_copy(ident_b[:, :], identity[:, :]).then_inc(set_up, 1)
            if unset:
                v.memset(top[:, :], -BIG).then_inc(merged, 1)
            else:
                v.sem_inc(merged)
            v.sem_inc(split, 2)
            v.sem_inc(reduced, 3)
            v.sem_inc(masked)

            def split_values(i, u, base):
                v.wait_ge(gathered[u], i * (16 * TPB) + 16 * TPB)
                chain = Chain(v, dve, base)
                chain.step(v.tensor_copy(part[:, u, :, 0, :], al[:, u, :, :]))
                chain.step(v.tensor_tensor(rem1[:, :, :], al[:, u, :, :], part[:, u, :, 0, :], ALU.subtract))
                chain.step(v.tensor_copy(part[:, u, :, 1, :], rem1[:, :, :]))
                chain.step(v.tensor_tensor(rem2[:, :, :], rem1[:, :, :], part[:, u, :, 1, :], ALU.subtract))
                v.tensor_copy(part[:, u, :, 2, :], rem2[:, :, :]).then_inc(split, 1)

            def merge(i, u):
                first = i * (2 * TPB) + u * TPB
                for j in range(TPB + 1):
                    if j < TPB:
                        v.wait_ge(masked, first + (j + 2))
                        if H == HB:
                            in_ = ps_m[:, j % 3, 0, 0:H * P].rearrange("p (h e) -> p h e", h=H)
                        else:
                            in_ = ps_m[:, j % 3, :, :].rearrange("p a (h e) -> p (a h) e", h=HB)
                        v.tensor_reduce(tile_max[:, j, :], in_, AX_X, ALU.max).then_inc(reduced, 1)
                    if j == 0:
                        blocks = blocks_of(nc, sh, mybir.EngineType.DVE, block_ids, i, u)
                    if j:
                        v.wait_ge(reduced, first + (j + 3))
                        v.wait_ge(merged, first + j)
                        here = top[:, bass.ds(blocks[j - 1] * H, H)]
                        v.tensor_tensor(here, here, tile_max[:, j - 1, :], ALU.max).then_inc(merged, 1)

            split_values(0, 0, 0)
            with v.Fori(0, sh.BATCHES // 2) as i:
                for u in range(2):
                    s, k = ring(i, u, 1)
                    v.wait_ge(masked, (i * 2 + u) * TPB + 1)
                    split_values(k, s, (i * 2 + (u + 1)) * 4)
                    merge(i, u)

        @block.tensor
        def _(pe):
            pe.wait_ge(set_up, 2)
            pe.wait_ge(pick_step, 4)

            def turn(i, u):
                n = i * 2 + u
                pe.wait_ge(split, n + 3)
                pe.wait_ge(turned_copied, n + 1)
                for half in range(2):
                    ins = pe.transpose(ps_T[:, half, :], part[:, u, half * HALF:(half + 1) * HALF, :, :].rearrange("p j s h -> p (j s h)"), ident_b[:, :])
                ins.then_inc(turned, 1)

            turn(0, 0)
            with pe.Fori(0, sh.BATCHES // 2) as i:
                for u in range(2):
                    for j in range(TPB):
                        n = i * (2 * TPB) + (u * TPB + j)
                        if j == 0:
                            pe.wait_ge(masks, i * 2 + (u + 1))
                            pe.wait_ge(turned_copied, i * 2 + (u + 2))
                        if j == HALF:
                            s, k = ring(i, u, 1)
                            turn(k, s)
                        pe.wait_ge(reduced, n + 1 + BANK_HELD[j])
                        for a in range(BANKS):
                            pe.matmul(ps_m[:, j % 3, a, 0:HB * P], other_node[:, u, j, :],
                                      minus_big[:, :].unsqueeze(1).broadcast_to([P, HB, P]), start=True, stop=False)
                            for h in range(HB):
                                ins = pe.matmul(ps_m[:, j % 3, a, h * P:(h + 1) * P], pick[:, j % HALF, a * HB + h, :],
                                                partT[:, u, j // HALF, :], start=False, stop=(h == HB - 1))
                        ins.then_inc(masked, 1)

        @block.scalar
        def _(act):
            act.sem_inc(turned_copied, 1)

            def copy_turned(i, u):
                act.wait_ge(turned, i * 2 + (u + 1))
                if not isinstance(i, int):
                    act.wait_ge(masked, (i * 2 + (u - 1)) * TPB + 1)
                act.activation(partT[:, u, :, :], ps_T[:, :, :], ACT.Copy).then_inc(turned_copied, 1)

            def mask(i, u, first=False):
                act.wait_ge(cols_in[u], i * 16 + 16)
                if not first:
                    act.wait_ge(masked, (i * 2 + (u - 1)) * TPB + 1)
                act.activation(own_f[:, u, :], cols[:, u, :, 0], ACT.Copy).then_inc(own_read, 1)
                act.wait_ge(own_read, i * 2 + (u + 1))
                for j in range(TPB):
                    ins = act.activation(other_node[:, u, j, :], iota_n[:, :], ACT.Abs, bias=own_f[:, u, j:j + 1], scale=-1.0)
                ins.then_inc(masks, 1)

            mask(0, 0, first=True)
            copy_turned(0, 0)
            with act.Fori(0, sh.BATCHES // 2) as i:
                for u in range(2):
                    s, k = ring(i, u, 1)
                    mask(k, s)
                    copy_turned(k, s)


def weighted_sums(nc, sh, tag, H, F, edges, table, look, total, block_ids, consts, scatter=None):
    iota_n, identity = consts["iota_n"], consts["identity"]
    HF = H * F
    R = HF + H
    BANKS = ceil_div(R, 512)
    RB = R // BANKS
    HALF = TPB // 2
    HV = H if H < 4 else H - 3
    with ExitStack() as ctx:
        def sb(name, shape, dt):
            return ctx.enter_context(nc.sbuf_tensor(f"{name}{tag}", shape, dt))

        def psum(name, shape, dt):
            return ctx.enter_context(nc.psum_tensor(f"{name}{tag}", shape, dt))

        def sem(name):
            return ctx.enter_context(nc.semaphore(f"{name}{tag}"))

        cols = sb("w_cols", [P, 2, TPB, 2], I32)
        rows = sb("w_rows", [P, 2, TPB, R], F32)
        own_node = sb("own_node", [P, 2, TPB, P], F32)
        own_nodeT = sb("own_nodeT", [P, 2, TPB, P], F32)
        z = sb("z", [P, TPB, H], F32)
        z2 = sb("z2", [P, TPB, H], F32)
        arg = sb("arg", [P, TPB, H], F32)
        ps_T = psum("ps_oT", [P, HALF, P], F32)
        ps_look = psum("ps_look", [P, TPB, 2 * H], F32)
        ps_sum = psum("ps_sum", [P, 3, BANKS, 512], F32)

        cols_in = [sem(f"w_cols_in{u}_") for u in range(2)]
        gathered = [sem(f"w_gathered{u}_") for u in range(2)]
        own = sem("own")
        turned = sem("w_turned")
        turned_copied = sem("w_turned_copied")
        looked_up = sem("looked_up")
        arg_ready = sem("arg_ready")
        weights_ready = sem("weights_ready")
        side = Scatter(nc, ctx, *scatter) if scatter else None
        weighted = sem("weighted")
        weighted_act = sem("weighted_act")
        summed = sem("summed")
        added = sem("added")
        dve = sem("w_dve")
        pool_turn = consts["pool_turn"]
        block = ctx.enter_context(nc.Block())

        @block.sync
        def _(sp):
            for u in range(2):
                sp.dma_start(cols[:, u, :, :], edges[u]).then_inc(cols_in[u], 16)
            if side:
                for u in range(2):
                    side.feed(sp, 0, u, first=True)

            def load(i, u, feed):
                sp.wait_ge(gathered[u], i * (16 * TPB))
                sp.wait_ge(own, i * 2 + (u - 1))
                sp.dma_start(cols[:, u, :, :], edges[bass.ds(i * 2 + u, 1)].rearrange("a p j e -> (a p) j e")).then_inc(cols_in[u], 16)
                if feed:
                    side.feed(sp, i, u)

            with_side = side.rounds if side else 1
            if side:
                with sp.Fori(1, with_side) as i:
                    for u in range(2):
                        load(i, u, True)
            with sp.Fori(with_side, sh.TAIL // 2) as i:
                for u in range(2):
                    load(i, u, False)
            for u in range(2):
                sp.wait_ge(cols_in[u], sh.TAIL // 2 * 16)

        @block.gpsimd
        def _(pool):
            def gather(i, u, beside=False):
                pool.wait_ge(cols_in[u], i * 16 + 16)
                pool.sem_inc(pool_turn)
                if beside:
                    side.wait_slot(pool, pool_turn, i, u)
                for j in range(TPB):
                    pool.wait_ge(summed, i * (2 * TPB) + (u * TPB + j + 1))
                    pool.sem_inc(pool_turn)
                    pool.indirect_dma_start(
                        out=rows[:, u, j, :], out_offset=None, in_=table,
                        in_offset=bass.IndirectOffsetOnAxis(ap=cols[:, u, j, 1:2].bitcast(U32), axis=0)).then_inc(gathered[u], 16)
                    if beside and j < side.PART:
                        side.put(pool, u, j)

            with_side = side.rounds if side else 0
            if side:
                with pool.Fori(0, with_side) as i:
                    for u in range(2):
                        gather(i, u, beside=True)
            if with_side < sh.BATCHES // 2:
                with pool.Fori(with_side, sh.BATCHES // 2) as i:
                    for u in range(2):
                        gather(i, u)
            gather(sh.BATCHES // 2, 0)
            if side:
                side.wait_all(pool)

        @block.vector
        def _(v):
            v.sem_inc(summed, 2 * TPB)
            def one_hot(i, u):
                v.wait_ge(cols_in[u], i * 16 + 16)
                v.tensor_tensor(own_node[:, u, :, :], iota_n[:, :].unsqueeze(1).broadcast_to([P, TPB, P]),
                                cols[:, u, :, 0:1].broadcast_to([P, TPB, P]), ALU.is_equal).then_inc(own, 1)

            def arguments(i, u):
                g = i * 2 + u
                v.wait_ge(looked_up, g + 1)
                v.wait_ge(gathered[u], i * (16 * TPB) + 16 * TPB)
                chain = Chain(v, dve, g * 3)
                chain.step(v.tensor_tensor(z[:, :, :], ps_look[:, :, 0:H], rows[:, u, :, HF:R], ALU.add))
                chain.step(v.scalar_tensor_tensor(z2[:, :, :], z[:, :, :], SLOPE, z[:, :, :], ALU.mult, ALU.max))
                chain.step(v.tensor_tensor(z[:, :, :], z2[:, :, :], ps_look[:, :, H:2 * H], ALU.subtract))
                if not (isinstance(g, int) and g == 0):
                    v.wait_ge(weights_ready, g)
                v.tensor_scalar(arg[:, :, :], z[:, :, :], 0.0, None, ALU.min).then_inc(arg_ready, 1)

            def weigh(i, u, j):
                feats = rows[:, u, j, 0:HV * F].rearrange("p (h f) -> p h f", h=HV)
                v.tensor_tensor(feats, feats, rows[:, u, j, HF:HF + HV].unsqueeze(2).broadcast_to([P, HV, F]), ALU.mult).then_inc(weighted, 1)

            def add_tile(i, u, j, b):
                n = i * (2 * TPB) + (u * TPB + j)
                v.wait_ge(summed, n + (2 * TPB + 1))
                v.wait_ge(added, n + 3)
                here = total[:, bass.ds(b * R, R)].rearrange("p (a c) -> p a c", a=BANKS)
                v.tensor_tensor(here, here, ps_sum[:, j % 3, :, 0:RB], ALU.add).then_inc(added, 1)

            one_hot(0, 0)
            v.memset(total[:, :], 0.0).then_inc(added, 3)
            arguments(0, 0)
            with v.Fori(0, sh.BATCHES // 2) as i:
                for u in range(2):
                    s, k = ring(i, u, 1)
                    v.wait_ge(weights_ready, i * 2 + (u + 1))
                    for j in range(TPB):
                        weigh(i, u, j)
                        if j == 0:
                            v.wait_ge(summed, (i * 2 + (u + 2)) * TPB)
                            one_hot(k, s)
                            blocks = blocks_of(nc, sh, mybir.EngineType.DVE, block_ids, i, u)
                        if j >= 2:
                            add_tile(i, u, j - 2, blocks[j - 2])
                    arguments(k, s)
                    add_tile(i, u, TPB - 2, blocks[TPB - 2])
                    add_tile(i, u, TPB - 1, blocks[TPB - 1])

        @block.scalar
        def _(act):
            def copy_turned(i, u, half):
                act.wait_ge(turned, (i * 2 + u) * 2 + (half + 1))
                act.activation(own_nodeT[:, u, half * HALF:(half + 1) * HALF, :], ps_T[:, :, :], ACT.Copy).then_inc(turned_copied, 1)

            def exponentials(i, u):
                act.wait_ge(arg_ready, i * 2 + (u + 1))
                act.activation(rows[:, u, :, HF:R], arg[:, :, :], ACT.Exp).then_inc(weights_ready, 1)

            act.sem_inc(turned_copied)
            for half in range(2):
                copy_turned(0, 0, half)
            exponentials(0, 0)
            with act.Fori(0, sh.BATCHES // 2) as i:
                for u in range(2):
                    s, k = ring(i, u, 1)
                    if HV < H:
                        act.wait_ge(weights_ready, i * 2 + (u + 1))
                    for j in range(TPB):
                        for h in range(HV, H):
                            head = rows[:, u, j, h * F:(h + 1) * F]
                            ins = act.activation(head, head, ACT.Copy, scale=rows[:, u, j, HF + h:HF + h + 1])
                        if HV < H:
                            ins.then_inc(weighted_act, 1)
                        if j == 3:
                            copy_turned(k, s, 0)
                        if j == 5:
                            copy_turned(k, s, 1)
                    exponentials(k, s)

        @block.tensor
        def _(pe):
            def turn(i, u, half):
                g = i * 2 + u
                pe.wait_ge(own, g + 1)
                pe.wait_ge(turned_copied, g * 2 + (half + 1))
                for j in range(HALF):
                    ins = pe.transpose(ps_T[:, j, :], own_node[:, u, half * HALF + j, :], identity[:, :])
                ins.then_inc(turned, 1)

            def look_up(i, u, blocks):
                g = i * 2 + u
                pe.wait_ge(turned_copied, g * 2 + 3)
                if not (isinstance(g, int) and g == 0):
                    pe.wait_ge(arg_ready, g)
                for j, b in enumerate(blocks):
                    ins = pe.matmul(ps_look[:, j, :], own_nodeT[:, u, j, :], look[:, bass.ds(b * 2 * H, 2 * H)], start=True, stop=True)
                ins.then_inc(looked_up, 1)

            turn(0, 0, 0)
            turn(0, 0, 1)
            look_up(0, 0, blocks_of(nc, sh, mybir.EngineType.PE, block_ids, 0, 0))
            with pe.Fori(0, sh.BATCHES // 2) as i:
                for u in range(2):
                    s, k = ring(i, u, 1)
                    for j in range(TPB):
                        n = i * (2 * TPB) + (u * TPB + j)
                        if j == 2 or j == 4:
                            turn(k, s, j // 2 - 1)
                        if j == 6:
                            look_up(k, s, blocks)
                        pe.wait_ge(weighted, n + 1)
                        if HV < H:
                            pe.wait_ge(weighted_act, n + 1)
                        pe.wait_ge(added, n + 1 + BANK_HELD[j])
                        for a in range(BANKS):
                            ins = pe.matmul(ps_sum[:, j % 3, a, 0:RB], own_node[:, u, j, :], rows[:, u, j, a * RB:(a + 1) * RB], start=True, stop=True)
                        ins.then_inc(summed, 1)
                        if j == 0:
                            blocks = blocks_of(nc, sh, mybir.EngineType.PE, block_ids, k, s)


def leaky_max(v, chain, sh, look, top, tmp, H):
    lk = look[:, :].rearrange("p (b c) -> p b c", c=2 * H)
    tp = top[:, :].rearrange("p (b c) -> p b c", c=H)
    tm = tmp[:, :].rearrange("p (b c) -> p b c", c=H)
    chain.step(v.tensor_tensor(tm, lk[:, :, 0:H], tp, ALU.add))
    chain.step(v.scalar_tensor_tensor(lk[:, :, H:2 * H], tm, SLOPE, tm, ALU.mult, ALU.max))


def dense_between(nc, sh, x, H0, F0, total0, zbuf, W1, b1, W2, b2, Wg, att_src, att_dst, tab1, alpha1,
                  look1, top1, self1, consts, scatter):
    identity = consts["identity"]
    D = sh.D
    R0 = H0 * F0 + H0
    K0 = D // P
    HID = W1.shape[1]
    M1 = HID // P
    D2 = W2.shape[1]
    M2 = D2 // P
    H1, F1 = att_src.shape
    HF1 = H1 * F1
    R1 = HF1 + H1
    GN = GRP * P
    with ExitStack() as ctx:
        def sb(name, shape, dt):
            return ctx.enter_context(nc.sbuf_tensor(name, shape, dt))

        def psum(name, shape, dt):
            return ctx.enter_context(nc.psum_tensor(name, shape, dt))

        def sem(name):
            return ctx.enter_context(nc.semaphore(name))

        w1 = sb("w1", [P, K0, HID], F32)
        w2 = sb("w2", [P, M1, D2], F32)
        wg = sb("wg", [P, M2, HF1 + 2 * H1], F32)
        att = sb("att", [P, 2, HF1], F32)
        att_tmp = sb("att_tmp", [P, HF1], F32)
        b1c = sb("b1c", [P, M1], F32)
        b2c = sb("b2c", [P, M2], F32)
        x4 = sb("x4", [P, GRP, D], F32)
        y4 = sb("y4", [P, GRP, D], F32)
        z4 = sb("z4", [P, GRP, D], F32)
        den = sb("den", [P, GRP, H0], F32)
        rden = sb("rden", [P, GRP, H0], F32)
        stats = sb("stats", [P, GRP, 6], F32)
        mv = sb("mv", [P, GRP, 2], F32)
        var = sb("var", [P, GRP], F32)
        std = sb("std", [P, GRP], F32)
        rstd = sb("rstd", [P, GRP], F32)
        zT = sb("zT", [P, K0, GN], F32)
        h1T = sb("h1T", [P, M1, GN], F32)
        h2T = sb("h2T", [P, M2, GN], F32)
        row1 = sb("row1", [P, GRP, R1], F32)
        ps_z = psum("ps_z", [P, 2, 512], F32)
        ps_1 = psum("ps_1", [P, 2, 512], F32)
        ps_2 = psum("ps_2", [P, 2, 512], F32)
        ps_x = psum("ps_x", [P, 2, 512], F32)

        side = Scatter(nc, ctx, *scatter)
        pool_turn, dve_turn = consts["pool_turn"], consts["dve_turn"]
        weights_in = sem("weights_in")
        att_ready = sem("att_ready")
        x4_in = sem("x4_in")
        added_x = sem("added_x")
        y_ready = sem("y_ready")
        var_ready = sem("var_ready")
        std_ready = sem("std_ready")
        z_ready = sem("z_ready")
        z_turned = sem("z_turned")
        zT_copied = sem("zT_copied")
        h1_mm = sem("h1_mm")
        h1_ready = sem("h1_ready")
        h2_mm = sem("h2_mm")
        h2_ready = sem("h2_ready")
        x1_mm = sem("x1_mm")
        x1_copied = sem("x1_copied")
        row_step = sem("row_step")
        z_stored = sem("z_stored")
        row_stored = sem("row_stored")
        aggregated = sem("aggregated")
        dve = sem("dve_dense")
        block = ctx.enter_context(nc.Block())
        FULL = sh.N // GN
        rest = sh.N - FULL * GN
        assert rest and FULL == sh.GROUPS - 1
        full_rest = rest // P
        DSTEPS = 2 * GRP + 4

        @block.sync
        def _(sp):
            sp.dma_start(w1[:, :, :], W1.rearrange("(k p) m -> p k m", p=P)).then_inc(weights_in, 16)
            sp.dma_start(w2[:, :, :], W2.rearrange("(k p) m -> p k m", p=P)).then_inc(weights_in, 16)
            sp.dma_start(wg[:, :, 0:HF1], Wg.rearrange("(k p) m -> p k m", p=P)).then_inc(weights_in, 16)
            sp.dma_start(att[:, 0, :], att_src.rearrange("h f -> (h f)").partition_broadcast(P)).then_inc(weights_in, 16)
            sp.dma_start(att[:, 1, :], att_dst.rearrange("h f -> (h f)").partition_broadcast(P)).then_inc(weights_in, 16)
            with nc.allow_non_contiguous_dma("biases as columns, 3 KB in all"):
                sp.dma_start(b1c[:, :], b1.rearrange("(m p) -> p m", p=P)).then_inc(weights_in, 16)
                sp.dma_start(b2c[:, :], b2.rearrange("(m p) -> p m", p=P)).then_inc(weights_in, 16)

            def load_x(i):
                sp.dma_start(x4[:, :, :], x[bass.ds(i * GN, GN), :].rearrange("(j p) d -> p j d", p=P)).then_inc(x4_in, 16)

            load_x(0)
            for u in range(2):
                side.feed(sp, 0, u, first=True)
            per = (side.rounds - 1) // (FULL - 1)
            with sp.Fori(1, FULL) as i:
                sp.wait_ge(y_ready, i)
                load_x(i)
                for r in range(per):
                    for u in range(2):
                        side.feed(sp, (i - 1) * per + (r + 1), u)
            sp.wait_ge(y_ready, FULL)
            for j in range(full_rest):
                sp.dma_start(x4[:, j, :], x[FULL * GN + j * P:FULL * GN + (j + 1) * P, :]).then_inc(x4_in, 16)
            if rest % P:
                sp.dma_start(x4[0:rest % P, full_rest, :], x[FULL * GN + full_rest * P:sh.N, :]).then_inc(x4_in, 16)
            for r in range(1 + (FULL - 1) * per, side.rounds):
                for u in range(2):
                    side.feed(sp, r, u)

        @block.gpsimd
        def _(pool):
            with pool.Fori(0, side.rounds) as i:
                for u in range(2):
                    side.wait_slot(pool, pool_turn, i, u)
                    for c in range(side.PART):
                        side.put(pool, u, c)
            side.wait_all(pool)

        @block.vector
        def _(v):
            v.wait_ge(weights_in, 16 * 7)
            chain = Chain(v, dve)
            for k in range(M2):
                for part in range(2):
                    chain.step(v.tensor_tensor(att_tmp[:, :], wg[:, k, 0:HF1], att[:, part, :], ALU.mult))
                    chain.step(v.tensor_reduce(wg[:, k, HF1 + part * H1:HF1 + (part + 1) * H1],
                                               att_tmp[:, :].rearrange("p (h f) -> p h f", h=H1), AX_X, ALU.add))
            v.sem_inc(att_ready)
            base = chain.value

            def group(i, loads, first=False):
                chain = Chain(v, dve, i * DSTEPS + base)
                at = i * (GRP * R0)
                tot = total0[:, bass.ds(at, GRP * R0)].rearrange("p (j r) -> p j r", r=R0)
                chain.step(v.tensor_scalar(den[:, :, :], tot[:, :, H0 * F0:R0], 1e-30, None, ALU.max))
                chain.step(v.reciprocal(rden[:, :, :], den[:, :, :]))
                for j in range(GRP):
                    chain.step(v.tensor_tensor(y4[:, j, :].rearrange("p (h f) -> p h f", h=H0),
                                               tot[:, j, 0:H0 * F0].rearrange("p (h f) -> p h f", h=H0),
                                               rden[:, j, :].unsqueeze(2).broadcast_to([P, H0, F0]), ALU.mult))
                v.wait_ge(x4_in, loads)
                for j in range(GRP):
                    v.scalar_tensor_tensor(y4[:, j, :], y4[:, j, :], 0.0, x4[:, j, :], ALU.max, ALU.add).then_inc(added_x, 1)
                v.wait_ge(added_x, i * GRP + GRP)
                v.sem_inc(y_ready)
                for j in range(GRP):
                    chain.step(v.bn_stats(stats[:, j, :], y4[:, j, :]))
                v.sem_inc(dve_turn)
                for j in range(GRP):
                    v.bn_aggr(mv[:, j, :], stats[:, j, :]).then_inc(aggregated, 1)
                v.wait_ge(aggregated, i * GRP + GRP)
                chain.step(v.tensor_scalar(var[:, :], mv[:, :, 1], EPS, None, ALU.add))
                v.sem_inc(var_ready)
                v.wait_ge(std_ready, i + 1)
                chain.step(v.reciprocal(rstd[:, :], std[:, :]))
                if not first:
                    v.wait_ge(z_stored, i * 16)
                v.wait_ge(z_turned, i * K0 + 1)
                for j in range(GRP):
                    v.tensor_scalar(z4[:, j, :], y4[:, j, :], mv[:, j, 0:1], rstd[:, j:j + 1], ALU.subtract, ALU.mult).then_inc(z_ready, 1)
                v.wait_ge(z_ready, i * GRP + GRP)

            v.sem_inc(z_turned)
            group(0, 16, first=True)
            with v.Fori(1, FULL) as i:
                group(i, i * 16 + 16)
            group(FULL, FULL * 16 + 16 * (full_rest + (1 if rest % P else 0)))

        @block.scalar
        def _(act):
            act.wait_ge(weights_in, 16 * 7)

            def std_and_store(i):
                act.wait_ge(var_ready, i + 1)
                act.activation(std[:, :], var[:, :], ACT.Sqrt).then_inc(std_ready, 1)
                act.wait_ge(z_ready, i * GRP + GRP)
                act.dma_start(zbuf[bass.ds(i * GN, GN), :].rearrange("(j p) d -> p j d", p=P), z4[:, :, :]).then_inc(z_stored, 16)

            def chain_of_layers(i, first=False, more=True):
                for k in range(K0):
                    act.wait_ge(z_turned, i * K0 + (k + 2))
                    act.activation(zT[:, k, :], ps_z[:, k % 2, :], ACT.Copy).then_inc(zT_copied, 1)
                for m in range(M1):
                    act.wait_ge(h1_mm, i * M1 + (m + 1))
                    act.activation(h1T[:, m, :], ps_1[:, m % 2, :], ACT.Relu, bias=b1c[:, m:m + 1]).then_inc(h1_ready, 1)
                if more:
                    std_and_store(i + 1)
                for m in range(M2):
                    act.wait_ge(h2_mm, i * M2 + (m + 1))
                    act.activation(h2T[:, m, :], ps_2[:, m % 2, :], ACT.Relu, bias=b2c[:, m:m + 1]).then_inc(h2_ready, 1)
                if not first:
                    act.wait_ge(row_stored, i * 32)
                for j in range(GRP):
                    act.wait_ge(x1_mm, i * GRP + (j + 1))
                    ps = ps_x[:, j % 2, :]
                    at = i * GRP + j
                    act.activation(row1[:, j, :], ps[:, 0:R1], ACT.Copy).then_inc(row_step, 1)
                    act.activation(top1[:, bass.ds(at * H1, H1)], ps[:, HF1:R1], ACT.Copy).then_inc(row_step, 1)
                    act.activation(self1[:, bass.ds(at * H1, H1)], ps[:, HF1:R1], ACT.Copy).then_inc(row_step, 1)
                    act.activation(look1[:, bass.ds(at * 2 * H1, H1)], ps[:, R1:R1 + H1], ACT.Copy).then_inc(x1_copied, 1)
                act.wait_ge(row_step, i * (3 * GRP) + 3 * GRP)
                nodes = bass.ds(i * GN, GN)
                act.dma_start(tab1[nodes, :].rearrange("(j p) d -> p j d", p=P), row1[:, :, :]).then_inc(row_stored, 16)
                act.dma_start(alpha1[nodes, :].rearrange("(j p) d -> p j d", p=P), row1[:, :, HF1:R1]).then_inc(row_stored, 16)

            act.sem_inc(x1_copied, 2)
            std_and_store(0)
            chain_of_layers(0, first=True)
            with act.Fori(1, sh.GROUPS - 1) as i:
                chain_of_layers(i)
            chain_of_layers(sh.GROUPS - 1, more=False)
            act.wait_ge(z_stored, sh.GROUPS * 16)
            act.wait_ge(row_stored, sh.GROUPS * 32)

        @block.tensor
        def _(pe):
            pe.wait_ge(att_ready, 1)
            with pe.Fori(0, sh.GROUPS) as i:
                pe.wait_ge(z_ready, i * GRP + GRP)
                for k in range(K0):
                    if k >= 2:
                        pe.wait_ge(zT_copied, i * K0 + (k - 1))
                    for j in range(GRP):
                        ins = pe.transpose(ps_z[:, k % 2, j * P:(j + 1) * P], z4[:, j, k * P:(k + 1) * P], identity[:, :])
                    ins.then_inc(z_turned, 1)
                pe.wait_ge(zT_copied, i * K0 + K0)
                for m in range(M1):
                    for k in range(K0):
                        ins = pe.matmul(ps_1[:, m % 2, :], w1[:, k, m * P:(m + 1) * P], zT[:, k, :], start=(k == 0), stop=(k == K0 - 1))
                    ins.then_inc(h1_mm, 1)
                pe.wait_ge(h1_ready, i * M1 + M1)
                for m in range(M2):
                    if m >= 2:
                        pe.wait_ge(h2_ready, i * M2 + (m - 1))
                    for k in range(M1):
                        ins = pe.matmul(ps_2[:, m % 2, :], w2[:, k, m * P:(m + 1) * P], h1T[:, k, :], start=(k == 0), stop=(k == M1 - 1))
                    ins.then_inc(h2_mm, 1)
                pe.wait_ge(h2_ready, i * M2 + M2)
                for j in range(GRP):
                    pe.wait_ge(x1_copied, i * GRP + (j + 1))
                    for k in range(M2):
                        ins = pe.matmul(ps_x[:, j % 2, 0:R1 + H1], h2T[:, k, j * P:(j + 1) * P], wg[:, k, :], start=(k == 0), stop=(k == M2 - 1))
                    ins.then_inc(x1_mm, 1)


def output(nc, sh, H, F, total1, zbuf, tab1, look1, top1, self1, bias_g, W3, b3, out, consts):
    identity = consts["identity"]
    D = sh.D
    HF = H * F
    R = HF + H
    K = HF // P
    GN = GRP * P
    S = sh.SLOTS
    with ExitStack() as ctx:
        def sb(name, shape, dt):
            return ctx.enter_context(nc.sbuf_tensor(name, shape, dt))

        def psum(name, shape, dt):
            return ctx.enter_context(nc.psum_tensor(name, shape, dt))

        def sem(name):
            return ctx.enter_context(nc.semaphore(name))

        w3 = sb("w3", [P, K, D], F32)
        b3r = sb("b3r", [P, D], F32)
        bg = sb("bg", [P, HF], F32)
        self_z = sb("self_z", [P, S, H], F32)
        self_l = sb("self_l", [P, S, H], F32)
        self_a = sb("self_a", [P, S, H], F32)
        self_w = sb("self_w", [P, S, H], F32)
        den = sb("o_den", [P, S, H], F32)
        den2 = sb("o_den2", [P, S, H], F32)
        rden = sb("o_rden", [P, S, H], F32)
        zin = sb("zin", [P, 2, D], F32)
        xp = sb("xp", [P, 2, R], F32)
        num = sb("num", [P, 2, HF], F32)
        agg = sb("agg", [P, 2, HF], F32)
        aggT = sb("aggT", [P, 2, K, P], F32)
        y = sb("o_y", [P, 2, D], F32)
        stats = sb("o_stats", [P, 2, 6], F32)
        mv = sb("o_mv", [P, 2, 2], F32)
        var = sb("o_var", [P, 2], F32)
        std = sb("o_std", [P, 2], F32)
        rstd = sb("o_rstd", [P, 2], F32)
        res = sb("res", [P, 2, D], F32)
        ps_t = psum("o_ps_t", [P, 2, 512], F32)
        ps_o = psum("o_ps_o", [P, 2, 512], F32)

        weights_in = sem("o_weights_in")
        xp_in = [sem(f"o_xp_in{u}") for u in range(2)]
        z_in = [sem(f"o_z_in{u}") for u in range(2)]
        z_biased = sem("z_biased")
        pool_turn, dve_turn = consts["pool_turn"], consts["dve_turn"]
        self_exp = sem("self_exp")
        num_ready = sem("num_ready")
        agg_ready = sem("agg_ready")
        turned = sem("o_turned")
        aggT_ready = sem("aggT_ready")
        out_mm = sem("out_mm")
        y_ready = sem("o_y_ready")
        var_ready = sem("o_var_ready")
        std_ready = sem("o_std_ready")
        res_ready = sem("res_ready")
        stored = [sem(f"o_stored{u}") for u in range(2)]
        rstd_ready = sem("rstd_ready")
        dve = sem("o_dve")
        block = ctx.enter_context(nc.Block())
        last = sh.N - (sh.BLOCKS - 1) * P
        PAIRS = ceil_div(sh.BLOCKS, 2)
        STEPS = 3
        SELF_STEPS = 6

        @block.sync
        def _(sp):
            sp.dma_start(w3[:, :, :], W3.rearrange("(k p) m -> p k m", p=P)).then_inc(weights_in, 16)
            sp.dma_start(b3r[:, :], b3.partition_broadcast(P)).then_inc(weights_in, 16)
            sp.dma_start(bg[:, :], bias_g.partition_broadcast(P)).then_inc(weights_in, 16)

            def load_xp(i, u):
                sp.dma_start(xp[:, u, :], tab1[bass.ds((i * 2 + u) * P, P), :]).then_inc(xp_in[u], 16)

            def load_z(i, u):
                sp.dma_start(zin[:, u, :], zbuf[bass.ds((i * 2 + u) * P, P), :]).then_inc(z_in[u], 16)

            for u in range(2):
                load_xp(0, u)
                load_z(0, u)
            with sp.Fori(1, PAIRS) as i:
                for u in range(2):
                    sp.wait_ge(num_ready, (i * 2 + (u - 1)) * H)
                    load_xp(i, u)
                    sp.wait_ge(y_ready, i * 2 + (u + 1))
                    load_z(i, u)

        @block.gpsimd
        def _(pool):
            pool.wait_ge(weights_in, 48)
            with pool.Fori(0, PAIRS) as i:
                for u in range(2):
                    pool.wait_ge(z_in[u], i * 16 + 16)
                    pool.sem_inc(pool_turn)
                    pool.tensor_tensor(zin[:, u, :], zin[:, u, :], b3r[:, :], ALU.add).then_inc(z_biased, 1)

        @block.vector
        def _(v):
            v.sem_inc(y_ready, 2)
            tot = total1[:, :].rearrange("p (b r) -> p b r", r=R)
            lk = look1[:, :].rearrange("p (b c) -> p b c", c=2 * H)
            chain = Chain(v, dve)
            chain.step(v.tensor_tensor(self_z[:, :, :], lk[:, :, 0:H], self1[:, :].rearrange("p (b c) -> p b c", c=H), ALU.add))
            chain.step(v.scalar_tensor_tensor(self_l[:, :, :], self_z[:, :, :], SLOPE, self_z[:, :, :], ALU.mult, ALU.max))
            chain.step(v.tensor_tensor(self_a[:, :, :], self_l[:, :, :], lk[:, :, H:2 * H], ALU.subtract))
            v.wait_ge(self_exp, 1)
            chain.step(v.tensor_tensor(den[:, :, :], tot[:, :, HF:R], self_w[:, :, :], ALU.add))
            chain.step(v.tensor_scalar(den2[:, :, :], den[:, :, :], 1e-16, None, ALU.max))
            chain.step(v.reciprocal(rden[:, :, :], den2[:, :, :]))
            v.wait_ge(weights_in, 48)

            def heads(i, u, first=False):
                n = i * 2 + u
                v.wait_ge(xp_in[u], i * 16 + 16)
                for h in range(H):
                    c = slice(h * F, (h + 1) * F)
                    sw = self_w[:, :, :].rearrange("p b h -> p (b h)")[:, bass.ds(n * H + h, 1)]
                    v.scalar_tensor_tensor(num[:, u, c], xp[:, u, c], sw, total1[:, bass.ds(n * R + h * F, F)],
                                           ALU.mult, ALU.add).then_inc(num_ready, 1)
                v.wait_ge(num_ready, n * H + H)
                if not first:
                    v.wait_ge(turned, n - 1)
                for h in range(H):
                    c = slice(h * F, (h + 1) * F)
                    rd = rden[:, :, :].rearrange("p b h -> p (b h)")[:, bass.ds(n * H + h, 1)]
                    v.scalar_tensor_tensor(agg[:, u, c], num[:, u, c], rd, bg[:, c], ALU.mult, ALU.add).then_inc(agg_ready, 1)

            def norm_stats(i, u):
                n = i * 2 + u
                chain = Chain(v, dve, n * STEPS + SELF_STEPS)
                v.wait_ge(out_mm, n + 1)
                v.wait_ge(z_biased, n + 1)
                chain.step(v.tensor_tensor(y[:, u, :], ps_o[:, u, :], zin[:, u, :], ALU.add))
                v.sem_inc(y_ready)
                chain.step(v.bn_stats(stats[:, u, :], y[:, u, :]))
                v.sem_inc(dve_turn)
                chain.step(v.bn_aggr(mv[:, u, :], stats[:, u, :]))
                v.tensor_scalar(var[:, u:u + 1], mv[:, u, 1:2], EPS, None, ALU.add).then_inc(var_ready, 1)

            def norm_rows(i, u, first=False):
                n = i * 2 + u
                v.wait_ge(std_ready, n + 1)
                v.reciprocal(rstd[:, u:u + 1], std[:, u:u + 1]).then_inc(rstd_ready, 1)
                v.wait_ge(rstd_ready, n + 1)
                if not first:
                    v.wait_ge(stored[u], i * 16)
                v.tensor_scalar(res[:, u, :], y[:, u, :], mv[:, u, 0:1], rstd[:, u:u + 1], ALU.subtract, ALU.mult).then_inc(res_ready, 1)

            heads(0, 0, first=True)
            heads(0, 1, first=True)
            norm_stats(0, 0)
            for n in range(2, 4):
                heads(n // 2, n % 2)
                norm_rows((n - 2) // 2, n % 2, first=True)
                norm_stats((n - 1) // 2, (n - 1) % 2)
            with v.Fori(2, PAIRS) as i:
                heads(i, 0)
                norm_rows(i - 1, 0)
                norm_stats(i - 1, 1)
                heads(i, 1)
                norm_rows(i - 1, 1)
                norm_stats(i, 0)
            norm_rows(PAIRS - 1, 0)
            norm_stats(PAIRS - 1, 1)
            norm_rows(PAIRS - 1, 1)

        @block.tensor
        def _(pe):
            pe.wait_ge(weights_in, 48)
            with pe.Fori(0, PAIRS) as i:
                for u in range(2):
                    n = i * 2 + u
                    pe.wait_ge(agg_ready, n * H + H)
                    for k in range(K):
                        ins = pe.transpose(ps_t[:, u, k * P:(k + 1) * P], agg[:, u, k * P:(k + 1) * P], identity[:, :])
                    ins.then_inc(turned, 1)
                    pe.wait_ge(aggT_ready, n + 1)
                    pe.wait_ge(y_ready, n + 1)
                    for k in range(K):
                        ins = pe.matmul(ps_o[:, u, 0:D], aggT[:, u, k, :], w3[:, k, :], start=(k == 0), stop=(k == K - 1))
                    ins.then_inc(out_mm, 1)

        @block.scalar
        def _(act):
            act.wait_ge(dve, 3)
            act.activation(self_w[:, :, :], self_a[:, :, :], ACT.Exp).then_inc(self_exp, 1)

            def turn_copy(i, u):
                act.wait_ge(turned, i * 2 + (u + 1))
                act.activation(aggT[:, u, :, :].rearrange("p k n -> p (k n)"), ps_t[:, u, 0:HF], ACT.Copy).then_inc(aggT_ready, 1)

            def finish(i, u, count):
                n = i * 2 + u
                act.wait_ge(var_ready, n + 1)
                act.activation(std[:, u:u + 1], var[:, u:u + 1], ACT.Sqrt).then_inc(std_ready, 1)
                if count:
                    store(n - 1, 1 - u, count)

            def store(n, u, count):
                act.wait_ge(res_ready, n + 1)
                if count == P:
                    act.dma_start(out[bass.ds(n * P, P), :], res[:, u, :]).then_inc(stored[u], 16)
                elif count:
                    act.dma_start(out[sh.N - count:sh.N, :], res[0:count, u, :]).then_inc(stored[u], 16)

            def count_of(n):
                return P if n < sh.BLOCKS - 1 else last if n == sh.BLOCKS - 1 else 0

            full = (sh.BLOCKS - 1) // 2
            turn_copy(0, 0)
            turn_copy(0, 1)
            finish(0, 0, 0)
            turn_copy(1, 0)
            finish(0, 1, P)
            with act.Fori(1, full) as i:
                turn_copy(i, 1)
                finish(i, 0, P)
                turn_copy(i + 1, 0)
                finish(i, 1, P)
            for n in range(2 * full, 2 * PAIRS):
                if n + 1 < 2 * PAIRS:
                    turn_copy((n + 1) // 2, (n + 1) % 2)
                finish(n // 2, n % 2, count_of(n - 1))
            store(2 * PAIRS - 1, 1, count_of(2 * PAIRS - 1))
            for u in range(2):
                act.wait_ge(stored[u], 16 * ((sh.BLOCKS + 1 - u) // 2))


def gnn(nc, x, src, dst, W0, att0, W1, b1, W2, b2, Wg, att_src, att_dst, bias_g, W3, b3, out):
    sh = Shapes(x.shape[0], x.shape[1], src.shape[0])
    H0, _, F0 = W0.shape
    H1, F1 = att_src.shape
    R0, R1 = H0 * F0 + H0, H1 * F1 + H1
    rows = sh.SLOTS * P

    def dram(name, shape, dt):
        return nc.dram_tensor(name, shape, dt, kind="Internal").ap()

    lists = [dram(f"edges_{s}", (sh.TAIL * BATCH, 2), I32) for s in ("by_src", "by_dst")]
    batches = [l.rearrange("(g p j) e -> g p j e", p=P, j=TPB) for l in lists]
    tab0 = dram("table0", (rows, R0), F32)
    alpha0 = dram("alpha0", (rows, H0), F32)
    zbuf = dram("z", (rows, sh.D), F32)
    tab1 = dram("table1", (rows, R1), F32)
    alpha1 = dram("alpha1", (rows, H1), F32)

    with ExitStack() as ctx:
        def sb(name, shape, dt):
            return ctx.enter_context(nc.sbuf_tensor(name, shape, dt))

        def sem(name):
            return ctx.enter_context(nc.semaphore(name))

        consts = {
            "iota_n": sb("iota_n", [P, P], F32),
            "identity": sb("identity", [P, P], F32),
            "part_id": sb("part_id", [P, 1], F32),
            "pool_turn": sem("pool_turn"),
            "dve_turn": sem("dve_turn"),
        }
        block_ids = [sb(f"block_ids{s}", [1, sh.TILES], I32) for s in range(2)]
        addr1 = sb("addr1", [P, sh.COLS], I32)
        value1 = sb("value1", [P, sh.COLS, 2], I32)
        look0 = sb("look0", [P, sh.SLOTS * 2 * H0], F32)
        top0 = sb("top0", [P, sh.SLOTS * H0], F32)
        look1 = sb("look1", [P, sh.SLOTS * 2 * H1], F32)
        top1 = sb("top1", [P, sh.SLOTS * H1], F32)
        self1 = sb("self1", [P, sh.SLOTS * H1], F32)
        max_tmp = sb("max_tmp", [P, sh.SLOTS * max(H0, H1)], F32)

        def finish_max(name, look, top, H):
            with nc.semaphore(name) as step, nc.Block() as block:
                @block.vector
                def _(v):
                    leaky_max(v, Chain(v, step), sh, look, top, max_tmp[:, 0:sh.SLOTS * H], H)

        every = sh.BATCHES // 2
        assert 2 * SIDE * 2 * every <= sh.COLS
        beside_max = (lists[1], addr1, value1, 0, SIDE, every)
        beside_sum = (lists[1], addr1, value1, 2 * SIDE * every, SIDE, every)
        rest = sh.COLS - 4 * SIDE * every
        beside_dense = (lists[1], addr1, value1, sh.COLS - rest, DENSE_SIDE, rest // (2 * DENSE_SIDE))
        assert rest % (2 * DENSE_SIDE) == 0
        prepare(nc, sh, x, src, dst, W0, att0, lists, addr1, value1, tab0, alpha0, look0, block_ids, consts)
        segment_max(nc, sh, "_0", H0, batches[0], alpha0, look0, top0, block_ids[0], consts, unset=True,
                    scatter=beside_max)
        finish_max("max_step_0", look0, top0, H0)
        with nc.sbuf_tensor("total0", [P, sh.SLOTS * R0], F32) as total0:
            weighted_sums(nc, sh, "_0", H0, F0, batches[0], tab0, look0, total0, block_ids[0], consts,
                          scatter=beside_sum)
            dense_between(nc, sh, x, H0, F0, total0, zbuf, W1, b1, W2, b2, Wg, att_src, att_dst,
                          tab1, alpha1, look1, top1, self1, consts, beside_dense)
        segment_max(nc, sh, "_1", H1, batches[1], alpha1, look1, top1, block_ids[1], consts, unset=False)
        finish_max("max_step_1", look1, top1, H1)
        with nc.sbuf_tensor("total1", [P, sh.SLOTS * R1], F32) as total1:
            weighted_sums(nc, sh, "_1", H1, F1, batches[1], tab1, look1, total1, block_ids[1], consts)
            output(nc, sh, H1, F1, total1, zbuf, tab1, look1, top1, self1, bias_g, W3, b3, out, consts)


_INS = ['x', 'src', 'dst', 'L0_gnn_W', 'L0_gnn_att_w', 'L1_gnn_W1', 'L1_gnn_b1', 'L1_gnn_W2', 'L1_gnn_b2', 'L1_gnn_Wg',
        'L1_gnn_att_src', 'L1_gnn_att_dst', 'L1_gnn_bias_g', 'L1_gnn_W3', 'L1_gnn_b3']


def kernel(**inputs):
    import numpy as _np
    import concourse.bacc as _bacc
    from concourse import mybir as _mybir
    from concourse.bass_utils import run_bass_kernel_spmd as _run

    nc = _bacc.Bacc("TRN2", target_bir_lowering=False, num_devices=1)
    arrays, args = {}, []
    for name in _INS:
        a = _np.ascontiguousarray(inputs[name])
        arrays[f"in_{name}_dram"] = a
        args.append(nc.dram_tensor(f"in_{name}_dram", a.shape, _mybir.dt.from_np(a.dtype), kind="ExternalInput").ap())
    args.append(nc.dram_tensor("out_0_dram", inputs['x'].shape, F32, kind="ExternalOutput").ap())
    gnn(nc, *args)
    r = _run(nc, [arrays], core_ids=[0])
    return r.results[0]["out_0_dram"]
```
